# Optimizing a Trainium2 kernel written in Bass

```python
import numpy as np
import jax
import jax.numpy as jnp

def _softmax(x, axis=-1):
    return jax.nn.softmax(x, axis=axis)

def _gelu(x):
    return jax.nn.gelu(x, approximate=True)

def _silu(x):
    return jax.nn.silu(x)

def _sigmoid(x):
    return jax.nn.sigmoid(x)

def _layernorm(x, axis=-1, eps=1e-05):
    m = jnp.mean(x, axis=axis, keepdims=True)
    v = jnp.var(x, axis=axis, keepdims=True)
    return (x - m) / jnp.sqrt(v + eps)

def _scatter_add(tgt, idx, src, axis=0):
    return tgt.at[idx].add(src)

def _segment_sum(src, seg, n):
    return jax.ops.segment_sum(src, seg, n)
kernel_name = 'mk_metaformer_d4_conv_nchw256_r4_5ba5d0'

def setup_inputs(seed: int=0):
    np.random.seed(seed)
    _w = jnp.asarray

    def _rec_inputs():
        import jax
        import jax.numpy as jnp
        _gk = jax.random.key(seed)
        x = 7.22e-05 + 1 * jax.random.normal(jax.random.fold_in(_gk, 1), (8, 64, 16, 16), jnp.float32)
        return x
    x = _rec_inputs()

    def _L0_conv_setup():
        import jax, jax.numpy as jnp
        import numpy as np
        IN_CH = 64
        OUT_CH = 64
        DIM = 8
        HEADS = IN_CH // DIM
        TOTAL = HEADS * DIM
        C3 = 3 * TOTAL
        SCALES = (3, 5)
        EPS = 1e-15

        def _conv(x, w, b, groups=1, pad=0):
            y = jax.lax.conv_general_dilated(x, w, window_strides=(1, 1), padding=[(pad, pad), (pad, pad)], dimension_numbers=('NCHW', 'OIHW', 'NCHW'), feature_group_count=groups)
            return y + b[None, :, None, None]

        def _relu_linear_att(qkv):
            B, C, H, W = qkv.shape
            qkv = qkv.reshape(B, -1, 3 * DIM, H * W)
            q = jax.nn.relu(qkv[:, :, :DIM])
            k = jax.nn.relu(qkv[:, :, DIM:2 * DIM])
            v = qkv[:, :, 2 * DIM:]
            v = jnp.concatenate([v, jnp.ones_like(v[:, :, :1])], axis=2)
            vk = jnp.einsum('bhdn,bhen->bhde', v, k)
            out = jnp.einsum('bhde,bhen->bhdn', vk, q)
            out = out[:, :, :-1] / (out[:, :, -1:] + EPS)
            return out.reshape(B, -1, H, W)
        key = jax.random.key(seed)
        ks = jax.random.split(key, 16)
        s = 0.02
        inp = {'x': jax.random.normal(ks[0], (8, IN_CH, 16, 16), jnp.float32), 'qkv_w': jax.random.normal(ks[1], (C3, IN_CH, 1, 1), jnp.float32) * s, 'qkv_b': jnp.zeros((C3,), jnp.float32), 'dw3_w': jax.random.normal(ks[2], (C3, 1, 3, 3), jnp.float32) * s, 'dw3_b': jnp.zeros((C3,), jnp.float32), 'pw3_w': jax.random.normal(ks[3], (C3, C3 // HEADS, 1, 1), jnp.float32) * s, 'pw3_b': jnp.zeros((C3,), jnp.float32), 'dw5_w': jax.random.normal(ks[4], (C3, 1, 5, 5), jnp.float32) * s, 'dw5_b': jnp.zeros((C3,), jnp.float32), 'pw5_w': jax.random.normal(ks[5], (C3, C3 // HEADS, 1, 1), jnp.float32) * s, 'pw5_b': jnp.zeros((C3,), jnp.float32), 'proj_w': jax.random.normal(ks[6], (OUT_CH, TOTAL * (1 + len(SCALES)), 1, 1), jnp.float32) * s, 'proj_b': jnp.zeros((OUT_CH,), jnp.float32)}
        return inp
    _L0_conv_all = _L0_conv_setup()
    _L0_conv_in = {k: v for k, v in _L0_conv_all.items() if k in ('qkv_w', 'qkv_b', 'dw3_w', 'dw3_b', 'pw3_w', 'pw3_b', 'dw5_w', 'dw5_b', 'pw5_w', 'pw5_b', 'proj_w', 'proj_b')}
    del _L0_conv_all

    def _L0_ffn_setup():
        import jax, jax.numpy as jnp
        import numpy as np
        B, T, D, H, E = (16, 1024, 64, 128, 8)
        key = jax.random.key(seed)
        ks = jax.random.split(key, 5)
        x = jax.random.normal(ks[0], (B, T, D), dtype=jnp.float32)
        gate_w = jax.random.normal(ks[1], (D, E), dtype=jnp.float32) * 0.02
        gate_b = jnp.zeros((E,), dtype=jnp.float32)
        W1 = jax.random.normal(ks[2], (E, D, H), dtype=jnp.float32) * 0.02
        b1 = jnp.zeros((E, H), dtype=jnp.float32)
        W2 = jax.random.normal(ks[3], (E, H, D), dtype=jnp.float32) * 0.02
        b2 = jnp.zeros((E, D), dtype=jnp.float32)
        return {'x': x, 'gate_w': gate_w, 'gate_b': gate_b, 'W1': W1, 'b1': b1, 'W2': W2, 'b2': b2}
    _L0_ffn_all = _L0_ffn_setup()
    _L0_ffn_in = {k: v for k, v in _L0_ffn_all.items() if k in ('gate_w', 'gate_b', 'W1', 'b1', 'W2', 'b2')}
    del _L0_ffn_all

    def _L1_conv_setup():
        import jax, jax.numpy as jnp
        import numpy as np

        def conv2d_same(x, w, b=None):
            out = jax.lax.conv_general_dilated(x, w, window_strides=(1, 1), padding='SAME', dimension_numbers=('NCHW', 'OIHW', 'NCHW'))
            if b is not None:
                out = out + b[None, :, None, None]
            return out

        def deform_conv(x, offset, wd, k=3, pad=1, dg=4):
            B, C, H, W = x.shape
            cg = C // dg
            K = k * k
            off = offset.reshape(B, dg, K, 2, H, W)
            dy, dx = (off[:, :, :, 0], off[:, :, :, 1])
            ky = (jnp.arange(K) // k - pad).astype(x.dtype)
            kx = (jnp.arange(K) % k - pad).astype(x.dtype)
            hh = jnp.arange(H, dtype=x.dtype)
            ww = jnp.arange(W, dtype=x.dtype)
            py = dy + ky[None, None, :, None, None] + hh[None, None, None, :, None]
            px = dx + kx[None, None, :, None, None] + ww[None, None, None, None, :]
            y0 = jnp.floor(py)
            x0 = jnp.floor(px)
            wy1 = py - y0
            wy0 = 1.0 - wy1
            wx1 = px - x0
            wx0 = 1.0 - wx1
            xg = x.reshape(B, dg, cg, H * W)

            def gather(yi, xi):
                valid = (yi >= 0) & (yi < H) & (xi >= 0) & (xi < W)
                yc = jnp.clip(yi, 0, H - 1).astype(jnp.int32)
                xc = jnp.clip(xi, 0, W - 1).astype(jnp.int32)
                idx = (yc * W + xc).reshape(B, dg, 1, K * H * W)
                g = jnp.take_along_axis(xg, jnp.broadcast_to(idx, (B, dg, cg, K * H * W)), axis=-1)
                g = g.reshape(B, dg, cg, K, H, W)
                return g * valid[:, :, None].astype(x.dtype)
            val = gather(y0, x0) * (wy0 * wx0)[:, :, None] + gather(y0, x0 + 1) * (wy0 * wx1)[:, :, None] + gather(y0 + 1, x0) * (wy1 * wx0)[:, :, None] + gather(y0 + 1, x0 + 1) * (wy1 * wx1)[:, :, None]
            wr = wd.reshape(wd.shape[0], dg, cg, K)
            return jnp.einsum('ogck,bgckhw->bohw', wr, val)
        key = jax.random.key(seed)
        k1, k2, k3, k4 = jax.random.split(key, 4)
        B, C, H, W = (8, 64, 16, 16)
        dg, ks = (4, 3)
        x = jax.random.normal(k1, (B, C, H, W), dtype=jnp.float32)
        w1 = jax.random.normal(k2, (C, C, 3, 3), dtype=jnp.float32) * 0.01
        b1 = jnp.zeros((C,), dtype=jnp.float32)
        w2 = jax.random.normal(k3, (dg * ks * ks * 2, C, 3, 3), dtype=jnp.float32) * 0.01
        b2 = jnp.zeros((dg * ks * ks * 2,), dtype=jnp.float32)
        wd = jax.random.normal(k4, (C, C, ks, ks), dtype=jnp.float32) * 0.01
        return {'x': x, 'w1': w1, 'b1': b1, 'w2': w2, 'b2': b2, 'wd': wd}
    _L1_conv_all = _L1_conv_setup()
    _L1_conv_in = {k: v for k, v in _L1_conv_all.items() if k in ('w1', 'b1', 'w2', 'b2', 'wd')}
    del _L1_conv_all

    def _L1_ffn_setup():
        import jax, jax.numpy as jnp
        import numpy as np
        B, S, D = (8, 1024, 64)
        H = 4 * D
        CAPACITY = 0.5
        key = jax.random.key(seed)
        ks = jax.random.split(key, 6)
        x = jax.random.normal(ks[0], (B, S, D), dtype=jnp.float32)
        attention_mask = jnp.zeros((B, 1, 1, S), dtype=jnp.float32)
        wr = jax.random.normal(ks[1], (D, 1), dtype=jnp.float32) * 0.02
        br = jnp.zeros((1,), dtype=jnp.float32)
        w1 = jax.random.normal(ks[2], (D, H), dtype=jnp.float32) * 0.02
        b1 = jnp.zeros((H,), dtype=jnp.float32)
        w2 = jax.random.normal(ks[3], (H, D), dtype=jnp.float32) * 0.02
        b2 = jnp.zeros((D,), dtype=jnp.float32)
        return {'x': x, 'attention_mask': attention_mask, 'wr': wr, 'br': br, 'w1': w1, 'b1': b1, 'w2': w2, 'b2': b2}
    _L1_ffn_all = _L1_ffn_setup()
    _L1_ffn_in = {k: v for k, v in _L1_ffn_all.items() if k in ('attention_mask', 'wr', 'br', 'w1', 'b1', 'w2', 'b2')}
    del _L1_ffn_all

    def _L2_conv_setup():
        import jax, jax.numpy as jnp
        import numpy as np
        key = jax.random.key(seed)
        k1, k2, k3 = jax.random.split(key, 3)
        B, C, H, W = (8, 64, 24, 24)
        x = jax.random.normal(k1, (B, C, H, W), dtype=jnp.float32)
        weight = jax.random.normal(k2, (4 * C, C), dtype=jnp.float32) * 0.02
        bias = jax.random.normal(k3, (4 * C,), dtype=jnp.float32) * 0.02
        return {'x': x, 'weight': weight, 'bias': bias}
    _L2_conv_all = _L2_conv_setup()
    _L2_conv_in = {k: v for k, v in _L2_conv_all.items() if k in ('weight', 'bias')}
    del _L2_conv_all

    def _L2_ffn_setup():
        import jax, jax.numpy as jnp
        import numpy as np
        BN_EPS = 0.001

        def _bn(h, g, b, m, v):
            return g * (h - m) * jax.lax.rsqrt(v + BN_EPS) + b
        key = jax.random.key(seed)
        ks = jax.random.split(key, 8)
        B, F, Df = (64, 16, 64)
        E, H, D = (8, 64, 64)
        s1 = 1.0 / np.sqrt(Df)
        s2 = 1.0 / np.sqrt(H)
        return {'x': jax.random.normal(ks[0], (B, F, Df), jnp.float32), 'Wr': jax.random.normal(ks[1], (Df, E), jnp.float32) * s1, 'br': jnp.zeros((E,), jnp.float32), 'W1': jax.random.normal(ks[2], (E, Df, H), jnp.float32) * s1, 'b1': jnp.zeros((E, H), jnp.float32), 'g1': jnp.ones((E, H), jnp.float32), 'be1': jnp.zeros((E, H), jnp.float32), 'm1': jnp.zeros((E, H), jnp.float32), 'v1': jnp.ones((E, H), jnp.float32), 'W2': jax.random.normal(ks[3], (E, H, H), jnp.float32) * s2, 'b2': jnp.zeros((E, H), jnp.float32), 'g2': jnp.ones((E, H), jnp.float32), 'be2': jnp.zeros((E, H), jnp.float32), 'm2': jnp.zeros((E, H), jnp.float32), 'v2': jnp.ones((E, H), jnp.float32), 'Wo': jax.random.normal(ks[4], (E, H, D), jnp.float32) * s2, 'bo': jnp.zeros((E, D), jnp.float32)}
    _L2_ffn_all = _L2_ffn_setup()
    _L2_ffn_in = {k: v for k, v in _L2_ffn_all.items() if k in ('Wr', 'br', 'W1', 'b1', 'g1', 'be1', 'm1', 'v1', 'W2', 'b2', 'g2', 'be2', 'm2', 'v2', 'Wo', 'bo')}
    del _L2_ffn_all

    def _L3_conv_setup():
        import jax, jax.numpy as jnp
        import numpy as np
        K = 3

        def dwconv3x3(x, w, b):
            y = jax.lax.conv_general_dilated(x, w, window_strides=(1, 1), padding='SAME', dimension_numbers=('NCHW', 'OIHW', 'NCHW'), feature_group_count=x.shape[1])
            return y + b[None, :, None, None]

        def conv1x1(x, w, b):
            return jnp.einsum('oc,bchw->bohw', w, x) + b[None, :, None, None]

        def extract_patches(x):
            B, C, H, W = x.shape
            p = (K - 1) // 2
            xp = jnp.pad(x, ((0, 0), (0, 0), (p, p), (p, p)))
            return jnp.stack([xp[:, :, i:i + H, j:j + W] for i in range(K) for j in range(K)], axis=2)

        def involution(x, w_red, b_red, w_span, b_span):
            kern = conv1x1(jax.nn.relu(conv1x1(x, w_red, b_red)), w_span, b_span)
            patches = extract_patches(x)
            return jnp.einsum('bkhw,bckhw->bchw', kern, patches)
        key = jax.random.key(seed)
        ks = jax.random.split(key, 10)
        dim, red = (64, 16)
        B, H, W = (8, 16, 16)
        s = 0.05
        return {'x': jax.random.normal(ks[0], (B, dim, H, W), jnp.float32), 'w_in': jax.random.normal(ks[1], (dim, 1, 3, 3), jnp.float32) * s, 'b_in': jax.random.normal(ks[2], (dim,), jnp.float32) * s, 'w_red': jax.random.normal(ks[3], (red, dim), jnp.float32) * s, 'b_red': jax.random.normal(ks[4], (red,), jnp.float32) * s, 'w_span': jax.random.normal(ks[5], (K * K, red), jnp.float32) * s, 'b_span': jax.random.normal(ks[6], (K * K,), jnp.float32) * s, 'w_out': jax.random.normal(ks[7], (dim, 1, 3, 3), jnp.float32) * s, 'b_out': jax.random.normal(ks[8], (dim,), jnp.float32) * s}
    _L3_conv_all = _L3_conv_setup()
    _L3_conv_in = {k: v for k, v in _L3_conv_all.items() if k in ('w_in', 'b_in', 'w_red', 'b_red', 'w_span', 'b_span', 'w_out', 'b_out')}
    del _L3_conv_all

    def _L3_ffn_setup():
        import math
        import jax, jax.numpy as jnp
        import numpy as np
        CAPACITY_FACTOR = 1.25
        key = jax.random.key(seed)
        ks = jax.random.split(key, 5)
        B, L, D, F, E = (8, 2048, 64, 256, 8)
        h = jax.random.normal(ks[0], (B, L, D), dtype=jnp.float32)
        gate_w = jax.random.normal(ks[1], (D, E), dtype=jnp.float32) * 0.02
        gate_b = jnp.zeros((E,), dtype=jnp.float32)
        w1 = jax.random.normal(ks[2], (E, D, F), dtype=jnp.float32) * (1.0 / math.sqrt(D))
        b1 = jnp.zeros((E, F), dtype=jnp.float32)
        w2 = jax.random.normal(ks[3], (E, F, D), dtype=jnp.float32) * (1.0 / math.sqrt(F))
        b2 = jnp.zeros((E, D), dtype=jnp.float32)
        return {'h': h, 'gate_w': gate_w, 'gate_b': gate_b, 'w1': w1, 'b1': b1, 'w2': w2, 'b2': b2}
    _L3_ffn_all = _L3_ffn_setup()
    _L3_ffn_in = {k: v for k, v in _L3_ffn_all.items() if k in ('gate_w', 'gate_b', 'w1', 'b1', 'w2', 'b2')}
    del _L3_ffn_all
    return {'x': x, 'L0_conv_qkv_w': _L0_conv_in['qkv_w'], 'L0_conv_qkv_b': _L0_conv_in['qkv_b'], 'L0_conv_dw3_w': _L0_conv_in['dw3_w'], 'L0_conv_dw3_b': _L0_conv_in['dw3_b'], 'L0_conv_pw3_w': _L0_conv_in['pw3_w'], 'L0_conv_pw3_b': _L0_conv_in['pw3_b'], 'L0_conv_dw5_w': _L0_conv_in['dw5_w'], 'L0_conv_dw5_b': _L0_conv_in['dw5_b'], 'L0_conv_pw5_w': _L0_conv_in['pw5_w'], 'L0_conv_pw5_b': _L0_conv_in['pw5_b'], 'L0_conv_proj_w': _L0_conv_in['proj_w'], 'L0_conv_proj_b': _L0_conv_in['proj_b'], 'L0_ffn_gate_w': _L0_ffn_in['gate_w'], 'L0_ffn_gate_b': _L0_ffn_in['gate_b'], 'L0_ffn_W1': _L0_ffn_in['W1'], 'L0_ffn_b1': _L0_ffn_in['b1'], 'L0_ffn_W2': _L0_ffn_in['W2'], 'L0_ffn_b2': _L0_ffn_in['b2'], 'L1_conv_w1': _L1_conv_in['w1'], 'L1_conv_b1': _L1_conv_in['b1'], 'L1_conv_w2': _L1_conv_in['w2'], 'L1_conv_b2': _L1_conv_in['b2'], 'L1_conv_wd': _L1_conv_in['wd'], 'L1_ffn_attention_mask': _L1_ffn_in['attention_mask'], 'L1_ffn_wr': _L1_ffn_in['wr'], 'L1_ffn_br': _L1_ffn_in['br'], 'L1_ffn_w1': _L1_ffn_in['w1'], 'L1_ffn_b1': _L1_ffn_in['b1'], 'L1_ffn_w2': _L1_ffn_in['w2'], 'L1_ffn_b2': _L1_ffn_in['b2'], 'L2_conv_weight': _L2_conv_in['weight'], 'L2_conv_bias': _L2_conv_in['bias'], 'L2_ffn_Wr': _L2_ffn_in['Wr'], 'L2_ffn_br': _L2_ffn_in['br'], 'L2_ffn_W1': _L2_ffn_in['W1'], 'L2_ffn_b1': _L2_ffn_in['b1'], 'L2_ffn_g1': _L2_ffn_in['g1'], 'L2_ffn_be1': _L2_ffn_in['be1'], 'L2_ffn_m1': _L2_ffn_in['m1'], 'L2_ffn_v1': _L2_ffn_in['v1'], 'L2_ffn_W2': _L2_ffn_in['W2'], 'L2_ffn_b2': _L2_ffn_in['b2'], 'L2_ffn_g2': _L2_ffn_in['g2'], 'L2_ffn_be2': _L2_ffn_in['be2'], 'L2_ffn_m2': _L2_ffn_in['m2'], 'L2_ffn_v2': _L2_ffn_in['v2'], 'L2_ffn_Wo': _L2_ffn_in['Wo'], 'L2_ffn_bo': _L2_ffn_in['bo'], 'L3_conv_w_in': _L3_conv_in['w_in'], 'L3_conv_b_in': _L3_conv_in['b_in'], 'L3_conv_w_red': _L3_conv_in['w_red'], 'L3_conv_b_red': _L3_conv_in['b_red'], 'L3_conv_w_span': _L3_conv_in['w_span'], 'L3_conv_b_span': _L3_conv_in['b_span'], 'L3_conv_w_out': _L3_conv_in['w_out'], 'L3_conv_b_out': _L3_conv_in['b_out'], 'L3_ffn_gate_w': _L3_ffn_in['gate_w'], 'L3_ffn_gate_b': _L3_ffn_in['gate_b'], 'L3_ffn_w1': _L3_ffn_in['w1'], 'L3_ffn_b1': _L3_ffn_in['b1'], 'L3_ffn_w2': _L3_ffn_in['w2'], 'L3_ffn_b2': _L3_ffn_in['b2']}

def reference(x, L0_conv_qkv_w, L0_conv_qkv_b, L0_conv_dw3_w, L0_conv_dw3_b, L0_conv_pw3_w, L0_conv_pw3_b, L0_conv_dw5_w, L0_conv_dw5_b, L0_conv_pw5_w, L0_conv_pw5_b, L0_conv_proj_w, L0_conv_proj_b, L0_ffn_gate_w, L0_ffn_gate_b, L0_ffn_W1, L0_ffn_b1, L0_ffn_W2, L0_ffn_b2, L1_conv_w1, L1_conv_b1, L1_conv_w2, L1_conv_b2, L1_conv_wd, L1_ffn_attention_mask, L1_ffn_wr, L1_ffn_br, L1_ffn_w1, L1_ffn_b1, L1_ffn_w2, L1_ffn_b2, L2_conv_weight, L2_conv_bias, L2_ffn_Wr, L2_ffn_br, L2_ffn_W1, L2_ffn_b1, L2_ffn_g1, L2_ffn_be1, L2_ffn_m1, L2_ffn_v1, L2_ffn_W2, L2_ffn_b2, L2_ffn_g2, L2_ffn_be2, L2_ffn_m2, L2_ffn_v2, L2_ffn_Wo, L2_ffn_bo, L3_conv_w_in, L3_conv_b_in, L3_conv_w_red, L3_conv_b_red, L3_conv_w_span, L3_conv_b_span, L3_conv_w_out, L3_conv_b_out, L3_ffn_gate_w, L3_ffn_gate_b, L3_ffn_w1, L3_ffn_b1, L3_ffn_w2, L3_ffn_b2):
    import jax
    import jax.numpy as jnp

    def _L0_conv_ref(x, qkv_w, qkv_b, dw3_w, dw3_b, pw3_w, pw3_b, dw5_w, dw5_b, pw5_w, pw5_b, proj_w, proj_b):
        import jax, jax.numpy as jnp
        import numpy as np
        IN_CH = 64
        OUT_CH = 64
        DIM = 8
        HEADS = IN_CH // DIM
        TOTAL = HEADS * DIM
        C3 = 3 * TOTAL
        SCALES = (3, 5)
        EPS = 1e-15

        def _conv(x, w, b, groups=1, pad=0):
            y = jax.lax.conv_general_dilated(x, w, window_strides=(1, 1), padding=[(pad, pad), (pad, pad)], dimension_numbers=('NCHW', 'OIHW', 'NCHW'), feature_group_count=groups)
            return y + b[None, :, None, None]

        def _relu_linear_att(qkv):
            B, C, H, W = qkv.shape
            qkv = qkv.reshape(B, -1, 3 * DIM, H * W)
            q = jax.nn.relu(qkv[:, :, :DIM])
            k = jax.nn.relu(qkv[:, :, DIM:2 * DIM])
            v = qkv[:, :, 2 * DIM:]
            v = jnp.concatenate([v, jnp.ones_like(v[:, :, :1])], axis=2)
            vk = jnp.einsum('bhdn,bhen->bhde', v, k)
            out = jnp.einsum('bhde,bhen->bhdn', vk, q)
            out = out[:, :, :-1] / (out[:, :, -1:] + EPS)
            return out.reshape(B, -1, H, W)
        qkv = _conv(x, qkv_w, qkv_b)
        s3 = _conv(_conv(qkv, dw3_w, dw3_b, groups=C3, pad=1), pw3_w, pw3_b, groups=HEADS)
        s5 = _conv(_conv(qkv, dw5_w, dw5_b, groups=C3, pad=2), pw5_w, pw5_b, groups=HEADS)
        multi = jnp.concatenate([qkv, s3, s5], axis=1)
        att = _relu_linear_att(multi)
        return _conv(att, proj_w, proj_b)

    def _L0_ffn_ref(x, gate_w, gate_b, W1, b1, W2, b2):
        import jax, jax.numpy as jnp
        import numpy as np
        B, T, D, H, E = (16, 1024, 64, 128, 8)
        Bb, Tt, Dd = x.shape
        Ee = gate_w.shape[1]
        xf = x.reshape(-1, Dd)
        N = xf.shape[0]
        logits = xf @ gate_w + gate_b
        probs = jax.nn.softmax(logits, axis=-1)
        top2_vals, top2_idx = jax.lax.top_k(probs, 2)
        cw = jnp.zeros((N, Ee), dtype=xf.dtype).at[jnp.arange(N)[:, None], top2_idx].add(top2_vals)

        def step(acc, params):
            w1, bb1, w2, bb2, we = params
            h = jax.nn.gelu(xf @ w1 + bb1, approximate=False)
            y = h @ w2 + bb2
            return (acc + we[:, None] * y, None)
        out, _ = jax.lax.scan(step, jnp.zeros_like(xf), (W1, b1, W2, b2, cw.T))
        return out.reshape(Bb, Tt, Dd)

    def _L1_conv_ref(x, w1, b1, w2, b2, wd):
        import jax, jax.numpy as jnp
        import numpy as np

        def conv2d_same(x, w, b=None):
            out = jax.lax.conv_general_dilated(x, w, window_strides=(1, 1), padding='SAME', dimension_numbers=('NCHW', 'OIHW', 'NCHW'))
            if b is not None:
                out = out + b[None, :, None, None]
            return out

        def deform_conv(x, offset, wd, k=3, pad=1, dg=4):
            B, C, H, W = x.shape
            cg = C // dg
            K = k * k
            off = offset.reshape(B, dg, K, 2, H, W)
            dy, dx = (off[:, :, :, 0], off[:, :, :, 1])
            ky = (jnp.arange(K) // k - pad).astype(x.dtype)
            kx = (jnp.arange(K) % k - pad).astype(x.dtype)
            hh = jnp.arange(H, dtype=x.dtype)
            ww = jnp.arange(W, dtype=x.dtype)
            py = dy + ky[None, None, :, None, None] + hh[None, None, None, :, None]
            px = dx + kx[None, None, :, None, None] + ww[None, None, None, None, :]
            y0 = jnp.floor(py)
            x0 = jnp.floor(px)
            wy1 = py - y0
            wy0 = 1.0 - wy1
            wx1 = px - x0
            wx0 = 1.0 - wx1
            xg = x.reshape(B, dg, cg, H * W)

            def gather(yi, xi):
                valid = (yi >= 0) & (yi < H) & (xi >= 0) & (xi < W)
                yc = jnp.clip(yi, 0, H - 1).astype(jnp.int32)
                xc = jnp.clip(xi, 0, W - 1).astype(jnp.int32)
                idx = (yc * W + xc).reshape(B, dg, 1, K * H * W)
                g = jnp.take_along_axis(xg, jnp.broadcast_to(idx, (B, dg, cg, K * H * W)), axis=-1)
                g = g.reshape(B, dg, cg, K, H, W)
                return g * valid[:, :, None].astype(x.dtype)
            val = gather(y0, x0) * (wy0 * wx0)[:, :, None] + gather(y0, x0 + 1) * (wy0 * wx1)[:, :, None] + gather(y0 + 1, x0) * (wy1 * wx0)[:, :, None] + gather(y0 + 1, x0 + 1) * (wy1 * wx1)[:, :, None]
            wr = wd.reshape(wd.shape[0], dg, cg, K)
            return jnp.einsum('ogck,bgckhw->bohw', wr, val)
        xd = jax.lax.stop_gradient(x)
        offset = conv2d_same(conv2d_same(xd, w1, b1), w2, b2)
        return jax.nn.relu(deform_conv(x, offset, wd, k=3, pad=1, dg=4))

    def _L1_ffn_ref(x, attention_mask, wr, br, w1, b1, w2, b2):
        import jax, jax.numpy as jnp
        import numpy as np
        B, S, D = (8, 1024, 64)
        H = 4 * D
        CAPACITY = 0.5
        b, s, d = x.shape
        weights = (jnp.einsum('bsd,do->bso', x, wr) + br)[..., 0]
        k = max(1, int(CAPACITY * s))
        kk = k - 1 if k > 1 else 1
        _, idx = jax.lax.top_k(weights, k)
        sel_idx = idx[:, :kk]
        sel = jnp.take_along_axis(x, sel_idx[:, :, None], axis=1)
        h = jax.nn.gelu(jnp.einsum('bkd,dh->bkh', sel, w1) + b1)
        y = jnp.einsum('bkh,hd->bkd', h, w2) + b2
        w_sel = jnp.take_along_axis(weights, sel_idx, axis=1)
        y = y * w_sel[..., None]
        batch_idx = jnp.arange(b)[:, None]
        processed = jnp.zeros_like(x).at[batch_idx, sel_idx].set(y)
        return processed + x

    def _L2_conv_ref(x, weight, bias):
        import jax, jax.numpy as jnp
        import numpy as np
        B, C, H, W = x.shape
        xs = x.transpose(0, 2, 3, 1).reshape(B * H, W, C)
        params = jax.nn.sigmoid(jnp.einsum('nwc,oc->nwo', xs, weight) + bias)
        A, Bg, Cg, Dg = jnp.split(params, 4, axis=-1)

        def step(h, inp):
            a_t, b_t, c_t, d_t, x_t = inp
            h = a_t * h + b_t * x_t
            y_t = c_t * h + d_t * x_t
            return (h, y_t)
        h0 = jnp.zeros((B * H, C), dtype=x.dtype)
        seq = (A.swapaxes(0, 1), Bg.swapaxes(0, 1), Cg.swapaxes(0, 1), Dg.swapaxes(0, 1), xs.swapaxes(0, 1))
        _, ys = jax.lax.scan(step, h0, seq)
        y = ys.swapaxes(0, 1).reshape(B, H, W, C).transpose(0, 3, 1, 2)
        return y

    def _L2_ffn_ref(x, Wr, br, W1, b1, g1, be1, m1, v1, W2, b2, g2, be2, m2, v2, Wo, bo):
        import jax, jax.numpy as jnp
        import numpy as np
        BN_EPS = 0.001

        def _bn(h, g, b, m, v):
            return g * (h - m) * jax.lax.rsqrt(v + BN_EPS) + b
        feat = jnp.mean(x, axis=0)
        w = jax.nn.softmax(feat @ Wr + br, axis=-1)
        h = jnp.einsum('bfd,edh->bfeh', x, W1) + b1
        h = jax.nn.relu(_bn(h, g1, be1, m1, v1))
        h = jnp.einsum('bfeh,ehk->bfek', h, W2) + b2
        h = jax.nn.relu(_bn(h, g2, be2, m2, v2))
        y = jnp.einsum('bfeh,ehd->bfed', h, Wo) + bo
        return jnp.einsum('bfed,fe->bfd', y, w)

    def _L3_conv_ref(x, w_in, b_in, w_red, b_red, w_span, b_span, w_out, b_out):
        import jax, jax.numpy as jnp
        import numpy as np
        K = 3

        def dwconv3x3(x, w, b):
            y = jax.lax.conv_general_dilated(x, w, window_strides=(1, 1), padding='SAME', dimension_numbers=('NCHW', 'OIHW', 'NCHW'), feature_group_count=x.shape[1])
            return y + b[None, :, None, None]

        def conv1x1(x, w, b):
            return jnp.einsum('oc,bchw->bohw', w, x) + b[None, :, None, None]

        def extract_patches(x):
            B, C, H, W = x.shape
            p = (K - 1) // 2
            xp = jnp.pad(x, ((0, 0), (0, 0), (p, p), (p, p)))
            return jnp.stack([xp[:, :, i:i + H, j:j + W] for i in range(K) for j in range(K)], axis=2)

        def involution(x, w_red, b_red, w_span, b_span):
            kern = conv1x1(jax.nn.relu(conv1x1(x, w_red, b_red)), w_span, b_span)
            patches = extract_patches(x)
            return jnp.einsum('bkhw,bckhw->bchw', kern, patches)
        x = dwconv3x3(x, w_in, b_in)
        x = involution(x, w_red, b_red, w_span, b_span)
        x = dwconv3x3(x, w_out, b_out)
        return x

    def _L3_ffn_ref(h, gate_w, gate_b, w1, b1, w2, b2):
        import math
        import jax, jax.numpy as jnp
        import numpy as np
        CAPACITY_FACTOR = 1.25
        B, L, D = h.shape
        E = gate_w.shape[1]
        T = B * L
        C = max(1, math.ceil(CAPACITY_FACTOR * T / E))
        x = h.reshape(T, D)
        logits = x @ gate_w + gate_b
        probs = jax.nn.softmax(logits, axis=-1)
        idx = jnp.argmax(probs, axis=-1)
        prb = jnp.take_along_axis(probs, idx[:, None], axis=1)[:, 0]
        one_hot = jax.nn.one_hot(idx, E, dtype=jnp.float32)
        pos = (jnp.cumsum(one_hot, axis=0) * one_hot).sum(-1).astype(jnp.int32) - 1
        kept = pos < C
        pos_safe = jnp.where(kept, pos, C)
        buf = jnp.zeros((E, C, D), dtype=h.dtype).at[idx, pos_safe].set(x, mode='drop')
        hmid = jax.nn.relu(jnp.einsum('ecd,edf->ecf', buf, w1) + b1[:, None, :])
        ybuf = jnp.einsum('ecf,efd->ecd', hmid, w2) + b2[:, None, :]
        pos_g = jnp.minimum(pos, C - 1)
        y_tok = ybuf[idx, pos_g] * (prb * kept)[:, None]
        y = y_tok.reshape(B, L, D)
        y = jnp.nan_to_num(y, nan=0.0, posinf=10000.0, neginf=-10000.0)
        return y

    def _gn(v, G=32, eps=1e-05):
        B_, C_, H_, W_ = v.shape
        g = v.reshape(B_, G, C_ // G, H_, W_)
        m = jnp.mean(g, axis=(2, 3, 4), keepdims=True)
        s = jnp.var(g, axis=(2, 3, 4), keepdims=True)
        return ((g - m) / jnp.sqrt(s + eps)).reshape(v.shape)

    def _ln_c(v, eps=1e-06):
        m = jnp.mean(v, axis=1, keepdims=True)
        s = jnp.var(v, axis=1, keepdims=True)
        return (v - m) / jnp.sqrt(s + eps)

    def _ln_t(v, eps=1e-05):
        m = jnp.mean(v, axis=-1, keepdims=True)
        s = jnp.var(v, axis=-1, keepdims=True)
        return (v - m) / jnp.sqrt(s + eps)

    def _to_tokens(v):
        B_, C_, H_, W_ = v.shape
        return v.reshape(B_, C_, H_ * W_).transpose(0, 2, 1)

    def _from_tokens(t, like):
        B_, C_, H_, W_ = like.shape
        return t.transpose(0, 2, 1).reshape(B_, C_, H_, W_)
    x = x + _L0_conv_ref(_ln_c(x), L0_conv_qkv_w, L0_conv_qkv_b, L0_conv_dw3_w, L0_conv_dw3_b, L0_conv_pw3_w, L0_conv_pw3_b, L0_conv_dw5_w, L0_conv_dw5_b, L0_conv_pw5_w, L0_conv_pw5_b, L0_conv_proj_w, L0_conv_proj_b)
    t = _to_tokens(x)
    t = t + _L0_ffn_ref(_ln_t(t), L0_ffn_gate_w, L0_ffn_gate_b, L0_ffn_W1, L0_ffn_b1, L0_ffn_W2, L0_ffn_b2)
    x = _from_tokens(t, x)
    x = x + _L1_conv_ref(_ln_c(x), L1_conv_w1, L1_conv_b1, L1_conv_w2, L1_conv_b2, L1_conv_wd)
    t = _to_tokens(x)
    t = t + _L1_ffn_ref(_ln_t(t), L1_ffn_attention_mask, L1_ffn_wr, L1_ffn_br, L1_ffn_w1, L1_ffn_b1, L1_ffn_w2, L1_ffn_b2)
    x = _from_tokens(t, x)
    x = x + _L2_conv_ref(_ln_c(x), L2_conv_weight, L2_conv_bias)
    t = _to_tokens(x)
    t = t + _L2_ffn_ref(_ln_t(t), L2_ffn_Wr, L2_ffn_br, L2_ffn_W1, L2_ffn_b1, L2_ffn_g1, L2_ffn_be1, L2_ffn_m1, L2_ffn_v1, L2_ffn_W2, L2_ffn_b2, L2_ffn_g2, L2_ffn_be2, L2_ffn_m2, L2_ffn_v2, L2_ffn_Wo, L2_ffn_bo)
    x = _from_tokens(t, x)
    x = x + _L3_conv_ref(_ln_c(x), L3_conv_w_in, L3_conv_b_in, L3_conv_w_red, L3_conv_b_red, L3_conv_w_span, L3_conv_b_span, L3_conv_w_out, L3_conv_b_out)
    t = _to_tokens(x)
    t = t + _L3_ffn_ref(_ln_t(t), L3_ffn_gate_w, L3_ffn_gate_b, L3_ffn_w1, L3_ffn_b1, L3_ffn_w2, L3_ffn_b2)
    x = _from_tokens(t, x)
    return x

_drawn_inputs = setup_inputs


def setup_inputs(seed=0):
    import zlib

    import numpy as np

    out = dict(_drawn_inputs(seed))
    spreads = {'L0_conv_qkv_b': (0.0, 0.483),
     'L0_conv_dw3_b': (0.0, 0.8),
     'L0_conv_pw3_b': (0.0, 0.449),
     'L0_conv_dw5_b': (0.0, 0.8),
     'L0_conv_pw5_b': (0.0, 0.405),
     'L0_conv_proj_b': (0.0, 0.1),
     'L0_ffn_gate_b': (0.0, 0.405),
     'L0_ffn_b1': (0.0, 0.8),
     'L0_ffn_b2': (0.0, 0.364),
     'L1_conv_b1': (0.0, 0.8),
     'L1_conv_b2': (0.0, 0.302),
     'L1_ffn_b1': (0.0, 0.8),
     'L1_ffn_b2': (0.0, 0.8),
     'L2_ffn_br': (0.0, 0.8),
     'L2_ffn_b1': (0.0, 0.8),
     'L2_ffn_g1': (1.0, 0.6),
     'L2_ffn_be1': (0.0, 0.8),
     'L2_ffn_m1': (0.0, 0.8),
     'L2_ffn_v1': (1.0, 0.6),
     'L2_ffn_b2': (0.0, 0.8),
     'L2_ffn_g2': (1.0, 0.6),
     'L2_ffn_be2': (0.0, 0.769),
     'L2_ffn_m2': (0.0, 0.735),
     'L2_ffn_v2': (1.0, 0.6),
     'L2_ffn_bo': (0.0, 0.555),
     'L3_ffn_gate_b': (0.0, 0.8),
     'L3_ffn_b1': (0.0, 2.0),
     'L3_ffn_b2': (0.0, 2.0)}
    factors = {'L0_conv_qkv_w': 8.0,
     'L0_conv_dw3_w': 8.0,
     'L0_conv_pw3_w': 8.0,
     'L0_conv_dw5_w': 8.0,
     'L0_conv_pw5_w': 8.0,
     'L0_ffn_gate_w': 3.32,
     'L0_ffn_W1': 8.0,
     'L0_ffn_W2': 8.0,
     'L1_conv_w1': 3.98,
     'L1_conv_w2': 3.6,
     'L1_ffn_wr': 8.0,
     'L1_ffn_w1': 8.0,
     'L1_ffn_w2': 8.0,
     'L2_conv_weight': 2.857,
     'L2_conv_bias': 25.893,
     'L3_conv_w_in': 8.0,
     'L3_conv_b_in': 8.0,
     'L3_conv_w_red': 8.0,
     'L3_conv_b_red': 8.0,
     'L3_conv_w_span': 8.0,
     'L3_conv_b_span': 8.0,
     'L3_conv_w_out': 8.0,
     'L3_conv_b_out': 25.42,
     'L3_ffn_gate_w': 7.867,
     'L3_ffn_w1': 8.0,
     'L3_ffn_w2': 8.0}
    for name, (base, spread) in spreads.items():
        noise = np.random.default_rng([zlib.crc32(name.encode()), seed]).standard_normal(out[name].shape)
        drawn = base * np.exp(spread * noise) if base else spread * noise
        out[name] = jnp.asarray(drawn.astype(out[name].dtype))
    for name, factor in factors.items():
        out[name] = (out[name] * factor).astype(out[name].dtype)
    return out
```

```python
from contextlib import ExitStack

import concourse.bass as bass
import numpy as np
from concourse import mybir

ALU = mybir.AluOpType
ACT = mybir.ActivationFunctionType
F32 = mybir.dt.float32
BF16 = mybir.dt.bfloat16
FP16 = mybir.dt.float16
I32 = mybir.dt.int32
AX = mybir.AxisListType

P = 128
B, C, H, W = 8, 64, 16, 16
NB = B // 2
PIX = H * W
COLS = NB * PIX
HC = COLS // 2
TILES = B * PIX // P
PITCH, PW = H + 2, W + 4
PROWS = 2 + NB * PITCH
AROWS = (NB - 1) * PITCH + H
E = 8
HD = 8
SCALES = 3
SAMPLES = 36
CG = 16
FH0, FH1, FH3 = 128, 256, 256
CAP = -(-5 * B * PIX // (4 * E))
TOPK = PIX // 2 - 1
GSCALE = 4096.0
BIG = 1.0e30

SECTIONS = [
    [("center", P), ("mean32", 32), ("spread", 4 * P), ("ident", P), ("ones", P), ("before", E * E), ("epsc", 1), ("epst", 1), ("epsa", 1), ("epsb", 1)],
    [("wq3", 3 * P), ("bq3", 3), ("wkv", 2 * P), ("bkv", SCALES * 2 * P), ("dw5", 75), ("db5", 3), ("dw3", 27), ("db3", 3),
     ("pwq", 6 * P), ("bqq", 3), ("pwkv", 12 * P), ("proj", 3 * P), ("bproj", 1), ("vkmask", P), ("headmask", 32), ("headspread", 4 * P)],
    [("gate0", 2 * E), ("gb0", E), ("w1_0", E * 2 * FH0), ("b1_0", E), ("w2_0", E * C), ("b2_0", C),
     ("sel24", E)],
    [("c1w", 9 * P), ("c1b", 1), ("c2w", 9 * 144), ("c2b", 72), ("pos", 2 * 72),
     ("qidx", 2), ("wd", 5 * C)],
    [("wr1", 2), ("br1", 1), ("before1", 2 * PIX), ("w1_1", 2 * FH1), ("b1_1", 2), ("w2_1", 2 * C), ("b2_1", 1)],
    [("ssw", 4 * P), ("ssb", 4)],
    [("wr2", E), ("br2", E), ("w1_2", E * P), ("w2_2", E * P), ("wo_2", E * P), ("bn1", 5 * E),
     ("bn2", 5 * E), ("bo2", P)],
    [("dwi", 9), ("dbi", 1), ("red", 32), ("bred", 1), ("span", 9 * P), ("dwo", 9), ("dbo", 1)],
    [("gate3", 2 * E), ("gb3", E), ("tri", P), ("w1_3", E * FH3), ("b1_3", E * 2), ("w2_3", E * 2 * C), ("b2_3", C)],
]
AT = {}
WIDTH = []
for _n, _s in enumerate(SECTIONS):
    _at = 0
    for _name, _cols in _s:
        AT[_name] = (_n, _at, _cols)
        _at += _cols
    WIDTH.append(_at)


def build(nc, x_dram, packs, out_dram):
    with ExitStack() as ctx:
        def sb(name, shape, dt=F32, where=None):
            return (where or ctx).enter_context(nc.sbuf_tensor(name, shape, dt))

        def sem(name):
            return ctx.enter_context(nc.semaphore(name))

        X = sb("X", [P, COLS])
        Y = sb("Y", [P, COLS])
        SQ = sb("SQ", [P, COLS])
        SD = sb("SD", [P, COLS])
        wconst = sb("wconst", [P, WIDTH[0]])
        wbuf = [sb(f"wbuf{i}", [P, max(w for n, w in enumerate(WIDTH) if n and n % 2 == i)]) for i in range(2)]
        wsb = [wconst if n == 0 else wbuf[n % 2] for n in range(len(SECTIONS))]
        PS = ctx.enter_context(nc.psum_tensor("PS", [P, 8 * 512], F32))

        def bank(n, cols=512):
            return PS[:, n * 512:n * 512 + cols]

        def wt(name, a=0, n=None, p0=0, p1=P):
            s, at, cols = AT[name]
            n = cols - a if n is None else n
            return wsb[s][p0:p1, at + a:at + a + n]

        x_in = sem("x_in")
        w_in = [sem(f"w_in{n}") for n in range(len(SECTIONS))]
        stored = sem("stored")
        ln_centered, ln_squared, ln_var, ln_sd, ln_rstd, ln_spread, ln_placed, ln_done = (sem(n) for n in (
            "ln_centered", "ln_squared", "ln_var", "ln_sd", "ln_rstd", "ln_spread", "ln_placed", "ln_done"))
        dve_step = sem("dve_step")
        act_step = sem("act_step")
        pool_step = sem("pool_step")
        steps = {"dve": 0, "act": 0, "pool": 0}

        def load_weights(sp, n):
            sp.dma_start(wsb[n][:, 0:WIDTH[n]], packs[n]).then_inc(w_in[n], 16)

        def after(eng, ins):
            steps["dve"] += 1
            ins.then_inc(dve_step, 1)
            eng.wait_ge(dve_step, steps["dve"])

        def after_act(eng, ins):
            steps["act"] += 1
            ins.then_inc(act_step, 1)
            eng.wait_ge(act_step, steps["act"])

        def after_pool(eng, ins):
            steps["pool"] += 1
            ins.then_inc(pool_step, 1)
            eng.wait_ge(pool_step, steps["pool"])

        def ln_pe(pe, n):
            for h in range(2):
                pe.matmul(bank(h), wt("center"), X[:, h * HC:(h + 1) * HC], start=True, stop=True).then_inc(ln_centered, 1)
            for h in range(2):
                pe.wait_ge(ln_squared, 2 * n + h + 1)
                for q in range(4):
                    mm = pe.matmul(bank(2 + h, P)[32 * q:32 * q + 32, :], wt("mean32"), SQ[:, h * HC + q * P:h * HC + (q + 1) * P],
                                   start=True, stop=True, tile_position=(0, 32 * q))
                mm.then_inc(ln_var, 1)
            for h in range(2):
                pe.wait_ge(ln_rstd, 2 * n + h + 1)
                for q in range(4):
                    mm = pe.matmul(bank(2 + h)[:, q * P:(q + 1) * P], wt("spread", q * P, P), SD[:, h * P:(h + 1) * P],
                                   start=True, stop=True)
                mm.then_inc(ln_spread, 1)

        def ln_act(act, n, eps):
            for h in range(2):
                act.wait_ge(ln_centered, 2 * n + h + 1)
                act.activation(SQ[:, h * HC:(h + 1) * HC], bank(h), ACT.Square).then_inc(ln_squared, 1)
            for h in range(2):
                act.wait_ge(ln_var, 2 * n + h + 1)
                act.activation(SD[:, h * P:(h + 1) * P], bank(2 + h, P), ACT.Sqrt, bias=wt(eps)).then_inc(ln_sd, 1)

        def ln_dve(dve, n, out_of):
            for h in range(2):
                o, view = out_of(h)
                dve.wait_ge(ln_squared, 2 * n + h + 1)
                dve.tensor_copy(o, view(bank(h))).then_inc(ln_placed, 1)
            for h in range(2):
                c = slice(h * P, (h + 1) * P)
                dve.wait_ge(ln_sd, 2 * n + h + 1)
                dve.reciprocal(SD[:, c], SD[:, c]).then_inc(ln_rstd, 1)
            for h in range(2):
                o, view = out_of(h)
                dve.wait_ge(ln_placed, 2 * n + h + 1)
                dve.wait_ge(ln_spread, 2 * n + h + 1)
                dve.tensor_tensor(o, o, view(bank(2 + h)), ALU.mult).then_inc(ln_done, 1)

        def flat(h):
            return Y[:, h * HC:(h + 1) * HC], lambda a: a

        def images(a):
            return a.rearrange("p (b r w) -> p b r w", b=2, r=H)

        def pair(pad, h, dy, dx):
            r0 = 2 * h * PITCH + dy
            if r0 + 2 * PITCH <= PROWS:
                v = pad[:, r0:r0 + 2 * PITCH, dx:dx + W].rearrange("p (b r) w -> p b r w", b=2)
                return v[:, :, 0:H, :]
            v = pad[:, r0 - (PITCH - H):r0 + 2 * PITCH - (PITCH - H), dx:dx + W].rearrange("p (b r) w -> p b r w", b=2)
            return v[:, :, PITCH - H:PITCH, :]

        def acc_images(acc, h):
            r0 = 2 * h * PITCH
            if r0 + 2 * PITCH <= AROWS:
                return acc[:, r0:r0 + 2 * PITCH, :].rearrange("p (b r) w -> p b r w", b=2)[:, :, 0:H, :]
            r0 -= PITCH - H
            return acc[:, r0:r0 + 2 * PITCH, :].rearrange("p (b r) w -> p b r w", b=2)[:, :, PITCH - H:PITCH, :]

        def tok(t):
            bh, r = t // (2 * NB), t % (2 * NB)
            return slice(C * bh, C * bh + C), slice(r * P, (r + 1) * P)

        with ExitStack() as sctx, nc.Block() as block:
            QKVP = [sb(f"QKVP{j}", [P, PROWS, PW], F32, sctx) for j in range(3)]
            D5 = [sb(f"D5_{j}", [P, AROWS, W], F32, sctx) for j in range(3)]
            D3 = [sb(f"D3_{j}", [P, COLS], F32, sctx) for j in range(3)]
            QR = [sb(f"QR{s}", [P, COLS], F32, sctx) for s in range(SCALES)]
            ATT = [sb(f"ATT{s}", [P, COLS], F32, sctx) for s in range(SCALES)]
            KV = sb("KV", [P, SCALES, NB, 2, 257], F32, sctx)
            VK = sb("VK", [P, SCALES, NB, P], F32, sctx)
            KSUM = sb("KSUM", [P, SCALES, NB, 32], F32, sctx)
            DG = sb("DG", [P, 27, P], F32, sctx)
            RD = sb("RD", [P, PIX], F32, sctx)
            TAP = [sb(f"TAP{i}", [P, AROWS, W], F32, sctx) for i in range(2)]
            D5B = [sb(f"D5B{i}", [P, AROWS, W], F32, sctx) for i in range(2)]
            padded, diag, ones_set, qkv_in, kv_ps, kv_biased, kv_ready, dw3_ps, d3_ready, d5_ready = (sem(n) for n in (
                "padded", "diag", "ones_set", "qkv_in", "kv_ps", "kv_biased", "kv_ready", "dw3_ps", "d3_ready", "d5_ready"))
            qkv_ps, q_ps, q_ready, vk_ps, vk_ready, den_ps, den_out, den_inv, num_ps, num_out, inv_ps, att_ready, proj_ps = (
                sem(n) for n in ("qkv_ps", "q_ps", "q_ready", "vk_ps", "vk_ready", "den_ps", "den_out", "den_inv", "num_ps",
                                 "num_out", "inv_ps", "att_ready", "proj_ps"))
            tap_ready, tap_used, d5a_ready = sem("tap_ready"), sem("tap_used"), sem("d5a_ready")
            VTAPS = 18
            GTAPS = 25 - VTAPS

            @block.sync
            def _(sp):
                xv = x_dram.rearrange("(g b) c p -> g c b p", g=2)
                for g in range(2):
                    sp.dma_start(X[C * g:C * g + C, :].rearrange("c (b p) -> c b p", b=NB), xv[g]).then_inc(x_in, 16)
                for n in range(3):
                    load_weights(sp, n)

            @block.gpsimd
            def _(pool):
                for j in range(3):
                    pool.memset(QKVP[j][:, :, :], 0.0).then_inc(padded, 1)
                pool.memset(KV[:, :, :, :, 256:257], 1.0).then_inc(ones_set, 1)
                pool.wait_ge(w_in[0], 16)
                pool.wait_ge(w_in[1], 16)
                for m in range(27):
                    pool.tensor_scalar(DG[:, m, :], wt("ident"), wt("dw3", m, 1), None, ALU.mult).then_inc(diag, 1)

                def keys(s):
                    for g in range(NB):
                        pool.wait_ge(kv_biased, 4 * s + g + 1)
                        k = KV[:, s, g, :, 0:P]
                        pool.tensor_scalar(k, k, 0.0, None, ALU.max).then_inc(kv_ready, 1)

                def join(j):
                    pool.wait_ge(d5a_ready, j + 1)
                    pool.tensor_tensor(D5[j][:, :, :], D5[j][:, :, :], D5B[j % 2][:, :, :], ALU.add).then_inc(d5_ready, 1)

                keys(0)
                for j in range(3):
                    for i in range(1, GTAPS):
                        n = j * (GTAPS - 1) + i
                        pool.wait_ge(tap_ready, j * GTAPS + i + 1)
                        pool.tensor_tensor(D5B[j % 2][:, :, :], D5B[j % 2][:, :, :], TAP[n % 2][:, :, :], ALU.add).then_inc(tap_used, 1)
                        pool.wait_ge(tap_used, n)
                    if j >= 1:
                        join(j - 1)
                join(2)
                keys(1)
                keys(2)

            @block.tensor
            def _(pe):
                pe.wait_ge(x_in, 32)
                pe.wait_ge(w_in[0], 16)
                ln_pe(pe, 0)
                pe.wait_ge(w_in[1], 16)
                qbank = [4, 5, 6, 7, 2, 3]
                for j in range(3):
                    for h in range(2):
                        if j == 0 or (j, h) == (2, 0):
                            pe.wait_ge(ln_done, 2 if j else h + 1)
                        pe.matmul(bank(qbank[2 * j + h]), wt("wq3", j * P, P), Y[:, h * HC:(h + 1) * HC],
                                  start=True, stop=True).then_inc(qkv_ps, 1)

                def kv_group(s, g):
                    n = 4 * s + g
                    if n >= 2:
                        pe.wait_ge(kv_biased, n - 1)
                    for i in range(2):
                        r = 2 * g + i
                        cc = slice(r * P, (r + 1) * P)
                        o = bank(n % 2)[:, i * 2 * P:(i + 1) * 2 * P]
                        if s == 0:
                            mm = pe.matmul(o, Y[:, cc], wt("wkv"), start=True, stop=True)
                        else:
                            for j in range(3):
                                r0 = g * PITCH + i * (H // 2)
                                src = D3[j][:, cc] if s == 1 else D5[j][:, r0:r0 + H // 2, :].rearrange("p r w -> p (r w)")
                                mm = pe.matmul(o, src, wt("pwkv", ((s - 1) * 3 + j) * 2 * P, 2 * P),
                                               start=(j == 0), stop=(j == 2))
                    mm.then_inc(kv_ps, 1)

                def vk(s):
                    pe.wait_ge(kv_ready, 4 * s + 4)
                    if s == 0:
                        pe.wait_ge(ones_set, 1)
                    for bp in range(2):
                        n = 2 * s + bp
                        if n >= 2:
                            pe.wait_ge(vk_ready, n - 1)
                            if bp == 1:
                                pe.wait_ge(den_out, s)
                        for i in range(2):
                            for half in range(2):
                                kv = KV[:, s, 2 * bp + i, half, :]
                                mm = pe.matmul(bank(6 + n % 2)[:, i * 129:(i + 1) * 129], kv[:, 0:P], kv[:, P:257],
                                               start=(half == 0), stop=(half == 1))
                        mm.then_inc(vk_ps, 1)

                def den(s):
                    pe.wait_ge(vk_ready, 2 * s + 2)
                    pe.wait_ge(q_ready, 2 * s + 2)
                    for bl in range(NB):
                        mm = pe.matmul(bank(7, PIX)[32 * bl:32 * bl + 32, :], KSUM[:, s, bl, :], QR[s][:, bl * PIX:(bl + 1) * PIX],
                                       start=True, stop=True, tile_position=(0, 32 * bl))
                    mm.then_inc(den_ps, 1)

                def attend(s):
                    for bp in range(2):
                        n = 2 * s + bp
                        if n >= 1:
                            pe.wait_ge(num_out, n)
                        for i in range(2):
                            bl = 2 * bp + i
                            mm = pe.matmul(bank(2)[:, i * PIX:(i + 1) * PIX], VK[:, s, bl, :],
                                           QR[s][:, bl * PIX:(bl + 1) * PIX], start=True, stop=True)
                        mm.then_inc(num_ps, 1)
                        pe.wait_ge(den_inv, s + 1)
                        if n >= 1:
                            pe.wait_ge(att_ready, n)
                        for i in range(2):
                            bl = 2 * bp + i
                            mm = pe.matmul(bank(3)[:, i * PIX:(i + 1) * PIX], wt("headspread", bl * P, P), RD[:, :],
                                           start=True, stop=True)
                        mm.then_inc(inv_ps, 1)

                def queries(s):
                    for h in range(2):
                        if s == 2:
                            pe.wait_ge(q_ready, 3 + h)
                        for j in range(3):
                            src = D3[j][:, h * HC:(h + 1) * HC] if s == 1 else acc_images(D5[j], h)
                            mm = pe.matmul(bank(4 + h), wt("pwq", ((s - 1) * 3 + j) * P, P), src,
                                           start=(j == 0), stop=(j == 2))
                        mm.then_inc(q_ps, 1)

                for g in range(4):
                    kv_group(0, g)
                pe.wait_ge(qkv_in, 6)
                pe.wait_ge(diag, 27)
                for j in range(3):
                    for h in range(2):
                        for m in range(9):
                            mm = pe.matmul(bank(qbank[2 * j + h]), DG[:, j * 9 + m, :],
                                           pair(QKVP[j], h, 1 + m // 3, 1 + m % 3), start=(m == 0), stop=(m == 8))
                        mm.then_inc(dw3_ps, 1)
                pe.wait_ge(d3_ready, 6)
                vk(0)
                queries(1)
                for g in range(4):
                    kv_group(1, g)
                den(0)
                pe.wait_ge(d5_ready, 3)
                queries(2)
                for g in range(4):
                    kv_group(2, g)
                attend(0)
                vk(1)
                den(1)
                vk(2)
                attend(1)
                den(2)
                attend(2)
                pe.wait_ge(att_ready, 2 * SCALES)
                for h in range(2):
                    for s in range(SCALES):
                        mm = pe.matmul(bank(h), wt("proj", s * P, P), ATT[s][:, h * HC:(h + 1) * HC],
                                       start=(s == 0), stop=(s == SCALES - 1))
                    mm.then_inc(proj_ps, 1)

            @block.scalar
            def _(act):
                qbank = [4, 5, 6, 7, 2, 3]
                act.wait_ge(w_in[0], 16)
                ln_act(act, 0, "epsc")
                act.wait_ge(w_in[1], 16)
                act.wait_ge(padded, 3)
                for j in range(3):
                    for h in range(2):
                        act.wait_ge(qkv_ps, 2 * j + h + 1)
                        src = bank(qbank[2 * j + h])
                        if j == 0:
                            act.activation(QR[0][:, h * HC:(h + 1) * HC], src, ACT.Relu, bias=wt("bqq", 0, 1)).then_inc(q_ready, 1)
                        act.activation(pair(QKVP[j], h, 2, 2), images(src), ACT.Identity, bias=wt("bq3", j, 1)).then_inc(qkv_in, 1)

                for j in range(3):
                    act.wait_ge(qkv_in, 2 * j + 2)
                    for i in range(GTAPS):
                        m = VTAPS + i
                        src = QKVP[j][:, m // 5:m // 5 + AROWS, m % 5:m % 5 + W]
                        if i == 0:
                            if j >= 2:
                                act.wait_ge(d5_ready, j - 1)
                            act.activation(D5B[j % 2][:, :, :], src, ACT.Identity, bias=wt("db5", j, 1), scale=wt("dw5", j * 25 + m, 1)).then_inc(tap_ready, 1)
                            continue
                        n = j * (GTAPS - 1) + i
                        if n > 2:
                            act.wait_ge(tap_used, n - 2)
                        act.activation(TAP[n % 2][:, :, :], src, ACT.Copy, scale=wt("dw5", j * 25 + m, 1)).then_inc(tap_ready, 1)
                    for h in range(2):
                        act.wait_ge(dw3_ps, 2 * j + h + 1)
                        act.activation(D3[j][:, h * HC:(h + 1) * HC], bank(qbank[2 * j + h]), ACT.Identity,
                                       bias=wt("db3", j, 1)).then_inc(d3_ready, 1)

                def queries(s):
                    for h in range(2):
                        act.wait_ge(q_ps, 2 * (s - 1) + h + 1)
                        act.activation(QR[s][:, h * HC:(h + 1) * HC], bank(4 + h), ACT.Relu, bias=wt("bqq", s, 1)).then_inc(q_ready, 1)

                def den(s):
                    act.wait_ge(den_ps, s + 1)
                    if s >= 1:
                        act.wait_ge(inv_ps, 2 * s)
                    act.activation(RD[:, :], bank(7, PIX), ACT.Identity, bias=wt("epsa")).then_inc(den_out, 1)

                def numerators(s):
                    for bp in range(2):
                        n = 2 * s + bp
                        act.wait_ge(num_ps, n + 1)
                        act.activation(ATT[s][:, bp * HC:(bp + 1) * HC], bank(2), ACT.Copy).then_inc(num_out, 1)

                queries(1)
                den(0)
                queries(2)
                numerators(0)
                den(1)
                numerators(1)
                den(2)
                numerators(2)

            @block.vector
            def _(dve):
                dve.wait_ge(w_in[0], 16)
                ln_dve(dve, 0, flat)
                dve.wait_ge(w_in[1], 16)

                def kv_bias(s):
                    for g in range(NB):
                        n = 4 * s + g
                        dve.wait_ge(kv_ps, n + 1)
                        bias = wt("bkv", s * 2 * P, 2 * P).rearrange("p (o c) -> p o c", o=1).broadcast_to([P, 2, 2 * P])
                        dve.tensor_tensor(KV[:, s, g, :, 0:2 * P], bank(n % 2).rearrange("p (t c) -> p t c", t=2), bias,
                                          ALU.add).then_inc(kv_biased, 1)

                def mask_vk(s):
                    for bp in range(2):
                        n = 2 * s + bp
                        dve.wait_ge(vk_ps, n + 1)
                        for i in range(2):
                            ps = bank(6 + n % 2)[:, i * 129:(i + 1) * 129]
                            dve.tensor_tensor(VK[:, s, 2 * bp + i, :], ps[:, 0:P], wt("vkmask"), ALU.mult)
                            ins = dve.tensor_scalar(KSUM[:, s, 2 * bp + i, :], wt("headmask"), ps[:, P:P + 1], None, ALU.mult)
                        ins.then_inc(vk_ready, 1)

                def invert(s):
                    dve.wait_ge(den_out, s + 1)
                    dve.reciprocal(RD[:, :], RD[:, :]).then_inc(den_inv, 1)

                def divide(s):
                    for bp in range(2):
                        n = 2 * s + bp
                        a = ATT[s][:, bp * HC:(bp + 1) * HC]
                        dve.wait_ge(num_out, n + 1)
                        dve.wait_ge(inv_ps, n + 1)
                        dve.tensor_tensor(a, a, bank(3), ALU.mult).then_inc(att_ready, 1)

                def depthwise5(j):
                    for m in range(VTAPS):
                        src = QKVP[j][:, m // 5:m // 5 + AROWS, m % 5:m % 5 + W]
                        w = wt("dw5", j * 25 + m, 1)
                        if m == 0:
                            after(dve, dve.tensor_scalar(D5[j][:, :, :], src, w, None, ALU.mult))
                        else:
                            ins = dve.scalar_tensor_tensor(out=D5[j][:, :, :], in0=src, scalar=w, in1=D5[j][:, :, :],
                                                           op0=ALU.mult, op1=ALU.add)
                            if m < VTAPS - 1:
                                after(dve, ins)
                            else:
                                ins.then_inc(d5a_ready, 1)

                kv_bias(0)
                dve.wait_ge(qkv_in, 6)
                for j in range(3):
                    depthwise5(j)
                mask_vk(0)
                kv_bias(1)
                invert(0)
                kv_bias(2)
                divide(0)
                mask_vk(1)
                invert(1)
                mask_vk(2)
                divide(1)
                invert(2)
                divide(2)
                for h in range(2):
                    c = slice(h * HC, (h + 1) * HC)
                    dve.wait_ge(proj_ps, h + 1)
                    dve.scalar_tensor_tensor(out=X[:, c], in0=bank(h), scalar=wt("bproj"), in1=X[:, c],
                                             op0=ALU.add, op1=ALU.add)

        def softmax_dve(dve, LG, RED, n, exps, k, summed):
            mx = RED[:, 0:n].rearrange("p (t o) -> p t o", o=1)
            after(dve, dve.tensor_reduce(RED[:, 0:n], LG[:, :, :], AX.X, ALU.max))
            dve.tensor_tensor(LG[:, :, :], LG[:, :, :], mx.broadcast_to([P, n, E]), ALU.subtract).then_inc(exps, 1)
            dve.wait_ge(summed, k)
            after(dve, dve.tensor_reduce(RED[:, 0:n], LG[:, :, :], AX.X, ALU.add))
            after(dve, dve.reciprocal(RED[:, 0:n], RED[:, 0:n]))
            after(dve, dve.tensor_tensor(LG[:, :, :], LG[:, :, :], mx.broadcast_to([P, n, E]), ALU.mult))

        def rank_dve(dve, PR, CMP, CMP2, RANK):
            shape = [P, TILES, E, E]
            ej = PR[:, :, :].rearrange("p t (o j) -> p t o j", o=1).broadcast_to(shape)
            ee = PR[:, :, :].rearrange("p t (e o) -> p t e o", o=1).broadcast_to(shape)
            low = wt("before").rearrange("p (o e j) -> p o e j", o=1, e=E).broadcast_to(shape)
            dve.tensor_tensor(CMP[:, :, :, :], ej, ee, ALU.is_gt)
            after(dve, dve.tensor_tensor(CMP2[:, :, :, :], ej, ee, ALU.is_equal))
            after(dve, dve.tensor_tensor(CMP2[:, :, :, :], CMP2[:, :, :, :], low, ALU.mult))
            after(dve, dve.tensor_tensor(CMP[:, :, :, :], CMP[:, :, :, :], CMP2[:, :, :, :], ALU.add))
            after(dve, dve.tensor_reduce(RANK[:, :, :], CMP[:, :, :, :], AX.X, ALU.add))

        with ExitStack() as sctx, nc.Block() as block:
            LG = sb("LG", [P, TILES, E], F32, sctx)
            RED = sb("RED", [P, TILES], F32, sctx)
            CMP = sb("CMP", [P, TILES, E, E], F32, sctx)
            CMP2 = sb("CMP2", [P, TILES, E, E], F32, sctx)
            RANK = sb("RANK", [P, TILES, E], F32, sctx)
            CW3 = sb("CW3", [P, TILES, 3, E], BF16, sctx)
            CWT = sb("CWT", [P, TILES * P], F32, sctx)
            CWT3 = sb("CWT3", [P, TILES * P], BF16, sctx)
            SELB = sb("SELB", [P, E * P], BF16, sctx)
            IDB = sb("IDB", [P, P], BF16, sctx)
            HID = sb("HID", [P, 2, HC], F32, sctx)
            HS = sb("HS", [P, 4, HC], F32, sctx)
            g_ps, g_exp, g_sum, cw_ready, cwt_ps, cwt_in, hid_ps, hid_in, bc_ps, hs_ready, hs_used, f0_ps, cast0, cwt3_ps = (
                sem(n) for n in ("g_ps", "g_exp", "g_sum", "cw_ready", "cwt_ps", "cwt_in", "hid_ps", "hid_in",
                                 "bc_ps", "hs_ready", "hs_used", "f0_ps", "cast0", "cwt3_ps"))
            CH = 4
            zeroed = sem("zeroed")

            @block.sync
            def _(sp):
                load_weights(sp, 3)

            @block.gpsimd
            def _(pool):
                pool.memset(CWT[:, :], 0.0).then_inc(zeroed, 1)
                pool.memset(CWT3[:, :], 0.0).then_inc(zeroed, 1)

            @block.tensor
            def _(pe):
                ln_pe(pe, 1)
                pe.wait_ge(w_in[2], 16)
                for r in range(TILES // 2):
                    pe.wait_ge(ln_done, 3 + r // NB)
                    mm = pe.matmul(bank(4)[:, r * 2 * E:(r + 1) * 2 * E], Y[:, r * P:(r + 1) * P], wt("gate0"), start=True, stop=True)
                mm.then_inc(g_ps, 1)
                pe.wait_ge(cw_ready, 1)
                for q in range(4):
                    for i in range(4):
                        t = 4 * q + i
                        mm = pe.transpose(bank(q)[0:E, i * P:(i + 1) * P], LG[:, t, :], wt("ident"))
                    mm.then_inc(cwt_ps, 1)
                pe.wait_ge(cast0, 2)
                for q in range(2):
                    for i in range(8):
                        t = 8 * q + i
                        o = bank(4 + q).bitcast(BF16)
                        mm = pe.transpose(o[0:3 * E, i * P:(i + 1) * P], CW3[:, t, :, :].rearrange("p s e -> p (s e)"), IDB[:, :])
                    mm.then_inc(cwt3_ps, 1)
                pe.wait_ge(cwt_in, 6)

                def up(n):
                    e, bp, bh = n // CH, (n // 2) % 2, n % 2
                    if n >= 3:
                        pe.wait_ge(hid_in, n - 2)
                        pe.wait_ge(hs_ready, n - 2)
                    pe.matmul(bank(2 + n % 3), wt("w1_0", (2 * e + bh) * FH0, FH0), Y[:, bp * HC:(bp + 1) * HC],
                              start=True, stop=True).then_inc(hid_ps, 1)
                    pe.matmul(bank(5 + n % 3), SELB[:, e * P:(e + 1) * P], CWT3[:, (2 * bh + bp) * HC:(2 * bh + bp + 1) * HC],
                              start=True, stop=True).then_inc(bc_ps, 1)

                def down(n):
                    e, bp = n // CH, (n // 2) % 2
                    for bh in range(2):
                        pe.wait_ge(hs_ready, n + bh + 1)
                        pe.matmul(bank(bp)[C * bh:C * bh + C, :], wt("w2_0", e * C, C), HS[:, (n + bh) % 4, :],
                                  start=(e == 0), stop=False).then_inc(hs_used, 1)

                up(0)
                up(1)
                for n in range(0, E * CH, 2):
                    if n + 2 < E * CH:
                        up(n + 2)
                        up(n + 3)
                    down(n)
                for bp in range(2):
                    for bh in range(2):
                        mm = pe.matmul(bank(bp)[C * bh:C * bh + C, :], wt("b2_0"), CWT[:, (2 * bh + bp) * HC:(2 * bh + bp + 1) * HC],
                                       start=False, stop=True)
                    mm.then_inc(f0_ps, 1)

            @block.scalar
            def _(act):
                ln_act(act, 1, "epst")
                act.wait_ge(w_in[2], 16)
                act.wait_ge(g_exp, 1)
                act.activation(LG[:, :, :], LG[:, :, :], ACT.Exp).then_inc(g_sum, 1)
                act.wait_ge(zeroed, 2)
                for q in range(4):
                    act.wait_ge(cwt_ps, q + 1)
                    act.activation(CWT[0:E, q * HC:(q + 1) * HC], bank(q)[0:E, :], ACT.Copy).then_inc(cwt_in, 1)
                for q in range(2):
                    act.wait_ge(cwt3_ps, q + 1)
                    act.activation(CWT3[0:3 * E, q * 1024:(q + 1) * 1024], bank(4 + q).bitcast(BF16)[0:3 * E, :], ACT.Copy).then_inc(cwt_in, 1)
                for n in range(E * CH):
                    act.wait_ge(hid_ps, n + 1)
                    if n >= 2:
                        act.wait_ge(hs_ready, n - 1)
                    act.activation(HID[:, n % 2, :], bank(2 + n % 3), ACT.Gelu, bias=wt("b1_0", n // CH, 1)).then_inc(hid_in, 1)

            @block.vector
            def _(dve):
                ln_dve(dve, 1, flat)
                dve.wait_ge(w_in[2], 16)
                sel = wt("sel24").rearrange("p (e o) -> p e o", o=1).broadcast_to([P, E, P])
                dve.tensor_copy(SELB[:, :].rearrange("p (e m) -> p e m", e=E), sel).then_inc(cast0, 1)
                dve.tensor_copy(IDB[:, :], wt("ident"))
                dve.wait_ge(g_ps, 1)
                for bh in range(2):
                    gb = wt("gb0").rearrange("p (o e) -> p o e", o=1).broadcast_to([P, 8, E])
                    raw = bank(4, TILES * E).rearrange("p (r h e) -> p h r e", h=2, e=E)
                    ins = dve.tensor_tensor(LG[:, 8 * bh:8 * bh + 8, :], raw[:, bh], gb, ALU.add)
                after(dve, ins)
                softmax_dve(dve, LG, RED, TILES, g_exp, 1, g_sum)
                rank_dve(dve, LG, CMP, CMP2, RANK)
                after(dve, dve.tensor_scalar(RANK[:, :, :], RANK[:, :, :], 2.0, None, ALU.is_lt))
                dve.tensor_tensor(LG[:, :, :], LG[:, :, :], RANK[:, :, :], ALU.mult).then_inc(cw_ready, 1)
                dve.wait_ge(cw_ready, 1)
                after(dve, dve.tensor_copy(CW3[:, :, 0, :], LG[:, :, :]))
                after(dve, dve.tensor_tensor(RANK[:, :, :], LG[:, :, :], CW3[:, :, 0, :], ALU.subtract))
                after(dve, dve.tensor_copy(CW3[:, :, 1, :], RANK[:, :, :]))
                after(dve, dve.tensor_tensor(RANK[:, :, :], RANK[:, :, :], CW3[:, :, 1, :], ALU.subtract))
                dve.tensor_copy(CW3[:, :, 2, :], RANK[:, :, :]).then_inc(cast0, 1)
                for n in range(E * CH):
                    dve.wait_ge(hid_in, n + 1)
                    dve.wait_ge(bc_ps, n + 1)
                    if n >= 4:
                        dve.wait_ge(hs_used, n - 3)
                    dve.tensor_tensor(HS[:, n % 4, :], bank(5 + n % 3), HID[:, n % 2, :], ALU.mult).then_inc(hs_ready, 1)
                for bp in range(2):
                    c = slice(bp * HC, (bp + 1) * HC)
                    dve.wait_ge(f0_ps, bp + 1)
                    dve.tensor_tensor(X[:, c], bank(bp), X[:, c], ALU.add)

        with ExitStack() as sctx, nc.Block() as block:
            VTA = sb("VTA", [P, 5, TILES * P], F32, sctx)
            front = VTA[:, :, :].rearrange("p n c -> p (n c)")
            YP = front[:, 0:PROWS * PW].rearrange("p (r w) -> p r w", w=PW)
            shifted = [front[:, PROWS * (PW + k * W):PROWS * (PW + (k + 1) * W)].rearrange("p (r w) -> p r w", w=W) for k in range(5)]
            XS, HS3 = shifted[0:2], shifted[2:5]
            GX = sb("GX", [P, 2, 2, NB, 4, P], FP16, sctx)
            PY = sb("PY", [P, TILES, 72], F32, sctx)
            BASE = sb("BASE", [P, TILES, 72], F32, sctx)
            U0 = sb("U0", [P, TILES, 72], F32, sctx)
            U1 = sb("U1", [P, TILES, 72], F32, sctx)
            WC = sb("WC", [P, SAMPLES, TILES, 4], F32, sctx)
            IDX = sb("IDX", [P, TILES, SAMPLES], FP16, sctx)
            IDXT = sb("IDXT", [SAMPLES, TILES * P], FP16, sctx)
            IDH = sb("IDH", [P, P], FP16, sctx)
            SELH = sb("SELH", [SAMPLES, SAMPLES * P], FP16, sctx)
            BC = sb("BC", [P, 2, 2048], FP16, sctx)
            OH = sb("OH", [P, 2, 2, 2048], FP16, sctx)
            U = [a[:, :].rearrange("p (t k c) -> p t k c", t=TILES, k=4) for a in (SQ, SD)]
            V1 = sb("V1", [P, TILES, 2, CG], F32, sctx)
            VAL = sb("VAL", [P, 2, TILES, 8, CG], F32, sctx)
            (y_pad, c1_ps, h_in, h_pad, c2_ps, gx_ps, gx_hi, gx_done, idx_ready, cast1, idxt_ps, idxt_in, bcx_ps, bcx_in,
             oh_ready, oh_used, ga_ps, u_ready, u_used, val_ready, vt_ps, vt_in, dc_ps, xs_ready) = (
                sem("s3_" + n) for n in ("y_pad", "c1_ps", "h_in", "h_pad", "c2_ps", "gx_ps", "gx_hi", "gx_done", "idx_ready",
                "cast1", "idxt_ps", "idxt_in", "bcx_ps", "bcx_in", "oh_ready", "oh_used", "ga_ps", "u_ready", "u_used",
                "val_ready", "vt_ps", "vt_in", "dc_ps", "xs_ready"))

            @block.sync
            def _(sp):
                load_weights(sp, 4)

            def padded_y(h):
                return pair(YP, h, 2, 2), images

            @block.gpsimd
            def _(pool):
                pool.memset(YP[:, :, :], 0.0).then_inc(y_pad, 1)
                for k in range(3):
                    pool.memset(HS3[k][:, :, :], 0.0).then_inc(h_pad, 1)
                for s in range(SAMPLES):
                    pool.wait_ge(u_ready, s + 1)
                    after_pool(pool, pool.tensor_tensor(V1[:, :, :, :], U[s % 2][:, :, 0:2, :], U[s % 2][:, :, 2:4, :], ALU.add))
                    if s >= 16 and s % 8 == 0:
                        pool.wait_ge(vt_ps, 4 * (s // 8 - 1))
                    pool.tensor_tensor(VAL[:, (s // 8) % 2, :, s % 8, :], V1[:, :, 0, :], V1[:, :, 1, :], ALU.add).then_inc(val_ready, 1)
                    steps["pool"] += 0
                    pool.wait_ge(val_ready, s + 1)

            @block.tensor
            def _(pe):
                ln_pe(pe, 2)
                pe.wait_ge(w_in[3], 16)
                for h in range(2):
                    pe.wait_ge(ln_done, 5 + h)
                    for m in range(9):
                        mm = pe.matmul(bank(4 + h), wt("c1w", m * P, P), pair(YP, h, 1 + m // 3, 1 + m % 3),
                                       start=(m == 0), stop=(m == 8))
                    mm.then_inc(c1_ps, 1)
                pe.wait_ge(xs_ready, 2)
                for n in range(2 * NB):
                    bl, qh = n // 2, n % 2
                    if n >= 4:
                        pe.wait_ge(gx_done, n - 3)
                    for k in range(4):
                        r0 = bl * PITCH + 2 + qh * (H // 2) + k // 2
                        src = XS[k % 2][:, r0:r0 + H // 2, :].rearrange("p r w -> p (r w)")
                        mm = pe.transpose(bank(n % 4)[:, k * P:(k + 1) * P], src, wt("ident"))
                    mm.then_inc(gx_ps, 1)
                pe.wait_ge(h_in, 6)
                pe.wait_ge(gx_done, 2 * NB)
                for g in range(NB):
                    for i in range(2):
                        for m in range(9):
                            r0 = g * PITCH + i * (H // 2) + 1 + m // 3
                            src = HS3[m % 3][:, r0:r0 + H // 2, :].rearrange("p r w -> p (r w)")
                            mm = pe.matmul(bank(g)[:, i * 144:(i + 1) * 144], src, wt("c2w", m * 144, 144),
                                           start=(m == 0), stop=(m == 8))
                    mm.then_inc(c2_ps, 1)
                pe.wait_ge(idx_ready, 1)
                for q in range(2):
                    for i in range(8):
                        mm = pe.transpose(bank(6 + q).bitcast(FP16)[0:SAMPLES, i * P:(i + 1) * P], IDX[:, 8 * q + i, :], IDH[:, :])
                    mm.then_inc(idxt_ps, 1)
                pe.wait_ge(idxt_in, 2)

                def spread(s):
                    for q in range(2):
                        n = 2 * s + q
                        if n >= 1:
                            pe.wait_ge(bcx_in, n)
                        for i in range(2):
                            c = (2 * q + i) * 512
                            mm = pe.matmul(bank(2 + i), SELH[:, s * P:(s + 1) * P], IDXT[:, c:c + 512], start=True, stop=True)
                        mm.then_inc(bcx_ps, 1)

                def gather(s):
                    g = s // 9
                    pe.wait_ge(oh_ready, s + 1)
                    for half in range(2):
                        if s >= 2:
                            pe.wait_ge(u_ready, s - 1)
                        for i in range(8):
                            t = 8 * half + i
                            o = bank(4 + 2 * (s % 2) + half)[:, i * 64:(i + 1) * 64]
                            for qh in range(2):
                                for part in range(2):
                                    src = GX[:, part, qh, i // 2, :, half * C + g * CG:half * C + (g + 1) * CG]
                                    mm = pe.matmul(o, OH[:, s % 2, qh, t * P:(t + 1) * P], src,
                                                   start=(qh == 0 and part == 0), stop=(qh == 1 and part == 1))
                    mm.then_inc(ga_ps, 1)

                def contract(ch):
                    ns = min(8, SAMPLES - 8 * ch)
                    rows = ns * CG
                    pe.wait_ge(val_ready, 8 * ch + ns)
                    for q in range(4):
                        n = 4 * ch + q
                        if n >= 1:
                            pe.wait_ge(vt_in, n)
                        for i in range(4):
                            src = VAL[:, ch % 2, 4 * q + i, 0:ns, :].rearrange("p s c -> p (s c)")
                            mm = pe.transpose(bank(1)[0:rows, i * P:(i + 1) * P], src, wt("ident"))
                        mm.then_inc(vt_ps, 1)
                    return rows

                spread(0)
                for s in range(SAMPLES):
                    if s + 1 < SAMPLES:
                        spread(s + 1)
                    gather(s)
                    if s >= 9 and s % 8 == 1:
                        contract(s // 8 - 1)
                contract(4)
                pe.wait_ge(vt_in, 20)
                for bp in range(2):
                    for ch in range(5):
                        rows = P if ch < 4 else 64
                        for bh in range(2):
                            mm = pe.matmul(bank(2 + bp)[C * bh:C * bh + C, :], wt("wd", ch * C, C, 0, rows),
                                           VTA[0:rows, ch, (2 * bh + bp) * HC:(2 * bh + bp + 1) * HC],
                                           start=(ch == 0), stop=(ch == 4))
                    mm.then_inc(dc_ps, 1)

            @block.scalar
            def _(act):
                ln_act(act, 2, "epsc")
                act.wait_ge(w_in[3], 16)
                act.wait_ge(h_pad, 3)
                for h in range(2):
                    act.wait_ge(c1_ps, h + 1)
                    for k in range(3):
                        a, b = max(0, 1 - k), min(W, W + 1 - k)
                        act.activation(pair(HS3[k], h, 2, 0)[:, :, :, a:b], images(bank(4 + h))[:, :, :, a + k - 1:b + k - 1],
                                       ACT.Identity, bias=wt("c1b")).then_inc(h_in, 1)
                for n in range(2 * NB):
                    bl, qh = n // 2, n % 2
                    act.wait_ge(gx_ps, n + 1)
                    act.activation(GX[:, 0, qh, bl, :, :], bank(n % 4).rearrange("p (k c) -> p k c", k=4), ACT.Copy,
                                   scale=GSCALE).then_inc(gx_hi, 1)
                for q in range(2):
                    act.wait_ge(idxt_ps, q + 1)
                    act.activation(IDXT[:, q * 1024:(q + 1) * 1024], bank(6 + q).bitcast(FP16)[0:SAMPLES, :], ACT.Copy).then_inc(idxt_in, 1)

                def spread(s):
                    for q in range(2):
                        n = 2 * s + q
                        act.wait_ge(bcx_ps, n + 1)
                        if s >= 2:
                            act.wait_ge(oh_ready, s - 1)
                        act.activation(BC[:, s % 2, q * 1024:(q + 1) * 1024], PS[:, 1024:2048], ACT.Copy).then_inc(bcx_in, 1)

                def evac(ch):
                    rows = P if ch < 4 else 64
                    for q in range(4):
                        act.wait_ge(vt_ps, 4 * ch + q + 1)
                        act.activation(VTA[0:rows, ch, q * 512:(q + 1) * 512], bank(1)[0:rows, :], ACT.Copy).then_inc(vt_in, 1)
                        
                spread(0)
                for s in range(SAMPLES):
                    if s + 1 < SAMPLES:
                        spread(s + 1)
                    if s >= 9 and s % 8 == 1:
                        evac(s // 8 - 1)
                evac(4)

            @block.vector
            def _(dve):
                dve.wait_ge(y_pad, 1)
                ln_dve(dve, 2, padded_y)
                dve.wait_ge(w_in[3], 16)
                dve.wait_ge(ln_done, 6)
                for k in range(2):
                    dve.tensor_copy(XS[k][:, :, :], YP[:, :, 2 + k:2 + k + W]).then_inc(xs_ready, 1)
                dve.tensor_copy(IDH[:, :], wt("ident"))
                sel = wt("ident", 0, SAMPLES, 0, SAMPLES).rearrange("p (s o) -> p s o", o=1).broadcast_to([SAMPLES, SAMPLES, P])
                dve.tensor_copy(SELH[:, :].rearrange("p (s m) -> p s m", s=SAMPLES), sel).then_inc(cast1, 1)
                for n in range(2 * NB):
                    bl, qh = n // 2, n % 2
                    dve.wait_ge(gx_hi, n + 1)
                    dve.scalar_tensor_tensor(out=GX[:, 1, qh, bl, :, :].rearrange("p k c -> p (k c)"), in0=bank(n % 4), scalar=GSCALE,
                                             in1=GX[:, 0, qh, bl, :, :].rearrange("p k c -> p (k c)"), op0=ALU.mult,
                                             op1=ALU.subtract).then_inc(gx_done, 1)
                bias = wt("c2b").rearrange("p (o q k) -> p o q k", o=1, q=1).broadcast_to([P, 2, 2, 72])
                for g in range(NB):
                    dve.wait_ge(c2_ps, g + 1)
                    o = PY[:, :, :].rearrange("p (h r) k -> p h r k", h=2)[:, :, 2 * g:2 * g + 2, :]
                    ins = dve.tensor_tensor(o, bank(g, 288).rearrange("p (r h k) -> p h r k", r=2, h=2), bias, ALU.add)
                after(dve, ins)
                pos = wt("pos").rearrange("p (o h k) -> p o h k", o=1, h=2).broadcast_to([P, B, 2, 72])
                pyv = PY[:, :, :].rearrange("p (b h) k -> p b h k", h=2)
                after(dve, dve.tensor_tensor(pyv, pyv, pos, ALU.add))
                after(dve, dve.tensor_scalar(BASE[:, :, :], PY[:, :, :], -0.5, 0.0, ALU.add, ALU.max))
                after(dve, dve.tensor_scalar(BASE[:, :, :], BASE[:, :, :], float(H - 2), 8388608.0, ALU.min, ALU.add))
                after(dve, dve.tensor_scalar(BASE[:, :, :], BASE[:, :, :], -8388608.0, None, ALU.add))
                after(dve, dve.scalar_tensor_tensor(out=IDX[:, :, :], in0=BASE[:, :, 0:36], scalar=float(W), in1=BASE[:, :, 36:72],
                                                    op0=ALU.mult, op1=ALU.add))
                dve.tensor_tensor(PY[:, :, :], PY[:, :, :], BASE[:, :, :], ALU.subtract).then_inc(idx_ready, 1)
                dve.wait_ge(idx_ready, 1)
                dve.tensor_scalar(U0[:, :, :], PY[:, :, :], -1.0, 1.0, ALU.mult, ALU.add)
                after(dve, dve.tensor_scalar(U1[:, :, :], PY[:, :, :], -1.0, 2.0, ALU.mult, ALU.add))
                dve.scalar_tensor_tensor(out=U0[:, :, :], in0=PY[:, :, :], scalar=1.0, in1=U0[:, :, :], op0=ALU.add, op1=ALU.min)
                after(dve, dve.scalar_tensor_tensor(out=U1[:, :, :], in0=PY[:, :, :], scalar=0.0, in1=U1[:, :, :],
                                                    op0=ALU.add, op1=ALU.min))
                dve.tensor_scalar(U0[:, :, :], U0[:, :, :], 0.0, None, ALU.max)
                after(dve, dve.tensor_scalar(U1[:, :, :], U1[:, :, :], 0.0, None, ALU.max))
                for k in range(4):
                    wy = (U0, U1)[k // 2][:, :, 0:36].rearrange("p t s -> p s t")
                    wx = (U0, U1)[k % 2][:, :, 36:72].rearrange("p t s -> p s t")
                    ins = dve.scalar_tensor_tensor(out=WC[:, :, :, k], in0=wy, scalar=1.0 / GSCALE, in1=wx, op0=ALU.mult, op1=ALU.mult)
                after(dve, ins)

                def compare(s):
                    dve.wait_ge(bcx_in, 2 * s + 2)
                    if s >= 2:
                        dve.wait_ge(ga_ps, s - 1)
                    for qh in range(2):
                        ins = dve.tensor_scalar(OH[:, s % 2, qh, :], BC[:, s % 2, :], wt("qidx", qh, 1), None, ALU.is_equal)
                    ins.then_inc(oh_ready, 1)

                def weigh(s):
                    dve.wait_ge(ga_ps, s + 1)
                    if s >= 2:
                        dve.wait_ge(val_ready, s - 1)
                    for half in range(2):
                        o = U[s % 2][:, 8 * half:8 * half + 8, :, :].rearrange("p t k c -> p (t k) c")
                        src = bank(4 + 2 * (s % 2) + half).rearrange("p (k c) -> p k c", c=CG)
                        w = WC[:, s, 8 * half:8 * half + 8, :].rearrange("p t (k o) -> p (t k) o", o=1).broadcast_to([P, 32, CG])
                        ins = dve.tensor_tensor(o, src, w, ALU.mult)
                    ins.then_inc(u_ready, 1)

                compare(0)
                for s in range(SAMPLES):
                    if s + 1 < SAMPLES:
                        compare(s + 1)
                    weigh(s)
                for bp in range(2):
                    c = slice(bp * HC, (bp + 1) * HC)
                    dve.wait_ge(dc_ps, bp + 1)
                    dve.scalar_tensor_tensor(out=X[:, c], in0=bank(2 + bp), scalar=0.0, in1=X[:, c], op0=ALU.max, op1=ALU.add)

        with ExitStack() as sctx, nc.Block() as block:
            WCOL = sb("WCOL", [P, TILES], F32, sctx)
            WSEL = sb("WSEL", [P, TILES], F32, sctx)
            CNT = sb("CNT", [P, 2, TILES], F32, sctx)
            JUNK = sb("JUNK", [P, 2, TILES, PIX], F32, sctx)
            DIAG = sb("DIAG", [P, TILES, P], F32, sctx)
            DIAG2 = sb("DIAG2", [P, TILES, P], F32, sctx)
            WMB = sb("WMB", [P, COLS], F32, sctx)
            HID = sb("HID1", [P, 4, HC], F32, sctx)
            w_ps, dg_ready, row_ps, dg2_ready, wm_ps, wm_in, hid_ps, hid_in, hid_used, f_ps = (sem("s4_" + n) for n in (
                "w_ps", "dg_ready", "row_ps", "dg2_ready", "wm_ps", "wm_in", "hid_ps", "hid_in", "hid_used", "f_ps"))
            UNITS = [(bh, bp, m) for bp in range(2) for m in range(2) for bh in range(2)]

            @block.sync
            def _(sp):
                load_weights(sp, 5)

            @block.tensor
            def _(pe):
                ln_pe(pe, 3)
                pe.wait_ge(w_in[4], 16)
                for r in range(TILES // 2):
                    pe.wait_ge(ln_done, 7 + r // NB)
                    mm = pe.matmul(bank(4)[:, r * 2:(r + 1) * 2], Y[:, r * P:(r + 1) * P], wt("wr1"), start=True, stop=True)
                mm.then_inc(w_ps, 1)
                for q in range(4):
                    pe.wait_ge(dg_ready, q + 1)
                    pe.matmul(bank(q), wt("ones"), DIAG[:, 4 * q:4 * q + 4, :], start=True, stop=True).then_inc(row_ps, 1)
                pe.wait_ge(dg2_ready, 1)
                for bp in range(2):
                    for bh in range(2):
                        q = 2 * bh + bp
                        mm = pe.matmul(bank(6 + bp)[C * bh:C * bh + C, :], wt("ones", 0, C), DIAG2[:, 4 * q:4 * q + 4, :],
                                       start=True, stop=True)
                    mm.then_inc(wm_ps, 1)

                def up(n):
                    bh, bp, m = UNITS[n]
                    if n >= 2:
                        pe.wait_ge(hid_in, n - 1)
                    pe.matmul(bank(2 + n % 2), wt("w1_1", bh * FH1 + m * P, P),
                              Y[:, bp * HC:(bp + 1) * HC], start=True, stop=True).then_inc(hid_ps, 1)

                up(0)
                up(1)
                for n in range(0, len(UNITS), 2):
                    if n + 2 < len(UNITS):
                        up(n + 2)
                        up(n + 3)
                    for i in range(2):
                        bh, bp, m = UNITS[n + i]
                        pe.wait_ge(hid_in, n + i + 1)
                        pe.matmul(bank(bp)[C * bh:C * bh + C, :], wt("w2_1", m * C, C), HID[:, (n + i) % 4, :],
                                  start=(m == 0), stop=(m == 1)).then_inc(hid_used, 1)

            @block.scalar
            def _(act):
                ln_act(act, 3, "epst")
                act.wait_ge(w_in[4], 16)
                for bp in range(2):
                    act.wait_ge(wm_ps, bp + 1)
                    act.activation(WMB[:, bp * HC:(bp + 1) * HC], bank(6 + bp), ACT.Copy).then_inc(wm_in, 1)
                for n, (bh, bp, m) in enumerate(UNITS):
                    act.wait_ge(hid_ps, n + 1)
                    if n >= 4:
                        act.wait_ge(hid_used, n - 3)
                    act.activation(HID[:, n % 4, :], bank(2 + n % 2), ACT.Gelu_apprx_tanh, bias=wt("b1_1", m, 1)).then_inc(hid_in, 1)

            @block.vector
            def _(dve):
                ln_dve(dve, 3, flat)
                dve.wait_ge(w_in[4], 16)
                dve.wait_ge(w_ps, 1)
                for bh in range(2):
                    raw = bank(4, TILES).rearrange("p (r h) -> p h r", h=2)
                    ins = dve.tensor_scalar(WCOL[:, 8 * bh:8 * bh + 8], raw[:, bh], wt("br1"), None, ALU.add)
                after(dve, ins)
                for t in range(TILES):
                    ins = dve.tensor_scalar(DIAG[:, t, :], wt("ident"), WCOL[:, t:t + 1], None, ALU.mult)
                    if t % 4 == 3:
                        ins.then_inc(dg_ready, 1)
                for t in range(TILES):
                    dve.wait_ge(row_ps, t // 4 + 1)
                    row = bank(t // 4)[:, ((t // 2) % 2) * PIX:((t // 2) % 2 + 1) * PIX]
                    dve.tensor_scalar(JUNK[:, 0, t, :], row, WCOL[:, t:t + 1], None, ALU.is_gt, ALU.add, accum_out=CNT[:, 0, t:t + 1])
                    ins = dve.scalar_tensor_tensor(out=JUNK[:, 1, t, :], in0=row, scalar=WCOL[:, t:t + 1],
                                                   in1=wt("before1", (t % 2) * PIX, PIX), op0=ALU.is_equal, op1=ALU.mult,
                                                   accum_out=CNT[:, 1, t:t + 1])
                after(dve, ins)
                after(dve, dve.tensor_tensor(WSEL[:, :], CNT[:, 0, :], CNT[:, 1, :], ALU.add))
                after(dve, dve.tensor_scalar(WSEL[:, :], WSEL[:, :], float(TOPK), None, ALU.is_lt))
                after(dve, dve.tensor_tensor(WSEL[:, :], WSEL[:, :], WCOL[:, :], ALU.mult))
                for t in range(TILES):
                    ins = dve.tensor_scalar(DIAG2[:, t, :], wt("ident"), WSEL[:, t:t + 1], None, ALU.mult)
                ins.then_inc(dg2_ready, 1)
                after(dve, dve.tensor_tensor(X[:, :], X[:, :], Y[:, :], ALU.add))
                for bp in range(2):
                    c = slice(bp * HC, (bp + 1) * HC)
                    dve.wait_ge(hid_used, 4 * bp + 4)
                    dve.wait_ge(wm_in, bp + 1)
                    after(dve, dve.scalar_tensor_tensor(out=SQ[:, c], in0=bank(bp), scalar=wt("b2_1"), in1=WMB[:, c],
                                                        op0=ALU.add, op1=ALU.mult))
                    dve.tensor_tensor(X[:, c], X[:, c], SQ[:, c], ALU.add)

        with ExitStack() as sctx, nc.Block() as block:
            GATES = [sb(f"GATE{k}", [P, COLS], F32, sctx) for k in range(4)]
            ST = sb("ST", [P, COLS], F32, sctx)
            gate_ps, gate_in = sem("s5_gate_ps"), sem("s5_gate_in")
            gbank = [4, 5, 6, 7, 0, 1, 2, 3]

            @block.sync
            def _(sp):
                load_weights(sp, 6)

            @block.tensor
            def _(pe):
                ln_pe(pe, 4)
                pe.wait_ge(w_in[5], 16)
                for k in range(4):
                    for h in range(2):
                        if k == 0:
                            pe.wait_ge(ln_done, 9 + h)
                        pe.matmul(bank(gbank[2 * k + h]), wt("ssw", k * P, P), Y[:, h * HC:(h + 1) * HC],
                                  start=True, stop=True).then_inc(gate_ps, 1)

            @block.scalar
            def _(act):
                ln_act(act, 4, "epsc")
                act.wait_ge(w_in[5], 16)
                for k in range(4):
                    for h in range(2):
                        act.wait_ge(gate_ps, 2 * k + h + 1)
                        act.activation(GATES[k][:, h * HC:(h + 1) * HC], bank(gbank[2 * k + h]), ACT.Sigmoid,
                                       bias=wt("ssb", k, 1)).then_inc(gate_in, 1)

            @block.vector
            def _(dve):
                ln_dve(dve, 4, flat)
                A, BG, CG_, DG_ = GATES
                dve.wait_ge(gate_in, 2)
                dve.memset(A[:, :].rearrange("p (r w) -> p r w", w=W)[:, :, 0:1], 0.0)
                dve.wait_ge(gate_in, 4)
                after(dve, dve.tensor_tensor(BG[:, :], BG[:, :], Y[:, :], ALU.mult))
                after(dve, dve.tensor_tensor_scan(ST[:, :], A[:, :], BG[:, :], 0.0, ALU.mult, ALU.add))
                dve.wait_ge(gate_in, 8)
                dve.tensor_tensor(DG_[:, :], DG_[:, :], Y[:, :], ALU.mult)
                after(dve, dve.tensor_tensor(CG_[:, :], CG_[:, :], ST[:, :], ALU.mult))
                after(dve, dve.tensor_tensor(X[:, :], X[:, :], DG_[:, :], ALU.add))
                dve.tensor_tensor(X[:, :], X[:, :], CG_[:, :], ALU.add)

        with ExitStack() as sctx, nc.Block() as block:
            SUM = sb("SUM", [P, PIX], F32, sctx)
            LG = sb("LG2", [P, 2, E], F32, sctx)
            RED = sb("RED2", [P, 2], F32, sctx)
            WT = sb("WT", [E, PIX], F32, sctx)
            SEL2 = sb("SEL2", [E, E, P], F32, sctx)
            WB = sb("WB", [P, E, PIX], F32, sctx)
            BNS = [sb(f"BNS{i}", [P, E], F32, sctx) for i in range(2)]
            BNT = [sb(f"BNT{i}", [P, E], F32, sctx) for i in range(2)]
            H1 = sb("H1", [P, 2, HC], F32, sctx)
            H2 = sb("H2", [P, 2, HC], F32, sctx)
            H2W = sb("H2W", [P, 2, HC], F32, sctx)
            (bn_sd, bn_done, sum_done, g_ps, g_exp, g_sum, g_ready, wt_ps, wt_in, wb_ps, wb_in, a_ps, a_in, b_ps, b_in, weighted,
             c_done, f_ps) = (sem("s6_" + n) for n in (
                "bn_sd", "bn_done", "sum_done", "g_ps", "g_exp", "g_sum", "g_ready", "wt_ps", "wt_in", "wb_ps", "wb_in", "a_ps",
                "a_in", "b_ps", "b_in", "weighted", "c_done", "f_ps"))
            NU = 2 * E

            @block.sync
            def _(sp):
                load_weights(sp, 7)

            @block.tensor
            def _(pe):
                ln_pe(pe, 5)
                pe.wait_ge(w_in[6], 16)
                pe.wait_ge(sum_done, 1)
                for h in range(2):
                    mm = pe.matmul(bank(4)[:, h * E:(h + 1) * E], SUM[:, h * P:(h + 1) * P], wt("wr2"), start=True, stop=True)
                mm.then_inc(g_ps, 1)
                pe.wait_ge(g_ready, 1)
                for h in range(2):
                    mm = pe.transpose(bank(5)[0:E, h * P:(h + 1) * P], LG[:, h, :], wt("ident"))
                mm.then_inc(wt_ps, 1)
                pe.wait_ge(wt_in, 1)
                for q in range(4):
                    for i in range(2):
                        mm = pe.matmul(bank(4 + q)[:, i * PIX:(i + 1) * PIX], SEL2[:, 2 * q + i, :], WT[:, :], start=True, stop=True)
                    mm.then_inc(wb_ps, 1)
                pe.wait_ge(wb_in, 4)

                def first(n):
                    e, h = n // 2, n % 2
                    if n >= 2:
                        pe.wait_ge(a_in, n - 1)
                    pe.matmul(bank(2 + n % 2), wt("w1_2", e * P, P), Y[:, h * HC:(h + 1) * HC], start=True, stop=True).then_inc(a_ps, 1)

                def second(n):
                    pe.wait_ge(a_in, n + 1)
                    if n >= 2:
                        pe.wait_ge(b_in, n - 1)
                    pe.matmul(bank(4 + n % 2), wt("w2_2", (n // 2) * P, P), H1[:, n % 2, :], start=True, stop=True).then_inc(b_ps, 1)

                def third(n):
                    pe.wait_ge(weighted, n + 1)
                    pe.matmul(bank(n % 2), wt("wo_2", (n // 2) * P, P), H2W[:, n % 2, :], start=(n < 2), stop=False).then_inc(c_done, 1)

                first(0)
                for n in range(NU):
                    if n + 1 < NU:
                        first(n + 1)
                    second(n)
                    if n >= 1:
                        third(n - 1)
                third(NU - 1)
                for h in range(2):
                    rhs = WT[:, :].rearrange("p (o n) -> p o n", o=1).broadcast_to([E, 2, PIX])
                    pe.matmul(bank(h), wt("bo2", 0, P, 0, E), rhs, start=False, stop=True).then_inc(f_ps, 1)

            @block.scalar
            def _(act):
                ln_act(act, 5, "epst")
                act.wait_ge(w_in[6], 16)
                for i in range(2):
                    act.activation(BNS[i][:, :], wt(f"bn{i + 1}", 4 * E, E), ACT.Sqrt, bias=wt("epsb")).then_inc(bn_sd, 1)
                act.wait_ge(g_exp, 1)
                act.activation(LG[:, :, :], LG[:, :, :], ACT.Exp).then_inc(g_sum, 1)
                act.wait_ge(wt_ps, 1)
                act.activation(WT[:, :], bank(5)[0:E, 0:PIX], ACT.Copy).then_inc(wt_in, 1)
                for q in range(4):
                    act.wait_ge(wb_ps, q + 1)
                    act.activation(WB[:, 2 * q:2 * q + 2, :], bank(4 + q).rearrange("p (e n) -> p e n", e=2), ACT.Copy).then_inc(wb_in, 1)
                act.wait_ge(bn_done, 1)

                def relu1(n):
                    act.wait_ge(a_ps, n + 1)
                    if n >= 2:
                        act.wait_ge(b_ps, n - 1)
                    act.activation(H1[:, n % 2, :], bank(2 + n % 2), ACT.Relu, bias=BNT[0][:, n // 2:n // 2 + 1],
                                   scale=BNS[0][:, n // 2:n // 2 + 1]).then_inc(a_in, 1)

                def relu2(n):
                    act.wait_ge(b_ps, n + 1)
                    if n >= 2:
                        act.wait_ge(weighted, n - 1)
                    act.activation(H2[:, n % 2, :], bank(4 + n % 2), ACT.Relu, bias=BNT[1][:, n // 2:n // 2 + 1],
                                   scale=BNS[1][:, n // 2:n // 2 + 1]).then_inc(b_in, 1)

                relu1(0)
                for n in range(NU):
                    if n + 1 < NU:
                        relu1(n + 1)
                    relu2(n)

            @block.vector
            def _(dve):
                ln_dve(dve, 5, flat)
                dve.wait_ge(ln_done, 12)
                dve.tensor_reduce(SUM[:, :], Y[:, :].rearrange("p (b n) -> p n b", b=NB), AX.X, ALU.add).then_inc(sum_done, 1)
                dve.wait_ge(w_in[6], 16)
                dve.tensor_copy(SEL2[:, :, :], wt("ident", 0, E, 0, E).rearrange("p (e o) -> p e o", o=1).broadcast_to([E, E, P]))
                dve.wait_ge(bn_sd, 2)
                for i in range(2):
                    name = f"bn{i + 1}"
                    after(dve, dve.reciprocal(BNS[i][:, :], BNS[i][:, :]))
                    dve.tensor_tensor(BNS[i][:, :], BNS[i][:, :], wt(name, E, E), ALU.mult)
                    after(dve, dve.tensor_tensor(BNT[i][:, :], wt(name, 0, E), wt(name, 3 * E, E), ALU.subtract))
                    after(dve, dve.tensor_tensor(BNT[i][:, :], BNT[i][:, :], BNS[i][:, :], ALU.mult))
                    ins = dve.tensor_tensor(BNT[i][:, :], BNT[i][:, :], wt(name, 2 * E, E), ALU.add)
                ins.then_inc(bn_done, 1)
                dve.wait_ge(g_ps, 1)
                br = wt("br2").rearrange("p (o e) -> p o e", o=1).broadcast_to([P, 2, E])
                after(dve, dve.scalar_tensor_tensor(out=LG[:, :, :], in0=bank(4, 2 * E).rearrange("p (h e) -> p h e", h=2),
                                                    scalar=1.0 / B, in1=br, op0=ALU.mult, op1=ALU.add))
                softmax_dve(dve, LG, RED, 2, g_exp, 1, g_sum)
                dve.engine_nop().then_inc(g_ready, 1)
                dve.wait_ge(wb_in, 4)
                for n in range(NU):
                    dve.wait_ge(b_in, n + 1)
                    if n >= 2:
                        dve.wait_ge(c_done, n - 1)
                    w = WB[:, n // 2, :].rearrange("p (o n) -> p o n", o=1).broadcast_to([P, 2, PIX])
                    dve.tensor_tensor(H2W[:, n % 2, :].rearrange("p (b n) -> p b n", b=2),
                                      H2[:, n % 2, :].rearrange("p (b n) -> p b n", b=2), w, ALU.mult).then_inc(weighted, 1)
                for h in range(2):
                    c = slice(h * HC, (h + 1) * HC)
                    dve.wait_ge(f_ps, h + 1)
                    dve.tensor_tensor(X[:, c], bank(h), X[:, c], ALU.add)

        with ExitStack() as sctx, nc.Block() as block:
            YP, ZP, OP = (sb(n, [P, PROWS, PW], F32, sctx) for n in ("YP7", "ZP7", "OP7"))
            DGI = sb("DGI", [P, 18, P], F32, sctx)
            R = sb("R", [33, COLS], F32, sctx)
            M = sb("M7", [P, 2, HC], F32, sctx)
            ACC = sb("ACC7", [P, COLS], F32, sctx)
            y_pad, pads, diag, ones_set, z_ps, z_in, r_ps, r_in, k_ps, k_used, o_ready, o_ps = (sem("s7_" + n) for n in (
                "y_pad", "pads", "diag", "ones_set", "z_ps", "z_in", "r_ps", "r_in", "k_ps", "k_used", "o_ready", "o_ps"))

            def padded_y7(h):
                return pair(YP, h, 2, 2), images

            @block.sync
            def _(sp):
                load_weights(sp, 8)

            @block.gpsimd
            def _(pool):
                pool.memset(YP[:, :, :], 0.0).then_inc(y_pad, 1)
                for b in (ZP, OP):
                    pool.memset(b[:, :, :], 0.0).then_inc(pads, 1)
                pool.wait_ge(w_in[7], 16)
                for i, name in enumerate(("dwi", "dwo")):
                    for m in range(9):
                        pool.tensor_scalar(DGI[:, 9 * i + m, :], wt("ident"), wt(name, m, 1), None, ALU.mult).then_inc(diag, 1)

            @block.tensor
            def _(pe):
                ln_pe(pe, 6)
                pe.wait_ge(w_in[7], 16)
                pe.wait_ge(diag, 9)
                for h in range(2):
                    pe.wait_ge(ln_done, 13 + h)
                    for m in range(9):
                        mm = pe.matmul(bank(4 + h), DGI[:, m, :], pair(YP, h, 1 + m // 3, 1 + m % 3), start=(m == 0), stop=(m == 8))
                    mm.then_inc(z_ps, 1)
                for h in range(2):
                    pe.wait_ge(z_in, h + 1)
                    pe.matmul(bank(6 + h)[0:32, :], wt("red"), pair(ZP, h, 2, 2), start=True, stop=True).then_inc(r_ps, 1)
                pe.wait_ge(r_in, 2)
                pe.wait_ge(ones_set, 1)
                for n in range(18):
                    if n >= 4:
                        pe.wait_ge(k_used, n - 3)
                    pe.matmul(bank(n % 4), wt("span", (n // 2) * P, P, 0, 33), R[:, (n % 2) * HC:(n % 2 + 1) * HC],
                              start=True, stop=True).then_inc(k_ps, 1)
                pe.wait_ge(diag, 18)
                pe.wait_ge(o_ready, 2)
                for h in range(2):
                    for m in range(9):
                        mm = pe.matmul(bank(4 + h), DGI[:, 9 + m, :], pair(OP, h, 1 + m // 3, 1 + m % 3), start=(m == 0), stop=(m == 8))
                    mm.then_inc(o_ps, 1)

            @block.scalar
            def _(act):
                ln_act(act, 6, "epsc")
                act.wait_ge(w_in[7], 16)
                act.wait_ge(pads, 1)
                for h in range(2):
                    act.wait_ge(z_ps, h + 1)
                    act.activation(pair(ZP, h, 2, 2), images(bank(4 + h)), ACT.Identity, bias=wt("dbi")).then_inc(z_in, 1)
                for h in range(2):
                    act.wait_ge(r_ps, h + 1)
                    act.activation(R[0:32, h * HC:(h + 1) * HC], bank(6 + h)[0:32, :], ACT.Relu, bias=wt("bred", 0, 1, 0, 32)).then_inc(r_in, 1)

            @block.vector
            def _(dve):
                dve.memset(R[32:33, :], 1.0).then_inc(ones_set, 1)
                dve.wait_ge(y_pad, 1)
                ln_dve(dve, 6, padded_y7)
                dve.wait_ge(w_in[7], 16)
                dve.wait_ge(pads, 2)
                dve.wait_ge(z_in, 2)
                for n in range(18):
                    k, h = n // 2, n % 2
                    c = slice(h * HC, (h + 1) * HC)
                    dve.wait_ge(k_ps, n + 1)
                    o = ACC[:, c] if k == 0 else M[:, n % 2, :]
                    dve.tensor_tensor(images(o), images(bank(n % 4)), pair(ZP, h, 1 + k // 3, 1 + k % 3), ALU.mult).then_inc(k_used, 1)
                    dve.wait_ge(k_used, n + 1)
                    if k == 8:
                        dve.tensor_tensor(pair(OP, h, 2, 2), images(ACC[:, c]), images(M[:, n % 2, :]), ALU.add).then_inc(o_ready, 1)
                    elif k:
                        after(dve, dve.tensor_tensor(ACC[:, c], ACC[:, c], M[:, n % 2, :], ALU.add))
                for h in range(2):
                    c = slice(h * HC, (h + 1) * HC)
                    dve.wait_ge(o_ps, h + 1)
                    dve.scalar_tensor_tensor(out=X[:, c], in0=bank(4 + h), scalar=wt("dbo"), in1=X[:, c], op0=ALU.add, op1=ALU.add)

        with ExitStack() as sctx, nc.Block() as block:
            LG = sb("LG8", [P, TILES, E], F32, sctx)
            RED = sb("RED8", [P, TILES], F32, sctx)
            CMP = sb("CMP8", [P, TILES, E, E], F32, sctx)
            CMP2 = sb("CMP28", [P, TILES, E, E], F32, sctx)
            RANK = sb("RANK8", [P, TILES, E], F32, sctx)
            OH8 = sb("OH8", [P, TILES, E], F32, sctx)
            TOT = sb("TOT", [P, 3, TILES, E], F32, sctx)
            GATE = sb("GATE8", [P, 2, TILES], F32, sctx)
            DIAG = sb("DIAG8", [P, TILES, P], F32, sctx)
            YU = sb("YU", [P, TILES * P], F32, sctx)
            OHT = sb("OHT", [P, TILES * P], F32, sctx)
            SCB = sb("SCB", [P, COLS], F32, sctx)
            HID = sb("HID8", [P, 4, HC], F32, sctx)
            FIN = sb("FIN", [P, 4, HC], F32, sctx)
            MASK = sb("MASK8", [P, HC], I32, sctx)
            (g_ps, g_exp, g_sum, oh_ready, cum_ps, nm_ready, t_ps, t_in, yu_in, scale_ready, sc_ps, sc_in, hid_ps, hid_in_a, hid_in_v,
             hid_used, f_ps) = (sem("s8_" + n) for n in (
                "g_ps", "g_exp", "g_sum", "oh_ready", "cum_ps", "nm_ready", "t_ps", "t_in", "yu_in", "scale_ready", "sc_ps", "sc_in",
                "hid_ps", "hid_in_a", "hid_in_v", "hid_used", "f_ps"))
            UNITS = [(e, m, bp, bh) for e in range(E) for bp in range(2) for m in range(2) for bh in range(2)]
            NU = len(UNITS)
            zeroed = sem("s8_zeroed")

            @block.gpsimd
            def _(pool):
                pool.memset(YU[:, :], 0.0).then_inc(zeroed, 1)
                pool.memset(OHT[:, :], 0.0).then_inc(zeroed, 1)

            @block.tensor
            def _(pe):
                ln_pe(pe, 7)
                pe.wait_ge(w_in[8], 16)
                for r in range(TILES // 2):
                    pe.wait_ge(ln_done, 15 + r // NB)
                    mm = pe.matmul(bank(4)[:, r * 2 * E:(r + 1) * 2 * E], Y[:, r * P:(r + 1) * P], wt("gate3"), start=True, stop=True)
                mm.then_inc(g_ps, 1)
                pe.wait_ge(oh_ready, 1)
                oh = OH8[:, :, :].rearrange("p t e -> p (t e)")
                pe.matmul(bank(6, P), wt("tri"), oh, start=True, stop=True)
                pe.matmul(bank(7, P), wt("ones"), oh, start=True, stop=True).then_inc(cum_ps, 1)
                for k in range(2):
                    if k == 1:
                        pe.wait_ge(nm_ready, 1)
                        pe.wait_ge(t_in, 4)
                    for q in range(4):
                        for i in range(4):
                            mm = pe.transpose(bank(q)[0:E, i * P:(i + 1) * P], (OH8, RANK)[k][:, 4 * q + i, :], wt("ident"))
                        mm.then_inc(t_ps, 1)
                pe.wait_ge(t_in, 8)
                pe.wait_ge(yu_in, 2)

                def up(n):
                    e, m, bp, bh = UNITS[n]
                    if n >= 4:
                        pe.wait_ge((hid_in_a, hid_in_v)[n % 2], n // 2 - 1)
                    pe.matmul(bank(2 + n % 4), wt("w1_3", e * FH3 + m * P, P), YU[:, (2 * bh + bp) * HC:(2 * bh + bp + 1) * HC],
                              start=True, stop=True).then_inc(hid_ps, 1)

                up(0)
                up(1)
                for n in range(0, NU, 2):
                    if n + 2 < NU:
                        up(n + 2)
                        up(n + 3)
                    for i, hid_in in enumerate((hid_in_a, hid_in_v)):
                        e, m, bp, bh = UNITS[n + i]
                        pe.wait_ge(hid_in, n // 2 + 1)
                        pe.matmul(bank(bp)[C * bh:C * bh + C, :], wt("w2_3", (2 * e + m) * C, C), HID[:, (n + i) % 4, :],
                                  start=(e == 0 and m == 0), stop=False).then_inc(hid_used, 1)
                for bp in range(2):
                    for bh in range(2):
                        mm = pe.matmul(bank(bp)[C * bh:C * bh + C, :], wt("b2_3"),
                                       OHT[:, (2 * bh + bp) * HC:(2 * bh + bp + 1) * HC], start=False, stop=True)
                    mm.then_inc(f_ps, 1)
                pe.wait_ge(scale_ready, 1)
                for bp in range(2):
                    for bh in range(2):
                        q = 2 * bh + bp
                        mm = pe.matmul(bank(6 + bp)[C * bh:C * bh + C, :], wt("ones", 0, C), DIAG[:, 4 * q:4 * q + 4, :],
                                       start=True, stop=True)
                    mm.then_inc(sc_ps, 1)

            @block.scalar
            def _(act):
                ln_act(act, 7, "epst")
                act.wait_ge(w_in[8], 16)
                act.wait_ge(ln_done, 16)
                act.wait_ge(zeroed, 2)
                for bh in range(2):
                    act.activation(YU[0:C, bh * COLS:(bh + 1) * COLS], Y[C * bh:C * bh + C, :], ACT.Copy).then_inc(yu_in, 1)
                act.wait_ge(g_exp, 1)
                act.activation(LG[:, :, :], LG[:, :, :], ACT.Exp).then_inc(g_sum, 1)
                for k in range(2):
                    for q in range(4):
                        act.wait_ge(t_ps, 4 * k + q + 1)
                        o = OHT[0:E, q * HC:(q + 1) * HC] if k == 0 else YU[C:C + E, q * HC:(q + 1) * HC]
                        act.activation(o, bank(q)[0:E, :], ACT.Copy).then_inc(t_in, 1)
                for n in range(0, NU, 2):
                    e, m, bp, bh = UNITS[n]
                    act.wait_ge(hid_ps, n + 1)
                    if n >= 4:
                        act.wait_ge(hid_used, n - 3)
                    act.activation(HID[:, n % 4, :], bank(2 + n % 4), ACT.Relu, bias=wt("b1_3", 2 * e + m, 1)).then_inc(hid_in_a, 1)
                for bp in range(2):
                    act.wait_ge(sc_ps, bp + 1)
                    act.activation(SCB[:, bp * HC:(bp + 1) * HC], bank(6 + bp), ACT.Copy).then_inc(sc_in, 1)

            @block.vector
            def _(dve):
                ln_dve(dve, 7, flat)
                dve.wait_ge(w_in[8], 16)
                dve.wait_ge(g_ps, 1)
                for bh in range(2):
                    gb = wt("gb3").rearrange("p (o e) -> p o e", o=1).broadcast_to([P, 8, E])
                    raw = bank(4, TILES * E).rearrange("p (r h e) -> p h r e", h=2, e=E)
                    ins = dve.tensor_tensor(LG[:, 8 * bh:8 * bh + 8, :], raw[:, bh], gb, ALU.add)
                after(dve, ins)
                softmax_dve(dve, LG, RED, TILES, g_exp, 1, g_sum)
                rank_dve(dve, LG, CMP, CMP2, RANK)
                dve.tensor_scalar(OH8[:, :, :], RANK[:, :, :], 1.0, None, ALU.is_lt).then_inc(oh_ready, 1)
                dve.wait_ge(oh_ready, 1)
                dve.tensor_scalar(RANK[:, :, :], RANK[:, :, :], 1.0, None, ALU.is_ge).then_inc(nm_ready, 1)
                dve.tensor_reduce(GATE[:, 0, :], LG[:, :, :], AX.X, ALU.max)
                dve.wait_ge(cum_ps, 1)
                tot = bank(7, P).rearrange("p (t e) -> p t e", e=E)
                after(dve, dve.tensor_copy(TOT[:, 0, :, :], tot))
                for i, d in enumerate((1, 2, 4, 8)):
                    src, dst = TOT[:, i % 2], TOT[:, (i + 1) % 2]
                    dve.tensor_copy(dst[:, 0:d, :], src[:, 0:d, :])
                    after(dve, dve.tensor_tensor(dst[:, d:TILES, :], src[:, d:TILES, :], src[:, 0:TILES - d, :], ALU.add))
                after(dve, dve.tensor_tensor(TOT[:, 1, :, :], TOT[:, 0, :, :], tot, ALU.subtract))
                after(dve, dve.tensor_tensor(TOT[:, 1, :, :], TOT[:, 1, :, :], bank(6, P).rearrange("p (t e) -> p t e", e=E), ALU.add))
                after(dve, dve.tensor_tensor(TOT[:, 1, :, :], TOT[:, 1, :, :], OH8[:, :, :], ALU.mult))
                after(dve, dve.tensor_reduce(GATE[:, 1, :], TOT[:, 1, :, :], AX.X, ALU.add))
                after(dve, dve.tensor_scalar(GATE[:, 1, :], GATE[:, 1, :], float(CAP), None, ALU.is_le))
                after(dve, dve.tensor_tensor(GATE[:, 0, :], GATE[:, 0, :], GATE[:, 1, :], ALU.mult))
                for t in range(TILES):
                    ins = dve.tensor_scalar(DIAG[:, t, :], wt("ident"), GATE[:, 0, t:t + 1], None, ALU.mult)
                ins.then_inc(scale_ready, 1)
                for n in range(1, NU, 2):
                    e, m, bp, bh = UNITS[n]
                    dve.wait_ge(hid_ps, n + 1)
                    if n >= 4:
                        dve.wait_ge(hid_used, n - 3)
                    dve.tensor_scalar(HID[:, n % 4, :], bank(2 + n % 4), wt("b1_3", 2 * e + m, 1), 0.0, ALU.add, ALU.max).then_inc(hid_in_v, 1)
                dve.memset(FIN[:, 2, :], 1.0e4)
                dve.memset(FIN[:, 3, :], -1.0e4)
                for bp in range(2):
                    c = slice(bp * HC, (bp + 1) * HC)
                    dve.memset(FIN[:, 1, :], 0.0)
                    dve.wait_ge(f_ps, bp + 1)
                    dve.wait_ge(sc_in, bp + 1)
                    after(dve, dve.tensor_tensor(FIN[:, 0, :], bank(bp), SCB[:, c], ALU.mult))
                    after(dve, dve.tensor_tensor(MASK[:, :], FIN[:, 0, :], FIN[:, 0, :], ALU.is_equal))
                    after(dve, dve.copy_predicated(FIN[:, 1, :], MASK[:, :], FIN[:, 0, :]))
                    after(dve, dve.tensor_scalar(MASK[:, :], FIN[:, 1, :], 3.4028234e38, None, ALU.is_gt))
                    after(dve, dve.copy_predicated(FIN[:, 1, :], MASK[:, :], FIN[:, 2, :]))
                    after(dve, dve.tensor_scalar(MASK[:, :], FIN[:, 1, :], -3.4028234e38, None, ALU.is_lt))
                    after(dve, dve.copy_predicated(FIN[:, 1, :], MASK[:, :], FIN[:, 3, :]))
                    after(dve, dve.tensor_tensor(X[:, c], X[:, c], FIN[:, 1, :], ALU.add))

        with nc.Block() as block:
            @block.sync
            def _(sp):
                ov = out_dram.rearrange("(g b) c p -> g c b p", g=2)
                for g in range(2):
                    sp.dma_start(ov[g], X[C * g:C * g + C, :].rearrange("c (b p) -> c b p", b=NB)).then_inc(stored, 16)
                sp.wait_ge(stored, 32)


def pack_weights(v):
    packs = [np.zeros((P, w), np.float32) for w in WIDTH]

    def put(name, a, p0=0, at=0):
        a = np.asarray(a)
        a = a.reshape(a.shape[0], -1)
        s, c0, cols = AT[name]
        assert at + a.shape[1] <= cols, name
        packs[s][p0:p0 + a.shape[0], c0 + at:c0 + at + a.shape[1]] = a

    def twice(name, a, at=0):
        a = np.asarray(a)
        put(name, a.reshape(a.shape[0], -1), 0, at)
        put(name, a.reshape(a.shape[0], -1), 64, at)

    def diag2(name, a, at=0, width=None):
        width = width or a.shape[1]
        put(name, a, 0, at)
        put(name, a, 64 if a.shape[0] == 64 else a.shape[0], at + width)

    def rows(name, a, at=0):
        put(name, np.broadcast_to(np.asarray(a).reshape(1, -1), (P, np.asarray(a).size)), 0, at)

    f = np.float32
    eye = np.eye(P, dtype=f)
    blocks = np.kron(np.eye(2, dtype=f), np.ones((C, C), f))
    put("ident", eye)
    put("center", eye - blocks / C)
    put("mean32", np.kron(np.eye(2, dtype=f), np.full((C, 16), 1.0 / C, f)))
    for q in range(4):
        for bh in range(2):
            put("spread", np.ones((1, C), f), 32 * q + 16 * bh, q * P + C * bh)
    put("epsc", np.full((P, 1), 1e-6, f))
    put("epst", np.full((P, 1), 1e-5, f))
    put("epsa", np.full((P, 1), 1e-15, f))
    put("epsb", np.full((P, 1), 1e-3, f))

    ch = [np.array([g * 24 + j * HD + e for g in range(8) for e in range(HD)]) for j in range(3)]
    qkv_w = v["L0_conv_qkv_w"][:, :, 0, 0]
    for j in range(3):
        diag2("wq3", qkv_w[ch[j]].T, j * P)
        twice("bq3", v["L0_conv_qkv_b"][ch[j]][:, None], j)
        for k in ("3", "5"):
            w = v[f"L0_conv_dw{k}_w"][ch[j], 0]
            twice("dw" + k, w.reshape(C, -1), j * w.shape[1] * w.shape[2])
            twice("db" + k, v[f"L0_conv_dw{k}_b"][ch[j]][:, None], j)
    for i in range(2):
        diag2("wkv", qkv_w[ch[1 + i]].T, i * P)
    for s, (w, b) in enumerate((("qkv_w", "qkv_b"), ("pw3_w", "pw3_b"), ("pw5_w", "pw5_b"))):
        b = v["L0_conv_" + b]
        rows("bkv", np.concatenate([b[ch[1]], b[ch[1]], b[ch[2]], b[ch[2]]]), s * 2 * P)
        twice("bqq", b[ch[0]][:, None], s)
        if s == 0:
            continue
        pw = v["L0_conv_" + w][:, :, 0, 0]
        for j in range(3):
            m = np.zeros((3, C, C), f)
            for o in range(3):
                for g in range(8):
                    m[o, g * HD:(g + 1) * HD, g * HD:(g + 1) * HD] = pw[g * 24 + o * HD:g * 24 + (o + 1) * HD,
                                                                        j * HD:(j + 1) * HD].T
            diag2("pwq", m[0], ((s - 1) * 3 + j) * P)
            for i in range(2):
                diag2("pwkv", m[1 + i], (2 * ((s - 1) * 3 + j) + i) * P)
    for s in range(SCALES):
        diag2("proj", v["L0_conv_proj_w"][:, s * C:(s + 1) * C, 0, 0].T, s * P)
    twice("bproj", v["L0_conv_proj_b"][:, None])
    heads = np.kron(np.eye(2 * E, dtype=f), np.ones((HD, 1), f))
    put("headmask", np.concatenate([heads, heads], 1))
    for bl in range(NB):
        put("headspread", heads.T, 32 * bl, bl * P)
    put("vkmask", np.kron(np.eye(16, dtype=f), np.ones((HD, HD), f)))

    diag2("gate0", v["L0_ffn_gate_w"])
    rows("gb0", v["L0_ffn_gate_b"])
    rows("before", np.tril(np.ones((E, E), f), -1))
    for e in range(E):
        diag2("w1_0", v["L0_ffn_W1"][e], e * 2 * FH0)
    put("b1_0", v["L0_ffn_b1"].T)
    for e in range(E):
        put("w2_0", v["L0_ffn_W2"][e], 0, e * C)
    put("b2_0", v["L0_ffn_b2"])
    put("sel24", np.tile(np.eye(E, dtype=f), (3, 1)))

    c1, c2 = v["L1_conv_w1"], v["L1_conv_w2"]
    order = np.array([(s * 2 + xy) for xy in range(2) for s in range(SAMPLES)])
    for m in range(9):
        diag2("c1w", c1[:, :, m // 3, m % 3].T, m * P)
        diag2("c2w", c2[order][:, :, m // 3, m % 3].T, m * 144)
    twice("c1b", v["L1_conv_b1"][:, None])
    rows("c2b", v["L1_conv_b2"][order])
    pix = np.arange(P)
    tap = np.arange(SAMPLES) % 9
    for h in range(2):
        py = (pix // W + h * H // 2)[:, None] + (tap // 3 - 1)[None]
        px = (pix % W)[:, None] + (tap % 3 - 1)[None]
        put("pos", np.concatenate([py, px], 1).astype(f), 0, h * 72)
        put("qidx", (pix + h * P)[:, None].astype(f), 0, h)
    wd = v["L1_conv_wd"].reshape(C, 4, CG, 9).transpose(1, 3, 2, 0).reshape(SAMPLES * CG, C)
    for n in range(5):
        put("wd", wd[n * P:(n + 1) * P], 0, n * C)

    diag2("wr1", v["L1_ffn_wr"])
    rows("br1", v["L1_ffn_br"])
    for h in range(2):
        put("before1", (np.arange(PIX)[None] < (pix + h * P)[:, None]).astype(f), 0, h * PIX)
    diag2("w1_1", v["L1_ffn_w1"])
    put("b1_1", v["L1_ffn_b1"].reshape(2, P).T)
    for m in range(2):
        put("w2_1", v["L1_ffn_w2"][m * P:(m + 1) * P], 0, m * C)
    twice("b2_1", v["L1_ffn_b2"][:, None])
    put("ones", np.ones((P, P), f))

    for k in range(4):
        diag2("ssw", v["L2_conv_weight"][k * C:(k + 1) * C].T, k * P)
        twice("ssb", v["L2_conv_bias"][k * C:(k + 1) * C, None], k)

    twice("wr2", v["L2_ffn_Wr"])
    rows("br2", v["L2_ffn_br"])
    for e in range(E):
        diag2("w1_2", v["L2_ffn_W1"][e], e * P)
        diag2("w2_2", v["L2_ffn_W2"][e], e * P)
        diag2("wo_2", v["L2_ffn_Wo"][e], e * P)
    for n in (1, 2):
        for i, name in enumerate(("b", "g", "be", "m", "v")):
            twice(f"bn{n}", v[f"L2_ffn_{name}{n}"].T, i * E)
    put("bo2", np.concatenate([v["L2_ffn_bo"], v["L2_ffn_bo"]], 1))

    twice("dwi", v["L3_conv_w_in"].reshape(C, 9))
    twice("dbi", v["L3_conv_b_in"][:, None])
    diag2("red", v["L3_conv_w_red"].T, 0)
    put("bred", v["L3_conv_b_red"][:, None], 0)
    put("bred", v["L3_conv_b_red"][:, None], 16)
    for k in range(9):
        a = np.broadcast_to(v["L3_conv_w_span"][k][:, None], (16, C))
        put("span", a, 0, k * P)
        put("span", a, 16, k * P + C)
        put("span", np.broadcast_to(v["L3_conv_b_span"][k:k + 1, None], (1, P)), 32, k * P)
    twice("dwo", v["L3_conv_w_out"].reshape(C, 9))
    twice("dbo", v["L3_conv_b_out"][:, None])

    diag2("gate3", v["L3_ffn_gate_w"])
    rows("gb3", v["L3_ffn_gate_b"])
    put("tri", np.triu(np.ones((P, P), f)))
    put("w1_3", v["L3_ffn_w1"].transpose(1, 0, 2))
    for e in range(E):
        put("w1_3", np.full((1, FH3), -BIG, f), C + e, e * FH3)
        for m in range(2):
            put("b1_3", v["L3_ffn_b1"][e, m * P:(m + 1) * P, None], 0, 2 * e + m)
            put("w2_3", v["L3_ffn_w2"][e, m * P:(m + 1) * P], 0, (2 * e + m) * C)
    put("b2_3", v["L3_ffn_b2"])
    return packs


def kernel(**inputs):
    import concourse.bacc as bacc
    from concourse.bass_utils import run_bass_kernel_spmd

    v = {k: np.asarray(a) for k, a in inputs.items()}
    nc = bacc.Bacc("TRN2", target_bir_lowering=False, num_devices=1)
    arrays = {"x_dram": np.ascontiguousarray(v["x"]).reshape(B, C, PIX)}
    x_dram = nc.dram_tensor("x_dram", (B, C, PIX), F32, kind="ExternalInput").ap()
    packs = []
    for n, a in enumerate(pack_weights(v)):
        arrays[f"pack{n}_dram"] = a
        packs.append(nc.dram_tensor(f"pack{n}_dram", a.shape, F32, kind="ExternalInput").ap())
    out = nc.dram_tensor("out_dram", (B, C, PIX), F32, kind="ExternalOutput").ap()
    build(nc, x_dram, packs, out)
    r = run_bass_kernel_spmd(nc, [arrays], core_ids=[0])
    return r.results[0]["out_dram"].reshape(B, C, H, W)
```

```python
from contextlib import ExitStack

import concourse.bass as bass
import numpy as np
from concourse import mybir

ALU = mybir.AluOpType
ACT = mybir.ActivationFunctionType
F32 = mybir.dt.float32
BF16 = mybir.dt.bfloat16
FP16 = mybir.dt.float16
I32 = mybir.dt.int32
AX = mybir.AxisListType

P = 128
B, C, H, W = 8, 64, 16, 16
NB = B // 2
PIX = H * W
COLS = NB * PIX
HC = COLS // 2
TILES = B * PIX // P
PITCH, PW = H + 2, W + 4
PROWS = 2 + NB * PITCH
AROWS = (NB - 1) * PITCH + H
E = 8
HD = 8
SCALES = 3
SAMPLES = 36
CG = 16
FH0, FH1, FH3 = 128, 256, 256
CAP = -(-5 * B * PIX // (4 * E))
TOPK = PIX // 2 - 1
GSCALE = 4096.0
BIG = 1.0e30

SECTIONS = [
    [("center", P), ("mean32", 32), ("spread", 4 * P), ("ident", P), ("ones", P), ("rev", E), ("epsc", 1), ("epst", 1), ("epsa", 1), ("epsb", 1)],
    [("wq3", 3 * P), ("bq3", 3), ("wkv", 2 * P), ("bkv", SCALES * 2 * P), ("dw5", 75), ("db5", 3), ("dw3", 27), ("db3", 3),
     ("pwq", 6 * P), ("bqq", 3), ("pwkv", 12 * P), ("proj", 3 * P), ("bproj", 1), ("vkmask", P), ("headmask", 32), ("headspread", 4 * P)],
    [("gate0", 2 * E), ("gb0", E), ("w1_0", E * 2 * FH0), ("b1_0", E), ("w2_0", E * C), ("b2_0", C),
     ("sel24", E)],
    [("c1w", 9 * P), ("c1b", 1), ("c2w", 9 * 144), ("c2b", 72), ("pos", 2 * 72),
     ("qidx", 2), ("wd", 5 * C)],
    [("wr1", 2), ("br1", 1), ("before1", 2 * PIX), ("w1_1", 2 * FH1), ("b1_1", 2), ("w2_1", 2 * C), ("b2_1", 1)],
    [("ssw", 4 * P), ("ssb", 4)],
    [("wr2", E), ("br2", E), ("w1_2", E * P), ("w2_2", E * P), ("wo_2", E * P), ("bn1", 5 * E),
     ("bn2", 5 * E), ("bo2", P)],
    [("dwi", 9), ("dbi", 1), ("red", 32), ("bred", 1), ("span", 9 * P), ("dwo", 9), ("dbo", 1)],
    [("gate3", 2 * E), ("gb3", E), ("tri", P), ("w1_3", E * FH3), ("b1_3", E * 2), ("w2_3", E * 2 * C), ("b2_3", C)],
]
AT = {}
WIDTH = []
for _n, _s in enumerate(SECTIONS):
    _at = 0
    for _name, _cols in _s:
        AT[_name] = (_n, _at, _cols)
        _at += _cols
    WIDTH.append(_at)


def build(nc, x_dram, packs, idx_dram, out_dram):
    with ExitStack() as ctx:
        def sb(name, shape, dt=F32, where=None):
            return (where or ctx).enter_context(nc.sbuf_tensor(name, shape, dt))

        def sem(name):
            return ctx.enter_context(nc.semaphore(name))

        X = sb("X", [P, COLS])
        Y = sb("Y", [P, COLS])
        SQ = sb("SQ", [P, COLS])
        SD = sb("SD", [P, COLS])
        wconst = sb("wconst", [P, WIDTH[0]])
        wbuf = [sb(f"wbuf{i}", [P, max(w for n, w in enumerate(WIDTH) if n and n % 2 == i)]) for i in range(2)]
        wsb = [wconst if n == 0 else wbuf[n % 2] for n in range(len(SECTIONS))]
        PS = ctx.enter_context(nc.psum_tensor("PS", [P, 8 * 512], F32))

        def bank(n, cols=512):
            return PS[:, n * 512:n * 512 + cols]

        def wt(name, a=0, n=None, p0=0, p1=P):
            s, at, cols = AT[name]
            n = cols - a if n is None else n
            return wsb[s][p0:p1, at + a:at + a + n]

        x_in = sem("x_in")
        w_in = [sem(f"w_in{n}") for n in range(len(SECTIONS))]
        stored = sem("stored")
        ln_centered, ln_squared, ln_var, ln_sd, ln_rstd, ln_spread, ln_placed, ln_done = (sem(n) for n in (
            "ln_centered", "ln_squared", "ln_var", "ln_sd", "ln_rstd", "ln_spread", "ln_placed", "ln_done"))
        dve_step = sem("dve_step")
        act_step = sem("act_step")
        pool_step = sem("pool_step")
        steps = {"dve": 0, "act": 0, "pool": 0}

        def load_weights(sp, n):
            sp.dma_start(wsb[n][:, 0:WIDTH[n]], packs[n]).then_inc(w_in[n], 16)

        def after(eng, ins):
            steps["dve"] += 1
            ins.then_inc(dve_step, 1)
            eng.wait_ge(dve_step, steps["dve"])

        def after_act(eng, ins):
            steps["act"] += 1
            ins.then_inc(act_step, 1)
            eng.wait_ge(act_step, steps["act"])

        def after_pool(eng, ins):
            steps["pool"] += 1
            ins.then_inc(pool_step, 1)
            eng.wait_ge(pool_step, steps["pool"])

        WARM = sb("WARM", [P, 32])
        warmed = [0]

        def warm(act, func):
            k = warmed[0]
            warmed[0] += 1
            act.activation(WARM[:, k:k + 1], wt("epsc"), func)

        def ln_pe(pe, n):
            for h in range(2):
                pe.matmul(bank(h), wt("center"), X[:, h * HC:(h + 1) * HC], start=True, stop=True).then_inc(ln_centered, 1)
            for h in range(2):
                pe.wait_ge(ln_squared, 2 * n + h + 1)
                for q in range(4):
                    mm = pe.matmul(bank(2 + h, P)[32 * q:32 * q + 32, :], wt("mean32"), SQ[:, h * HC + q * P:h * HC + (q + 1) * P],
                                   start=True, stop=True, tile_position=(0, 32 * q))
                mm.then_inc(ln_var, 1)
            for h in range(2):
                pe.wait_ge(ln_rstd, 2 * n + h + 1)
                for q in range(4):
                    mm = pe.matmul(bank(2 + h)[:, q * P:(q + 1) * P], wt("spread", q * P, P), SD[:, h * P:(h + 1) * P],
                                   start=True, stop=True)
                mm.then_inc(ln_spread, 1)

        def ln_act(act, n, eps):
            warm(act, ACT.Sqrt)
            for h in range(2):
                act.wait_ge(ln_centered, 2 * n + h + 1)
                act.activation(SQ[:, h * HC:(h + 1) * HC], bank(h), ACT.Square).then_inc(ln_squared, 1)
            for h in range(2):
                act.wait_ge(ln_var, 2 * n + h + 1)
                act.activation(SD[:, h * P:(h + 1) * P], bank(2 + h, P), ACT.Sqrt, bias=wt(eps)).then_inc(ln_sd, 1)

        def ln_dve(dve, n, out_of):
            for h in range(2):
                o, view = out_of(h)
                dve.wait_ge(ln_squared, 2 * n + h + 1)
                dve.tensor_copy(o, view(bank(h))).then_inc(ln_placed, 1)
            for h in range(2):
                c = slice(h * P, (h + 1) * P)
                dve.wait_ge(ln_sd, 2 * n + h + 1)
                dve.reciprocal(SD[:, c], SD[:, c]).then_inc(ln_rstd, 1)
            for h in range(2):
                o, view = out_of(h)
                dve.wait_ge(ln_placed, 2 * n + h + 1)
                dve.wait_ge(ln_spread, 2 * n + h + 1)
                dve.tensor_tensor(o, o, view(bank(2 + h)), ALU.mult).then_inc(ln_done, 1)

        def flat(h):
            return Y[:, h * HC:(h + 1) * HC], lambda a: a

        def images(a):
            return a.rearrange("p (b r w) -> p b r w", b=2, r=H)

        def pair(pad, h, dy, dx):
            r0 = 2 * h * PITCH + dy
            if r0 + 2 * PITCH <= PROWS:
                v = pad[:, r0:r0 + 2 * PITCH, dx:dx + W].rearrange("p (b r) w -> p b r w", b=2)
                return v[:, :, 0:H, :]
            v = pad[:, r0 - (PITCH - H):r0 + 2 * PITCH - (PITCH - H), dx:dx + W].rearrange("p (b r) w -> p b r w", b=2)
            return v[:, :, PITCH - H:PITCH, :]

        def acc_images(acc, h):
            r0 = 2 * h * PITCH
            if r0 + 2 * PITCH <= AROWS:
                return acc[:, r0:r0 + 2 * PITCH, :].rearrange("p (b r) w -> p b r w", b=2)[:, :, 0:H, :]
            r0 -= PITCH - H
            return acc[:, r0:r0 + 2 * PITCH, :].rearrange("p (b r) w -> p b r w", b=2)[:, :, PITCH - H:PITCH, :]

        def tok(t):
            bh, r = t // (2 * NB), t % (2 * NB)
            return slice(C * bh, C * bh + C), slice(r * P, (r + 1) * P)

        with ExitStack() as sctx, nc.Block() as block:
            QKVP = [sb(f"QKVP{j}", [P, PROWS, PW], F32, sctx) for j in range(3)]
            D5 = [sb(f"D5_{j}", [P, AROWS, W], F32, sctx) for j in range(3)]
            D3 = [sb(f"D3_{j}", [P, COLS], F32, sctx) for j in range(3)]
            QR = [sb(f"QR{s}", [P, COLS], F32, sctx) for s in range(SCALES)]
            ATT = [sb(f"ATT{s}", [P, COLS], F32, sctx) for s in range(SCALES)]
            KV = sb("KV", [P, SCALES, NB, 2, 257], F32, sctx)
            VK = sb("VK", [P, SCALES, NB, P], F32, sctx)
            KSUM = sb("KSUM", [P, SCALES, NB, 32], F32, sctx)
            DG = sb("DG", [P, 27, P], F32, sctx)
            RD = sb("RD", [P, PIX], F32, sctx)
            TAP = [sb(f"TAP{i}", [P, AROWS, W], F32, sctx) for i in range(2)]
            D5B = [sb(f"D5B{i}", [P, AROWS, W], F32, sctx) for i in range(2)]
            padded, diag, ones_set, qkv_in, kv_ps, kv_biased, kv_ready, dw3_ps, d3_ready, d5_ready = (sem(n) for n in (
                "padded", "diag", "ones_set", "qkv_in", "kv_ps", "kv_biased", "kv_ready", "dw3_ps", "d3_ready", "d5_ready"))
            qkv_ps, q_ps, q_ready, vk_ps, vk_ready, den_ps, den_out, den_inv, num_ps, num_out, inv_ps, att_ready, proj_ps = (
                sem(n) for n in ("qkv_ps", "q_ps", "q_ready", "vk_ps", "vk_ready", "den_ps", "den_out", "den_inv", "num_ps",
                                 "num_out", "inv_ps", "att_ready", "proj_ps"))
            tap_ready, tap_used, d5a_ready = sem("tap_ready"), sem("tap_used"), sem("d5a_ready")
            VTAPS = 18
            GTAPS = 25 - VTAPS

            @block.sync
            def _(sp):
                xv = x_dram.rearrange("(g b) c p -> g c b p", g=2)
                for g in range(2):
                    sp.dma_start(X[C * g:C * g + C, :].rearrange("c (b p) -> c b p", b=NB), xv[g]).then_inc(x_in, 16)
                for n in range(3):
                    load_weights(sp, n)

            @block.gpsimd
            def _(pool):
                for j in range(3):
                    pool.memset(QKVP[j][:, :, :], 0.0).then_inc(padded, 1)
                pool.memset(KV[:, :, :, :, 256:257], 1.0).then_inc(ones_set, 1)
                pool.wait_ge(w_in[0], 16)
                pool.wait_ge(w_in[1], 16)
                for m in range(27):
                    pool.tensor_scalar(DG[:, m, :], wt("ident"), wt("dw3", m, 1), None, ALU.mult).then_inc(diag, 1)

                def keys(s):
                    for g in range(NB):
                        pool.wait_ge(kv_biased, 4 * s + g + 1)
                        k = KV[:, s, g, :, 0:P]
                        pool.tensor_scalar(k, k, 0.0, None, ALU.max).then_inc(kv_ready, 1)

                def join(j):
                    pool.wait_ge(d5a_ready, j + 1)
                    pool.tensor_tensor(D5[j][:, :, :], D5[j][:, :, :], D5B[j % 2][:, :, :], ALU.add).then_inc(d5_ready, 1)

                keys(0)
                for j in range(3):
                    for i in range(1, GTAPS):
                        n = j * (GTAPS - 1) + i
                        pool.wait_ge(tap_ready, j * GTAPS + i + 1)
                        pool.tensor_tensor(D5B[j % 2][:, :, :], D5B[j % 2][:, :, :], TAP[n % 2][:, :, :], ALU.add).then_inc(tap_used, 1)
                        pool.wait_ge(tap_used, n)
                    if j >= 1:
                        join(j - 1)
                join(2)
                keys(1)
                keys(2)

            @block.tensor
            def _(pe):
                pe.wait_ge(x_in, 32)
                pe.wait_ge(w_in[0], 16)
                ln_pe(pe, 0)
                pe.wait_ge(w_in[1], 16)
                qbank = [4, 5, 6, 7, 2, 3]
                for j in range(3):
                    for h in range(2):
                        if j == 0 or (j, h) == (2, 0):
                            pe.wait_ge(ln_done, 2 if j else h + 1)
                        pe.matmul(bank(qbank[2 * j + h]), wt("wq3", j * P, P), Y[:, h * HC:(h + 1) * HC],
                                  start=True, stop=True).then_inc(qkv_ps, 1)

                def kv_group(s, g):
                    n = 4 * s + g
                    if n >= 2:
                        pe.wait_ge(kv_biased, n - 1)
                    for i in range(2):
                        r = 2 * g + i
                        cc = slice(r * P, (r + 1) * P)
                        o = bank(n % 2)[:, i * 2 * P:(i + 1) * 2 * P]
                        if s == 0:
                            mm = pe.matmul(o, Y[:, cc], wt("wkv"), start=True, stop=True)
                        else:
                            for j in range(3):
                                r0 = g * PITCH + i * (H // 2)
                                src = D3[j][:, cc] if s == 1 else D5[j][:, r0:r0 + H // 2, :].rearrange("p r w -> p (r w)")
                                mm = pe.matmul(o, src, wt("pwkv", ((s - 1) * 3 + j) * 2 * P, 2 * P),
                                               start=(j == 0), stop=(j == 2))
                    mm.then_inc(kv_ps, 1)

                def vk(s):
                    pe.wait_ge(kv_ready, 4 * s + 4)
                    if s == 0:
                        pe.wait_ge(ones_set, 1)
                    for bp in range(2):
                        n = 2 * s + bp
                        if n >= 2:
                            pe.wait_ge(vk_ready, n - 1)
                            if bp == 1:
                                pe.wait_ge(den_out, s)
                        for i in range(2):
                            for half in range(2):
                                kv = KV[:, s, 2 * bp + i, half, :]
                                mm = pe.matmul(bank(6 + n % 2)[:, i * 129:(i + 1) * 129], kv[:, 0:P], kv[:, P:257],
                                               start=(half == 0), stop=(half == 1))
                        mm.then_inc(vk_ps, 1)

                def den(s):
                    pe.wait_ge(vk_ready, 2 * s + 2)
                    pe.wait_ge(q_ready, 2 * s + 2)
                    for bl in range(NB):
                        mm = pe.matmul(bank(7, PIX)[32 * bl:32 * bl + 32, :], KSUM[:, s, bl, :], QR[s][:, bl * PIX:(bl + 1) * PIX],
                                       start=True, stop=True, tile_position=(0, 32 * bl))
                    mm.then_inc(den_ps, 1)

                def attend(s):
                    for bp in range(2):
                        n = 2 * s + bp
                        if n >= 1:
                            pe.wait_ge(num_out, n)
                        for i in range(2):
                            bl = 2 * bp + i
                            mm = pe.matmul(bank(2)[:, i * PIX:(i + 1) * PIX], VK[:, s, bl, :],
                                           QR[s][:, bl * PIX:(bl + 1) * PIX], start=True, stop=True)
                        mm.then_inc(num_ps, 1)
                        pe.wait_ge(den_inv, s + 1)
                        if n >= 1:
                            pe.wait_ge(att_ready, n)
                        for i in range(2):
                            bl = 2 * bp + i
                            mm = pe.matmul(bank(3)[:, i * PIX:(i + 1) * PIX], wt("headspread", bl * P, P), RD[:, :],
                                           start=True, stop=True)
                        mm.then_inc(inv_ps, 1)

                def queries(s):
                    for h in range(2):
                        if s == 2:
                            pe.wait_ge(q_ready, 3 + h)
                        for j in range(3):
                            src = D3[j][:, h * HC:(h + 1) * HC] if s == 1 else acc_images(D5[j], h)
                            mm = pe.matmul(bank(4 + h), wt("pwq", ((s - 1) * 3 + j) * P, P), src,
                                           start=(j == 0), stop=(j == 2))
                        mm.then_inc(q_ps, 1)

                for g in range(4):
                    kv_group(0, g)
                pe.wait_ge(qkv_in, 6)
                pe.wait_ge(diag, 27)
                for j in range(3):
                    for h in range(2):
                        for m in range(9):
                            mm = pe.matmul(bank(qbank[2 * j + h]), DG[:, j * 9 + m, :],
                                           pair(QKVP[j], h, 1 + m // 3, 1 + m % 3), start=(m == 0), stop=(m == 8))
                        mm.then_inc(dw3_ps, 1)
                pe.wait_ge(d3_ready, 6)
                vk(0)
                queries(1)
                for g in range(4):
                    kv_group(1, g)
                den(0)
                pe.wait_ge(d5_ready, 3)
                queries(2)
                for g in range(4):
                    kv_group(2, g)
                attend(0)
                vk(1)
                den(1)
                vk(2)
                attend(1)
                den(2)
                attend(2)
                pe.wait_ge(att_ready, 2 * SCALES)
                for h in range(2):
                    for s in range(SCALES):
                        mm = pe.matmul(bank(h), wt("proj", s * P, P), ATT[s][:, h * HC:(h + 1) * HC],
                                       start=(s == 0), stop=(s == SCALES - 1))
                    mm.then_inc(proj_ps, 1)

            @block.scalar
            def _(act):
                qbank = [4, 5, 6, 7, 2, 3]
                act.wait_ge(w_in[0], 16)
                ln_act(act, 0, "epsc")
                act.wait_ge(w_in[1], 16)
                act.wait_ge(padded, 3)
                for j in range(3):
                    for h in range(2):
                        act.wait_ge(qkv_ps, 2 * j + h + 1)
                        src = bank(qbank[2 * j + h])
                        if j == 0:
                            act.activation(QR[0][:, h * HC:(h + 1) * HC], src, ACT.Relu, bias=wt("bqq", 0, 1)).then_inc(q_ready, 1)
                        act.activation(pair(QKVP[j], h, 2, 2), images(src), ACT.Identity, bias=wt("bq3", j, 1)).then_inc(qkv_in, 1)

                for j in range(3):
                    act.wait_ge(qkv_in, 2 * j + 2)
                    for i in range(GTAPS):
                        m = VTAPS + i
                        src = QKVP[j][:, m // 5:m // 5 + AROWS, m % 5:m % 5 + W]
                        if i == 0:
                            if j >= 2:
                                act.wait_ge(d5_ready, j - 1)
                            act.activation(D5B[j % 2][:, :, :], src, ACT.Identity, bias=wt("db5", j, 1), scale=wt("dw5", j * 25 + m, 1)).then_inc(tap_ready, 1)
                            continue
                        n = j * (GTAPS - 1) + i
                        if n > 2:
                            act.wait_ge(tap_used, n - 2)
                        act.activation(TAP[n % 2][:, :, :], src, ACT.Copy, scale=wt("dw5", j * 25 + m, 1)).then_inc(tap_ready, 1)
                    for h in range(2):
                        act.wait_ge(dw3_ps, 2 * j + h + 1)
                        act.activation(D3[j][:, h * HC:(h + 1) * HC], bank(qbank[2 * j + h]), ACT.Identity,
                                       bias=wt("db3", j, 1)).then_inc(d3_ready, 1)

                def queries(s):
                    for h in range(2):
                        act.wait_ge(q_ps, 2 * (s - 1) + h + 1)
                        act.activation(QR[s][:, h * HC:(h + 1) * HC], bank(4 + h), ACT.Relu, bias=wt("bqq", s, 1)).then_inc(q_ready, 1)

                def den(s):
                    act.wait_ge(den_ps, s + 1)
                    if s >= 1:
                        act.wait_ge(inv_ps, 2 * s)
                    act.activation(RD[:, :], bank(7, PIX), ACT.Identity, bias=wt("epsa")).then_inc(den_out, 1)

                def numerators(s):
                    for bp in range(2):
                        n = 2 * s + bp
                        act.wait_ge(num_ps, n + 1)
                        act.activation(ATT[s][:, bp * HC:(bp + 1) * HC], bank(2), ACT.Copy).then_inc(num_out, 1)

                queries(1)
                den(0)
                queries(2)
                numerators(0)
                den(1)
                numerators(1)
                den(2)
                numerators(2)

            @block.vector
            def _(dve):
                dve.wait_ge(w_in[0], 16)
                ln_dve(dve, 0, flat)
                dve.wait_ge(w_in[1], 16)

                def kv_bias(s):
                    for g in range(NB):
                        n = 4 * s + g
                        dve.wait_ge(kv_ps, n + 1)
                        bias = wt("bkv", s * 2 * P, 2 * P).rearrange("p (o c) -> p o c", o=1).broadcast_to([P, 2, 2 * P])
                        dve.tensor_tensor(KV[:, s, g, :, 0:2 * P], bank(n % 2).rearrange("p (t c) -> p t c", t=2), bias,
                                          ALU.add).then_inc(kv_biased, 1)

                def mask_vk(s):
                    for bp in range(2):
                        n = 2 * s + bp
                        dve.wait_ge(vk_ps, n + 1)
                        for i in range(2):
                            ps = bank(6 + n % 2)[:, i * 129:(i + 1) * 129]
                            dve.tensor_tensor(VK[:, s, 2 * bp + i, :], ps[:, 0:P], wt("vkmask"), ALU.mult)
                            ins = dve.tensor_scalar(KSUM[:, s, 2 * bp + i, :], wt("headmask"), ps[:, P:P + 1], None, ALU.mult)
                        ins.then_inc(vk_ready, 1)

                def invert(s):
                    dve.wait_ge(den_out, s + 1)
                    dve.reciprocal(RD[:, :], RD[:, :]).then_inc(den_inv, 1)

                def divide(s):
                    for bp in range(2):
                        n = 2 * s + bp
                        a = ATT[s][:, bp * HC:(bp + 1) * HC]
                        dve.wait_ge(num_out, n + 1)
                        dve.wait_ge(inv_ps, n + 1)
                        dve.tensor_tensor(a, a, bank(3), ALU.mult).then_inc(att_ready, 1)

                def depthwise5(j):
                    for m in range(VTAPS):
                        src = QKVP[j][:, m // 5:m // 5 + AROWS, m % 5:m % 5 + W]
                        w = wt("dw5", j * 25 + m, 1)
                        if m == 0:
                            after(dve, dve.tensor_scalar(D5[j][:, :, :], src, w, None, ALU.mult))
                        else:
                            ins = dve.scalar_tensor_tensor(out=D5[j][:, :, :], in0=src, scalar=w, in1=D5[j][:, :, :],
                                                           op0=ALU.mult, op1=ALU.add)
                            if m < VTAPS - 1:
                                after(dve, ins)
                            else:
                                ins.then_inc(d5a_ready, 1)

                kv_bias(0)
                dve.wait_ge(qkv_in, 6)
                for j in range(3):
                    depthwise5(j)
                mask_vk(0)
                kv_bias(1)
                invert(0)
                kv_bias(2)
                divide(0)
                mask_vk(1)
                invert(1)
                mask_vk(2)
                divide(1)
                invert(2)
                divide(2)
                for h in range(2):
                    c = slice(h * HC, (h + 1) * HC)
                    dve.wait_ge(proj_ps, h + 1)
                    dve.scalar_tensor_tensor(out=X[:, c], in0=bank(h), scalar=wt("bproj"), in1=X[:, c],
                                             op0=ALU.add, op1=ALU.add)

        def softmax_dve(dve, LG, RED, n, exps, k, summed):
            mx = RED[:, 0:n].rearrange("p (t o) -> p t o", o=1)
            after(dve, dve.tensor_reduce(RED[:, 0:n], LG[:, :, :], AX.X, ALU.max))
            dve.tensor_tensor(LG[:, :, :], LG[:, :, :], mx.broadcast_to([P, n, E]), ALU.subtract).then_inc(exps, 1)
            dve.wait_ge(summed, k)
            after(dve, dve.tensor_reduce(RED[:, 0:n], LG[:, :, :], AX.X, ALU.add))
            after(dve, dve.reciprocal(RED[:, 0:n], RED[:, 0:n]))
            after(dve, dve.tensor_tensor(LG[:, :, :], LG[:, :, :], mx.broadcast_to([P, n, E]), ALU.mult))

        def first_max_dve(dve, V, KEY, RED, OUT):
            mx = RED[:, 0:TILES].rearrange("p (t o) -> p t o", o=1).broadcast_to([P, TILES, E])
            rev = wt("rev").rearrange("p (o e) -> p o e", o=1).broadcast_to([P, TILES, E])
            after(dve, dve.tensor_reduce(RED[:, 0:TILES], V[:, :, :], AX.X, ALU.max))
            after(dve, dve.tensor_tensor(KEY[:, :, :], V[:, :, :], mx, ALU.is_equal))
            after(dve, dve.tensor_tensor(KEY[:, :, :], KEY[:, :, :], rev, ALU.mult))
            after(dve, dve.tensor_reduce(RED[:, 0:TILES], KEY[:, :, :], AX.X, ALU.max))
            after(dve, dve.tensor_tensor(OUT[:, :, :], KEY[:, :, :], mx, ALU.is_equal))

        with ExitStack() as sctx, nc.Block() as block:
            LG = sb("LG", [P, TILES, E], F32, sctx)
            RED = sb("RED", [P, TILES], F32, sctx)
            KEY, FIRST, REST, SECOND, RANK = (sb(n, [P, TILES, E], F32, sctx) for n in ("KEY", "FIRST", "REST", "SECOND", "RANK"))
            CW3 = sb("CW3", [P, TILES, 3, E], BF16, sctx)
            CWT = sb("CWT", [P, TILES * P], F32, sctx)
            CWT3 = sb("CWT3", [P, TILES * P], BF16, sctx)
            SELB = sb("SELB", [P, E * P], BF16, sctx)
            IDB = sb("IDB", [P, P], BF16, sctx)
            AHEAD, HBUF = 6, 6
            HID = sb("HID", [P, HBUF, HC], F32, sctx)
            HS = sb("HS", [P, 4, HC], F32, sctx)
            g_ps, g_exp, g_sum, cw_ready, cwt_ps, cwt_in, hid_ps, hid_in, bc_ps, hs_ready, hs_used, f0_ps, cast0, cwt3_ps = (
                sem(n) for n in ("g_ps", "g_exp", "g_sum", "cw_ready", "cwt_ps", "cwt_in", "hid_ps", "hid_in",
                                 "bc_ps", "hs_ready", "hs_used", "f0_ps", "cast0", "cwt3_ps"))
            CH = 4
            zeroed = sem("zeroed")

            @block.sync
            def _(sp):
                load_weights(sp, 3)

            @block.gpsimd
            def _(pool):
                pool.memset(CWT[:, :], 0.0).then_inc(zeroed, 1)
                pool.memset(CWT3[:, :], 0.0).then_inc(zeroed, 1)

            @block.tensor
            def _(pe):
                def up(n):
                    e, bp, bh = n // CH, (n // 2) % 2, n % 2
                    if n >= 3:
                        pe.wait_ge(hid_in, n - 2)
                    if n == 0:
                        pe.wait_ge(ln_done, 4)
                    pe.matmul(bank(5 + n % 3), wt("w1_0", (2 * e + bh) * FH0, FH0), Y[:, bp * HC:(bp + 1) * HC],
                              start=True, stop=True).then_inc(hid_ps, 1)

                def bc(n):
                    e, bp, bh = n // CH, (n // 2) % 2, n % 2
                    if n >= 3:
                        pe.wait_ge(hs_ready, n - 2)
                    pe.matmul(bank(2 + n % 3), SELB[:, e * P:(e + 1) * P], CWT3[:, (2 * bh + bp) * HC:(2 * bh + bp + 1) * HC],
                              start=True, stop=True).then_inc(bc_ps, 1)

                def down(n):
                    e, bp = n // CH, (n // 2) % 2
                    for bh in range(2):
                        pe.wait_ge(hs_ready, n + bh + 1)
                        pe.matmul(bank(bp)[C * bh:C * bh + C, :], wt("w2_0", e * C, C), HS[:, (n + bh) % 4, :],
                                  start=(e == 0), stop=False).then_inc(hs_used, 1)

                ln_pe(pe, 1)
                pe.wait_ge(w_in[2], 16)
                for r in range(TILES // 2):
                    pe.wait_ge(ln_done, 3 + r // NB)
                    mm = pe.matmul(bank(4)[:, r * 2 * E:(r + 1) * 2 * E], Y[:, r * P:(r + 1) * P], wt("gate0"), start=True, stop=True)
                mm.then_inc(g_ps, 1)
                for n in range(AHEAD):
                    up(n)
                pe.wait_ge(cast0, 2)
                for q in range(2):
                    for i in range(8):
                        t = 8 * q + i
                        o = bank(2 + q).bitcast(BF16)
                        mm = pe.transpose(o[0:3 * E, i * P:(i + 1) * P], CW3[:, t, :, :].rearrange("p s e -> p (s e)"), IDB[:, :])
                    mm.then_inc(cwt3_ps, 1)
                for q in range(4):
                    if q >= 2:
                        pe.wait_ge(cwt_in, q + 1)
                    for i in range(4):
                        t = 4 * q + i
                        mm = pe.transpose(bank(q % 2)[0:E, i * P:(i + 1) * P], LG[:, t, :], wt("ident"))
                    mm.then_inc(cwt_ps, 1)
                pe.wait_ge(cwt_in, 6)

                bc(0)
                bc(1)
                for n in range(0, E * CH, 2):
                    for i in (n + AHEAD, n + AHEAD + 1):
                        if i < E * CH:
                            up(i)
                    for i in (n + 2, n + 3):
                        if i < E * CH:
                            bc(i)
                    down(n)
                for bp in range(2):
                    for bh in range(2):
                        mm = pe.matmul(bank(bp)[C * bh:C * bh + C, :], wt("b2_0"), CWT[:, (2 * bh + bp) * HC:(2 * bh + bp + 1) * HC],
                                       start=False, stop=True)
                    mm.then_inc(f0_ps, 1)

            @block.scalar
            def _(act):
                ln_act(act, 1, "epst")
                act.wait_ge(w_in[2], 16)
                warm(act, ACT.Exp)
                act.wait_ge(g_exp, 1)
                act.activation(LG[:, :, :], LG[:, :, :], ACT.Exp).then_inc(g_sum, 1)
                act.wait_ge(zeroed, 2)

                def hidden(n):
                    act.wait_ge(hid_ps, n + 1)
                    if n >= HBUF:
                        act.wait_ge(hs_ready, n - HBUF + 1)
                    act.activation(HID[:, n % HBUF, :], bank(5 + n % 3), ACT.Gelu, bias=wt("b1_0", n // CH, 1)).then_inc(hid_in, 1)

                for n in range(AHEAD - 2):
                    hidden(n)
                for q in range(2):
                    act.wait_ge(cwt3_ps, q + 1)
                    act.activation(CWT3[0:3 * E, q * 1024:(q + 1) * 1024], bank(2 + q).bitcast(BF16)[0:3 * E, :], ACT.Copy).then_inc(cwt_in, 1)
                for q in range(4):
                    act.wait_ge(cwt_ps, q + 1)
                    act.activation(CWT[0:E, q * HC:(q + 1) * HC], bank(q % 2)[0:E, :], ACT.Copy).then_inc(cwt_in, 1)
                for n in range(AHEAD - 2, E * CH):
                    hidden(n)

            @block.vector
            def _(dve):
                ln_dve(dve, 1, flat)
                dve.wait_ge(w_in[2], 16)
                sel = wt("sel24").rearrange("p (e o) -> p e o", o=1).broadcast_to([P, E, P])
                dve.tensor_copy(SELB[:, :].rearrange("p (e m) -> p e m", e=E), sel).then_inc(cast0, 1)
                dve.tensor_copy(IDB[:, :], wt("ident"))
                dve.wait_ge(g_ps, 1)
                for bh in range(2):
                    gb = wt("gb0").rearrange("p (o e) -> p o e", o=1).broadcast_to([P, 8, E])
                    raw = bank(4, TILES * E).rearrange("p (r h e) -> p h r e", h=2, e=E)
                    ins = dve.tensor_tensor(LG[:, 8 * bh:8 * bh + 8, :], raw[:, bh], gb, ALU.add)
                after(dve, ins)
                softmax_dve(dve, LG, RED, TILES, g_exp, 1, g_sum)
                first_max_dve(dve, LG, KEY, RED, FIRST)
                after(dve, dve.scalar_tensor_tensor(out=REST[:, :, :], in0=FIRST[:, :, :], scalar=-2.0, in1=LG[:, :, :],
                                                    op0=ALU.mult, op1=ALU.add))
                first_max_dve(dve, REST, KEY, RED, SECOND)
                after(dve, dve.tensor_tensor(RANK[:, :, :], FIRST[:, :, :], SECOND[:, :, :], ALU.add))
                dve.tensor_tensor(LG[:, :, :], LG[:, :, :], RANK[:, :, :], ALU.mult).then_inc(cw_ready, 1)
                dve.wait_ge(cw_ready, 1)
                after(dve, dve.tensor_copy(CW3[:, :, 0, :], LG[:, :, :]))
                after(dve, dve.tensor_tensor(RANK[:, :, :], LG[:, :, :], CW3[:, :, 0, :], ALU.subtract))
                after(dve, dve.tensor_copy(CW3[:, :, 1, :], RANK[:, :, :]))
                after(dve, dve.tensor_tensor(RANK[:, :, :], RANK[:, :, :], CW3[:, :, 1, :], ALU.subtract))
                dve.tensor_copy(CW3[:, :, 2, :], RANK[:, :, :]).then_inc(cast0, 1)
                for n in range(E * CH):
                    dve.wait_ge(hid_in, n + 1)
                    dve.wait_ge(bc_ps, n + 1)
                    if n >= 4:
                        dve.wait_ge(hs_used, n - 3)
                    dve.tensor_tensor(HS[:, n % 4, :], bank(2 + n % 3), HID[:, n % HBUF, :], ALU.mult).then_inc(hs_ready, 1)
                for bp in range(2):
                    c = slice(bp * HC, (bp + 1) * HC)
                    dve.wait_ge(f0_ps, bp + 1)
                    dve.tensor_tensor(X[:, c], bank(bp), X[:, c], ALU.add)

        with ExitStack() as sctx, nc.Block() as block:
            VTA = sb("VTA", [P, 5, TILES * P], F32, sctx)
            front = VTA[:, :, :].rearrange("p n c -> p (n c)")
            YP = front[:, 0:PROWS * PW].rearrange("p (r w) -> p r w", w=PW)
            shifted = [front[:, PROWS * (PW + k * W):PROWS * (PW + (k + 1) * W)].rearrange("p (r w) -> p r w", w=W) for k in range(5)]
            XS, HS3 = shifted[0:2], shifted[2:5]
            GX = sb("GX", [P, 2, 2, NB, 4, P], FP16, sctx)
            POS = sb("POS", [P, 4, 72], F32, sctx)
            PY = sb("PY", [P, TILES, 72], F32, sctx)
            BASE = sb("BASE", [P, TILES, 72], F32, sctx)
            U0 = sb("U0", [P, TILES, 72], F32, sctx)
            U1 = sb("U1", [P, TILES, 72], F32, sctx)
            WC = sb("WC", [P, SAMPLES, TILES, 4], F32, sctx)
            IDX = sb("IDX", [P, TILES, SAMPLES], FP16, sctx)
            IDXT = sb("IDXT", [SAMPLES, TILES * P], FP16, sctx)
            IDH = sb("IDH", [P, P], FP16, sctx)
            NBC = 4
            BC = sb("BC", [P, NBC, TILES * P], FP16, sctx)
            OH = sb("OH", [P, 2, 2, 2048], FP16, sctx)
            U = [a[:, :].rearrange("p (t k c) -> p t k c", t=TILES, k=4) for a in (SQ, SD)]
            V1 = sb("V1", [P, TILES, 2, CG], F32, sctx)
            VAL = sb("VAL", [P, 2, TILES, 8, CG], F32, sctx)
            (y_pad, c1_ps, h_in, h_pad, c2_ps, gx_ps, gx_hi, gx_done, idx_ready, cast1, idxt_ps, idxt_in, idx_out,
             oh_ready, oh_used, ga_ps, u_ready, u_used, val_ready, vt_ps, vt_in, dc_ps, xs_ready) = (
                sem("s3_" + n) for n in ("y_pad", "c1_ps", "h_in", "h_pad", "c2_ps", "gx_ps", "gx_hi", "gx_done", "idx_ready",
                "cast1", "idxt_ps", "idxt_in", "idx_out", "oh_ready", "oh_used", "ga_ps", "u_ready", "u_used",
                "val_ready", "vt_ps", "vt_in", "dc_ps", "xs_ready"))

            bc_in = [sem(f"bc_in{i}") for i in range(NBC)]

            @block.sync
            def _(sp):
                load_weights(sp, 4)
                for g in range(NB):
                    sp.wait_ge(idxt_in, g + 1)
                    sp.dma_start(idx_dram[:, g * HC:(g + 1) * HC], IDXT[:, g * HC:(g + 1) * HC]).then_inc(idx_out, 16)
                sp.wait_ge(idx_out, 16 * NB)
                for s in range(SAMPLES):
                    if s >= NBC:
                        sp.wait_ge(oh_ready, s - NBC + 1)
                    sp.dma_start(BC[:, s % NBC, :], idx_dram[s:s + 1, :].broadcast_to([P, TILES * P])).then_inc(bc_in[s % NBC], 16)

            def padded_y(h):
                return pair(YP, h, 2, 2), images

            @block.gpsimd
            def _(pool):
                pool.memset(YP[:, :, :], 0.0).then_inc(y_pad, 1)
                for k in range(3):
                    pool.memset(HS3[k][:, :, :], 0.0).then_inc(h_pad, 1)
                for s in range(SAMPLES):
                    pool.wait_ge(u_ready, s + 1)
                    after_pool(pool, pool.tensor_tensor(V1[:, :, :, :], U[s % 2][:, :, 0:2, :], U[s % 2][:, :, 2:4, :], ALU.add))
                    if s >= 16 and s % 8 == 0:
                        pool.wait_ge(vt_ps, 4 * (s // 8 - 1))
                    pool.tensor_tensor(VAL[:, (s // 8) % 2, :, s % 8, :], V1[:, :, 0, :], V1[:, :, 1, :], ALU.add).then_inc(val_ready, 1)
                    steps["pool"] += 0
                    pool.wait_ge(val_ready, s + 1)

            @block.tensor
            def _(pe):
                ln_pe(pe, 2)
                pe.wait_ge(w_in[3], 16)
                for h in range(2):
                    pe.wait_ge(ln_done, 5 + h)
                    for m in range(9):
                        mm = pe.matmul(bank(4 + h), wt("c1w", m * P, P), pair(YP, h, 1 + m // 3, 1 + m % 3),
                                       start=(m == 0), stop=(m == 8))
                    mm.then_inc(c1_ps, 1)
                pe.wait_ge(xs_ready, 2)
                for n in range(2 * NB):
                    bl, qh = n // 2, n % 2
                    if n >= 4:
                        pe.wait_ge(gx_done, n - 3)
                    for k in range(4):
                        r0 = bl * PITCH + 2 + qh * (H // 2) + k // 2
                        src = XS[k % 2][:, r0:r0 + H // 2, :].rearrange("p r w -> p (r w)")
                        mm = pe.transpose(bank(n % 4)[:, k * P:(k + 1) * P], src, wt("ident"))
                    mm.then_inc(gx_ps, 1)
                pe.wait_ge(h_in, 6)
                for g in range(NB):
                    for i in range(2):
                        for m in range(9):
                            r0 = g * PITCH + i * (H // 2) + 1 + m // 3
                            src = HS3[m % 3][:, r0:r0 + H // 2, :].rearrange("p r w -> p (r w)")
                            mm = pe.matmul(bank(4 + g)[:, i * 144:(i + 1) * 144], src, wt("c2w", m * 144, 144),
                                           start=(m == 0), stop=(m == 8))
                    mm.then_inc(c2_ps, 1)
                for g in range(NB):
                    pe.wait_ge(idx_ready, g + 1)
                    for i in range(4):
                        mm = pe.transpose(bank(g).bitcast(FP16)[0:SAMPLES, i * P:(i + 1) * P], IDX[:, 4 * g + i, :], IDH[:, :])
                    mm.then_inc(idxt_ps, 1)
                def gather(s):
                    g = s // 9
                    pe.wait_ge(oh_ready, s + 1)
                    if s >= 2:
                        pe.wait_ge(u_ready, s - 1)
                    for t in range(TILES):
                        bl, bh = t // 4, (t // 2) % 2
                        o = bank(4 + 2 * (s % 2) + t // 8)[:, (t % 8) * 64:(t % 8 + 1) * 64]
                        for qh in range(2):
                            for part in range(2):
                                src = GX[:, part, qh, bl, :, bh * C + g * CG:bh * C + (g + 1) * CG]
                                mm = pe.matmul(o, OH[:, s % 2, qh, t * P:(t + 1) * P], src,
                                               start=(qh == 0 and part == 0), stop=(qh == 1 and part == 1))
                    mm.then_inc(ga_ps, 1)

                def contract(ch):
                    ns = min(8, SAMPLES - 8 * ch)
                    rows = ns * CG
                    pe.wait_ge(val_ready, 8 * ch + ns)
                    for q in range(4):
                        n = 4 * ch + q
                        if n >= 2:
                            pe.wait_ge(vt_in, n - 1)
                        for i in range(4):
                            t = 4 * (2 * (q % 2) + i // 2) + 2 * (q // 2) + i % 2
                            src = VAL[:, ch % 2, t, 0:ns, :].rearrange("p s c -> p (s c)")
                            mm = pe.transpose(bank(q % 2)[0:rows, i * P:(i + 1) * P], src, wt("ident"))
                        mm.then_inc(vt_ps, 1)
                    return rows

                def project(ch):
                    rows = P if ch < 4 else 64
                    pe.wait_ge(vt_in, 4 * ch + 4)
                    for bp in range(2):
                        for bh in range(2):
                            mm = pe.matmul(bank(2 + bp)[C * bh:C * bh + C, :], wt("wd", ch * C, C, 0, rows),
                                           VTA[0:rows, ch, (2 * bh + bp) * HC:(2 * bh + bp + 1) * HC],
                                           start=(ch == 0), stop=(ch == 4))
                        mm.then_inc(dc_ps, 1)

                for s in range(SAMPLES):
                    gather(s)
                    if s >= 9 and s % 8 == 1:
                        contract(s // 8 - 1)
                    if s >= 12 and s % 8 == 4:
                        project(s // 8 - 1)
                contract(4)
                project(3)
                project(4)

            @block.scalar
            def _(act):
                ln_act(act, 2, "epsc")
                act.wait_ge(w_in[3], 16)
                act.wait_ge(h_pad, 3)
                for h in range(2):
                    act.wait_ge(c1_ps, h + 1)
                    for k in range(3):
                        a, b = max(0, 1 - k), min(W, W + 1 - k)
                        act.activation(pair(HS3[k], h, 2, 0)[:, :, :, a:b], images(bank(4 + h))[:, :, :, a + k - 1:b + k - 1],
                                       ACT.Identity, bias=wt("c1b")).then_inc(h_in, 1)
                for n in range(2 * NB):
                    bl, qh = n // 2, n % 2
                    act.wait_ge(gx_ps, n + 1)
                    act.activation(GX[:, 0, qh, bl, :, :], bank(n % 4).rearrange("p (k c) -> p k c", k=4), ACT.Copy,
                                   scale=GSCALE).then_inc(gx_hi, 1)
                for g in range(NB):
                    act.wait_ge(idxt_ps, g + 1)
                    act.activation(IDXT[:, g * HC:(g + 1) * HC], bank(g).bitcast(FP16)[0:SAMPLES, 0:HC], ACT.Copy).then_inc(idxt_in, 1)

                def evac(ch):
                    rows = P if ch < 4 else 64
                    for q in range(4):
                        act.wait_ge(vt_ps, 4 * ch + q + 1)
                        act.activation(VTA[0:rows, ch, q * 512:(q + 1) * 512], bank(q % 2)[0:rows, :], ACT.Copy).then_inc(vt_in, 1)
                for ch in range(5):
                    evac(ch)

            @block.vector
            def _(dve):
                dve.wait_ge(y_pad, 1)
                ln_dve(dve, 2, padded_y)
                dve.wait_ge(w_in[3], 16)
                dve.wait_ge(ln_done, 6)
                for k in range(2):
                    dve.tensor_copy(XS[k][:, :, :], YP[:, :, 2 + k:2 + k + W]).then_inc(xs_ready, 1)
                dve.tensor_copy(IDH[:, :], wt("ident")).then_inc(cast1, 1)
                for n in range(2 * NB):
                    bl, qh = n // 2, n % 2
                    dve.wait_ge(gx_hi, n + 1)
                    dve.scalar_tensor_tensor(out=GX[:, 1, qh, bl, :, :].rearrange("p k c -> p (k c)"), in0=bank(n % 4), scalar=GSCALE,
                                             in1=GX[:, 0, qh, bl, :, :].rearrange("p k c -> p (k c)"), op0=ALU.mult,
                                             op1=ALU.subtract).then_inc(gx_done, 1)
                for h in range(2):
                    pos = wt("pos").rearrange("p (i k) -> p i k", i=2)
                    bias = wt("c2b").rearrange("p (o k) -> p o k", o=1).broadcast_to([P, 2, 72])
                    ins = dve.tensor_tensor(POS[:, 2 * h:2 * h + 2, :], pos, bias, ALU.add)
                after(dve, ins)
                for g in range(NB):
                    t = slice(4 * g, 4 * g + 4)
                    py, base, u0, u1 = PY[:, t, :], BASE[:, t, :], U0[:, t, :], U1[:, t, :]
                    dve.wait_ge(c2_ps, g + 1)
                    after(dve, dve.tensor_tensor(py.rearrange("p (h i) k -> p h i k", h=2),
                                                 bank(4 + g, 288).rearrange("p (i h k) -> p h i k", i=2, h=2),
                                                 POS[:, :, :].rearrange("p (h i) k -> p h i k", h=2), ALU.add))
                    after(dve, dve.tensor_scalar(base, py, -0.5, 0.0, ALU.add, ALU.max))
                    after(dve, dve.tensor_scalar(base, base, float(H - 2), 8388608.0, ALU.min, ALU.add))
                    after(dve, dve.tensor_scalar(base, base, -8388608.0, None, ALU.add))
                    dve.scalar_tensor_tensor(out=IDX[:, t, :], in0=base[:, :, 0:36], scalar=float(W), in1=base[:, :, 36:72],
                                             op0=ALU.mult, op1=ALU.add).then_inc(idx_ready, 1)
                    after(dve, dve.tensor_tensor(py, py, base, ALU.subtract))
                    dve.tensor_scalar(u0, py, -1.0, 1.0, ALU.mult, ALU.add)
                    after(dve, dve.tensor_scalar(u1, py, -1.0, 2.0, ALU.mult, ALU.add))
                    dve.scalar_tensor_tensor(out=u0, in0=py, scalar=1.0, in1=u0, op0=ALU.add, op1=ALU.min)
                    after(dve, dve.scalar_tensor_tensor(out=u1, in0=py, scalar=0.0, in1=u1, op0=ALU.add, op1=ALU.min))
                    dve.tensor_scalar(u0, u0, 0.0, None, ALU.max)
                    after(dve, dve.tensor_scalar(u1, u1, 0.0, None, ALU.max))
                    for k in range(4):
                        wy = (u0, u1)[k // 2][:, :, 0:36].rearrange("p t s -> p s t")
                        wx = (u0, u1)[k % 2][:, :, 36:72].rearrange("p t s -> p s t")
                        ins = dve.scalar_tensor_tensor(out=WC[:, :, t, k], in0=wy, scalar=1.0 / GSCALE, in1=wx,
                                                       op0=ALU.mult, op1=ALU.mult)
                after(dve, ins)

                def compare(s):
                    dve.wait_ge(bc_in[s % NBC], 16 * (s // NBC + 1))
                    if s >= 2:
                        dve.wait_ge(ga_ps, s - 1)
                    for qh in range(2):
                        ins = dve.tensor_scalar(OH[:, s % 2, qh, :], BC[:, s % NBC, :], wt("qidx", qh, 1), None, ALU.is_equal)
                    ins.then_inc(oh_ready, 1)

                def weigh(s):
                    dve.wait_ge(ga_ps, s + 1)
                    if s >= 2:
                        dve.wait_ge(val_ready, s - 1)
                    for half in range(2):
                        o = U[s % 2][:, 8 * half:8 * half + 8, :, :].rearrange("p t k c -> p (t k) c")
                        src = bank(4 + 2 * (s % 2) + half).rearrange("p (k c) -> p k c", c=CG)
                        w = WC[:, s, 8 * half:8 * half + 8, :].rearrange("p t (k o) -> p (t k) o", o=1).broadcast_to([P, 32, CG])
                        ins = dve.tensor_tensor(o, src, w, ALU.mult)
                    ins.then_inc(u_ready, 1)

                compare(0)
                for s in range(SAMPLES):
                    if s + 1 < SAMPLES:
                        compare(s + 1)
                    weigh(s)
                for bp in range(2):
                    c = slice(bp * HC, (bp + 1) * HC)
                    dve.wait_ge(dc_ps, 8 + bp + 1)
                    dve.scalar_tensor_tensor(out=X[:, c], in0=bank(2 + bp), scalar=0.0, in1=X[:, c], op0=ALU.max, op1=ALU.add)

        with ExitStack() as sctx, nc.Block() as block:
            WCOL = sb("WCOL", [P, TILES], F32, sctx)
            WSEL = sb("WSEL", [P, TILES], F32, sctx)
            CNT = sb("CNT", [P, 2, TILES], F32, sctx)
            JUNK = sb("JUNK", [P, 2, TILES, PIX], F32, sctx)
            DIAG = sb("DIAG", [P, TILES, P], F32, sctx)
            DIAG2 = sb("DIAG2", [P, TILES, P], F32, sctx)
            WMB = sb("WMB", [P, COLS], F32, sctx)
            HID = sb("HID1", [P, 4, HC], F32, sctx)
            w_ps, dg_ready, row_ps, dg2_ready, wm_ps, wm_in, hid_ps, hid_in, hid_used, f_ps = (sem("s4_" + n) for n in (
                "w_ps", "dg_ready", "row_ps", "dg2_ready", "wm_ps", "wm_in", "hid_ps", "hid_in", "hid_used", "f_ps"))
            UNITS = [(bh, bp, m) for bp in range(2) for m in range(2) for bh in range(2)]

            @block.sync
            def _(sp):
                load_weights(sp, 5)

            @block.tensor
            def _(pe):
                ln_pe(pe, 3)
                pe.wait_ge(w_in[4], 16)
                for r in range(TILES // 2):
                    pe.wait_ge(ln_done, 7 + r // NB)
                    mm = pe.matmul(bank(4)[:, r * 2:(r + 1) * 2], Y[:, r * P:(r + 1) * P], wt("wr1"), start=True, stop=True)
                mm.then_inc(w_ps, 1)
                for q in range(4):
                    pe.wait_ge(dg_ready, q + 1)
                    pe.matmul(bank(q), wt("ones"), DIAG[:, 4 * q:4 * q + 4, :], start=True, stop=True).then_inc(row_ps, 1)
                pe.wait_ge(dg2_ready, 1)
                for bp in range(2):
                    for bh in range(2):
                        q = 2 * bh + bp
                        mm = pe.matmul(bank(6 + bp)[C * bh:C * bh + C, :], wt("ones", 0, C), DIAG2[:, 4 * q:4 * q + 4, :],
                                       start=True, stop=True)
                    mm.then_inc(wm_ps, 1)

                def up(n):
                    bh, bp, m = UNITS[n]
                    if n >= 2:
                        pe.wait_ge(hid_in, n - 1)
                    pe.matmul(bank(2 + n % 2), wt("w1_1", bh * FH1 + m * P, P),
                              Y[:, bp * HC:(bp + 1) * HC], start=True, stop=True).then_inc(hid_ps, 1)

                up(0)
                up(1)
                for n in range(0, len(UNITS), 2):
                    if n + 2 < len(UNITS):
                        up(n + 2)
                        up(n + 3)
                    for i in range(2):
                        bh, bp, m = UNITS[n + i]
                        pe.wait_ge(hid_in, n + i + 1)
                        pe.matmul(bank(bp)[C * bh:C * bh + C, :], wt("w2_1", m * C, C), HID[:, (n + i) % 4, :],
                                  start=(m == 0), stop=(m == 1)).then_inc(hid_used, 1)

            @block.scalar
            def _(act):
                ln_act(act, 3, "epst")
                act.wait_ge(w_in[4], 16)
                for bp in range(2):
                    act.wait_ge(wm_ps, bp + 1)
                    act.activation(WMB[:, bp * HC:(bp + 1) * HC], bank(6 + bp), ACT.Copy).then_inc(wm_in, 1)
                for n, (bh, bp, m) in enumerate(UNITS):
                    act.wait_ge(hid_ps, n + 1)
                    if n >= 4:
                        act.wait_ge(hid_used, n - 3)
                    act.activation(HID[:, n % 4, :], bank(2 + n % 2), ACT.Gelu_apprx_tanh, bias=wt("b1_1", m, 1)).then_inc(hid_in, 1)

            @block.vector
            def _(dve):
                ln_dve(dve, 3, flat)
                dve.wait_ge(w_in[4], 16)
                dve.wait_ge(w_ps, 1)
                for bh in range(2):
                    raw = bank(4, TILES).rearrange("p (r h) -> p h r", h=2)
                    ins = dve.tensor_scalar(WCOL[:, 8 * bh:8 * bh + 8], raw[:, bh], wt("br1"), None, ALU.add)
                after(dve, ins)
                for t in range(TILES):
                    ins = dve.tensor_scalar(DIAG[:, t, :], wt("ident"), WCOL[:, t:t + 1], None, ALU.mult)
                    if t % 4 == 3:
                        ins.then_inc(dg_ready, 1)
                for t in range(TILES):
                    dve.wait_ge(row_ps, t // 4 + 1)
                    row = bank(t // 4)[:, ((t // 2) % 2) * PIX:((t // 2) % 2 + 1) * PIX]
                    dve.tensor_scalar(JUNK[:, 0, t, :], row, WCOL[:, t:t + 1], None, ALU.is_gt, ALU.add, accum_out=CNT[:, 0, t:t + 1])
                    ins = dve.scalar_tensor_tensor(out=JUNK[:, 1, t, :], in0=row, scalar=WCOL[:, t:t + 1],
                                                   in1=wt("before1", (t % 2) * PIX, PIX), op0=ALU.is_equal, op1=ALU.mult,
                                                   accum_out=CNT[:, 1, t:t + 1])
                after(dve, ins)
                after(dve, dve.tensor_tensor(WSEL[:, :], CNT[:, 0, :], CNT[:, 1, :], ALU.add))
                after(dve, dve.tensor_scalar(WSEL[:, :], WSEL[:, :], float(TOPK), None, ALU.is_lt))
                after(dve, dve.tensor_tensor(WSEL[:, :], WSEL[:, :], WCOL[:, :], ALU.mult))
                for t in range(TILES):
                    ins = dve.tensor_scalar(DIAG2[:, t, :], wt("ident"), WSEL[:, t:t + 1], None, ALU.mult)
                ins.then_inc(dg2_ready, 1)
                after(dve, dve.tensor_tensor(X[:, :], X[:, :], Y[:, :], ALU.add))
                for bp in range(2):
                    c = slice(bp * HC, (bp + 1) * HC)
                    dve.wait_ge(hid_used, 4 * bp + 4)
                    dve.wait_ge(wm_in, bp + 1)
                    after(dve, dve.scalar_tensor_tensor(out=SQ[:, c], in0=bank(bp), scalar=wt("b2_1"), in1=WMB[:, c],
                                                        op0=ALU.add, op1=ALU.mult))
                    dve.tensor_tensor(X[:, c], X[:, c], SQ[:, c], ALU.add)

        with ExitStack() as sctx, nc.Block() as block:
            GATES = [sb(f"GATE{k}", [P, COLS], F32, sctx) for k in range(4)]
            ST = sb("ST", [P, COLS], F32, sctx)
            gate_ps, gate_in = sem("s5_gate_ps"), sem("s5_gate_in")
            gbank = [4, 5, 6, 7, 0, 1, 2, 3]

            @block.sync
            def _(sp):
                load_weights(sp, 6)

            @block.tensor
            def _(pe):
                ln_pe(pe, 4)
                pe.wait_ge(w_in[5], 16)
                for k in range(4):
                    for h in range(2):
                        if k == 0:
                            pe.wait_ge(ln_done, 9 + h)
                        pe.matmul(bank(gbank[2 * k + h]), wt("ssw", k * P, P), Y[:, h * HC:(h + 1) * HC],
                                  start=True, stop=True).then_inc(gate_ps, 1)

            @block.scalar
            def _(act):
                ln_act(act, 4, "epsc")
                act.wait_ge(w_in[5], 16)
                warm(act, ACT.Sigmoid)
                for k in range(4):
                    for h in range(2):
                        act.wait_ge(gate_ps, 2 * k + h + 1)
                        act.activation(GATES[k][:, h * HC:(h + 1) * HC], bank(gbank[2 * k + h]), ACT.Sigmoid,
                                       bias=wt("ssb", k, 1)).then_inc(gate_in, 1)

            @block.vector
            def _(dve):
                ln_dve(dve, 4, flat)
                A, BG, CG_, DG_ = GATES
                dve.wait_ge(gate_in, 2)
                dve.memset(A[:, :].rearrange("p (r w) -> p r w", w=W)[:, :, 0:1], 0.0)
                dve.wait_ge(gate_in, 4)
                after(dve, dve.tensor_tensor(BG[:, :], BG[:, :], Y[:, :], ALU.mult))
                after(dve, dve.tensor_tensor_scan(ST[:, :], A[:, :], BG[:, :], 0.0, ALU.mult, ALU.add))
                dve.wait_ge(gate_in, 8)
                dve.tensor_tensor(DG_[:, :], DG_[:, :], Y[:, :], ALU.mult)
                after(dve, dve.tensor_tensor(CG_[:, :], CG_[:, :], ST[:, :], ALU.mult))
                after(dve, dve.tensor_tensor(X[:, :], X[:, :], DG_[:, :], ALU.add))
                dve.tensor_tensor(X[:, :], X[:, :], CG_[:, :], ALU.add)

        with ExitStack() as sctx, nc.Block() as block:
            DGI = sb("DGI", [P, 18, P])
            diag7 = sem("s7_diag")
            SUM = sb("SUM", [P, PIX], F32, sctx)
            LG = sb("LG2", [P, 2, E], F32, sctx)
            RED = sb("RED2", [P, 2], F32, sctx)
            WT = sb("WT", [P, PIX], F32, sctx)
            SEL2 = sb("SEL2", [P, E, P], F32, sctx)
            WB = sb("WB", [P, E, PIX], F32, sctx)
            BNS = [sb(f"BNS{i}", [P, E], F32, sctx) for i in range(2)]
            BNT = [sb(f"BNT{i}", [P, E], F32, sctx) for i in range(2)]
            H1 = sb("H1", [P, 2, HC], F32, sctx)
            H2 = sb("H2", [P, 2, HC], F32, sctx)
            H2W = sb("H2W", [P, 2, HC], F32, sctx)
            (bn_sd, bn_done, sum_done, g_ps, g_exp, g_sum, g_ready, wt_ps, wt_in, wb_ps, wb_in, a_ps, a_in, b_ps, b_in, weighted,
             c_done, f_ps) = (sem("s6_" + n) for n in (
                "bn_sd", "bn_done", "sum_done", "g_ps", "g_exp", "g_sum", "g_ready", "wt_ps", "wt_in", "wb_ps", "wb_in", "a_ps",
                "a_in", "b_ps", "b_in", "weighted", "c_done", "f_ps"))
            NU = 2 * E

            wt_zeroed = sem("s6_wt_zeroed")

            @block.sync
            def _(sp):
                load_weights(sp, 7)

            @block.gpsimd
            def _(pool):
                pool.memset(WT[:, :], 0.0).then_inc(wt_zeroed, 1)
                pool.wait_ge(w_in[7], 16)
                for i, name in enumerate(("dwi", "dwo")):
                    for m in range(9):
                        pool.tensor_scalar(DGI[:, 9 * i + m, :], wt("ident"), wt(name, m, 1), None, ALU.mult).then_inc(diag7, 1)

            @block.tensor
            def _(pe):
                ln_pe(pe, 5)
                pe.wait_ge(w_in[6], 16)
                pe.wait_ge(sum_done, 1)
                for h in range(2):
                    mm = pe.matmul(bank(4)[:, h * E:(h + 1) * E], SUM[:, h * P:(h + 1) * P], wt("wr2"), start=True, stop=True)
                mm.then_inc(g_ps, 1)
                pe.wait_ge(g_ready, 1)
                for h in range(2):
                    mm = pe.transpose(bank(5)[0:E, h * P:(h + 1) * P], LG[:, h, :], wt("ident"))
                mm.then_inc(wt_ps, 1)
                pe.wait_ge(wt_in, 1)
                for q in range(4):
                    for i in range(2):
                        mm = pe.matmul(bank(4 + q)[:, i * PIX:(i + 1) * PIX], SEL2[:, 2 * q + i, :], WT[:, :], start=True, stop=True)
                    mm.then_inc(wb_ps, 1)
                pe.wait_ge(wb_in, 4)

                def first(n):
                    e, h = n // 2, n % 2
                    if n >= 2:
                        pe.wait_ge(a_in, n - 1)
                    pe.matmul(bank(2 + n % 2), wt("w1_2", e * P, P), Y[:, h * HC:(h + 1) * HC], start=True, stop=True).then_inc(a_ps, 1)

                def second(n):
                    pe.wait_ge(a_in, n + 1)
                    if n >= 2:
                        pe.wait_ge(b_in, n - 1)
                    pe.matmul(bank(4 + n % 2), wt("w2_2", (n // 2) * P, P), H1[:, n % 2, :], start=True, stop=True).then_inc(b_ps, 1)

                def third(n):
                    pe.wait_ge(weighted, n + 1)
                    pe.matmul(bank(n % 2), wt("wo_2", (n // 2) * P, P), H2W[:, n % 2, :], start=(n < 2), stop=False).then_inc(c_done, 1)

                first(0)
                for n in range(NU):
                    if n + 1 < NU:
                        first(n + 1)
                    second(n)
                    if n >= 1:
                        third(n - 1)
                third(NU - 1)
                for h in range(2):
                    rhs = WT[:, :].rearrange("p (o n) -> p o n", o=1).broadcast_to([P, 2, PIX])
                    pe.matmul(bank(h), wt("bo2"), rhs, start=False, stop=True).then_inc(f_ps, 1)

            @block.scalar
            def _(act):
                ln_act(act, 5, "epst")
                act.wait_ge(w_in[6], 16)
                for i in range(2):
                    act.activation(BNS[i][:, :], wt(f"bn{i + 1}", 4 * E, E), ACT.Sqrt, bias=wt("epsb")).then_inc(bn_sd, 1)
                warm(act, ACT.Exp)
                act.wait_ge(g_exp, 1)
                act.activation(LG[:, :, :], LG[:, :, :], ACT.Exp).then_inc(g_sum, 1)
                act.wait_ge(wt_ps, 1)
                act.wait_ge(wt_zeroed, 1)
                act.activation(WT[0:E, :], bank(5)[0:E, 0:PIX], ACT.Copy).then_inc(wt_in, 1)
                for q in range(4):
                    act.wait_ge(wb_ps, q + 1)
                    act.activation(WB[:, 2 * q:2 * q + 2, :], bank(4 + q).rearrange("p (e n) -> p e n", e=2), ACT.Copy).then_inc(wb_in, 1)
                act.wait_ge(bn_done, 1)

                def relu1(n):
                    act.wait_ge(a_ps, n + 1)
                    if n >= 2:
                        act.wait_ge(b_ps, n - 1)
                    act.activation(H1[:, n % 2, :], bank(2 + n % 2), ACT.Relu, bias=BNT[0][:, n // 2:n // 2 + 1],
                                   scale=BNS[0][:, n // 2:n // 2 + 1]).then_inc(a_in, 1)

                def relu2(n):
                    act.wait_ge(b_ps, n + 1)
                    if n >= 2:
                        act.wait_ge(weighted, n - 1)
                    act.activation(H2[:, n % 2, :], bank(4 + n % 2), ACT.Relu, bias=BNT[1][:, n // 2:n // 2 + 1],
                                   scale=BNS[1][:, n // 2:n // 2 + 1]).then_inc(b_in, 1)

                relu1(0)
                for n in range(NU):
                    if n + 1 < NU:
                        relu1(n + 1)
                    relu2(n)

            @block.vector
            def _(dve):
                ln_dve(dve, 5, flat)
                dve.wait_ge(ln_done, 12)
                dve.tensor_reduce(SUM[:, :], Y[:, :].rearrange("p (b n) -> p n b", b=NB), AX.X, ALU.add).then_inc(sum_done, 1)
                dve.wait_ge(w_in[6], 16)
                dve.tensor_copy(SEL2[:, :, :], wt("ident", 0, E).rearrange("p (e o) -> p e o", o=1).broadcast_to([P, E, P]))
                dve.wait_ge(bn_sd, 2)
                for i in range(2):
                    name = f"bn{i + 1}"
                    after(dve, dve.reciprocal(BNS[i][:, :], BNS[i][:, :]))
                    dve.tensor_tensor(BNS[i][:, :], BNS[i][:, :], wt(name, E, E), ALU.mult)
                    after(dve, dve.tensor_tensor(BNT[i][:, :], wt(name, 0, E), wt(name, 3 * E, E), ALU.subtract))
                    after(dve, dve.tensor_tensor(BNT[i][:, :], BNT[i][:, :], BNS[i][:, :], ALU.mult))
                    ins = dve.tensor_tensor(BNT[i][:, :], BNT[i][:, :], wt(name, 2 * E, E), ALU.add)
                ins.then_inc(bn_done, 1)
                dve.wait_ge(g_ps, 1)
                br = wt("br2").rearrange("p (o e) -> p o e", o=1).broadcast_to([P, 2, E])
                after(dve, dve.scalar_tensor_tensor(out=LG[:, :, :], in0=bank(4, 2 * E).rearrange("p (h e) -> p h e", h=2),
                                                    scalar=1.0 / B, in1=br, op0=ALU.mult, op1=ALU.add))
                softmax_dve(dve, LG, RED, 2, g_exp, 1, g_sum)
                dve.engine_nop().then_inc(g_ready, 1)
                dve.wait_ge(wb_in, 4)
                for n in range(NU):
                    dve.wait_ge(b_in, n + 1)
                    if n >= 2:
                        dve.wait_ge(c_done, n - 1)
                    w = WB[:, n // 2, :].rearrange("p (o n) -> p o n", o=1).broadcast_to([P, 2, PIX])
                    dve.tensor_tensor(H2W[:, n % 2, :].rearrange("p (b n) -> p b n", b=2),
                                      H2[:, n % 2, :].rearrange("p (b n) -> p b n", b=2), w, ALU.mult).then_inc(weighted, 1)
                for h in range(2):
                    c = slice(h * HC, (h + 1) * HC)
                    dve.wait_ge(f_ps, h + 1)
                    dve.tensor_tensor(X[:, c], bank(h), X[:, c], ALU.add)

        with ExitStack() as sctx, nc.Block() as block:
            YP, ZP, OP = (sb(n, [P, PROWS, PW], F32, sctx) for n in ("YP7", "ZP7", "OP7"))
            R = sb("R", [P, COLS], F32, sctx)
            M = sb("M7", [P, 2, HC], F32, sctx)
            ACC = sb("ACC7", [P, COLS], F32, sctx)
            y_pad, pads, ones_set, z_ps, r_ps, r_in, k_ps, k_used, o_ready, o_ps = (sem("s7_" + n) for n in (
                "y_pad", "pads", "ones_set", "z_ps", "r_ps", "r_in", "k_ps", "k_used", "o_ready", "o_ps"))
            z_in = [sem(f"s7_z_in{h}") for h in range(2)]
            PTAPS = 4
            WROWS = PITCH + H
            WIN = sb("WIN", [P, WROWS, W], F32, sctx)

            def padded_y7(h):
                return pair(YP, h, 2, 2), images

            @block.sync
            def _(sp):
                load_weights(sp, 8)

            @block.gpsimd
            def _(pool):
                pool.memset(YP[:, :, :], 0.0).then_inc(y_pad, 1)
                for b in (ZP, OP):
                    pool.memset(b[:, :, :], 0.0).then_inc(pads, 1)
                after_pool(pool, pool.memset(R[:, :], 0.0))
                pool.memset(R[32:33, :], 1.0).then_inc(ones_set, 1)

            @block.tensor
            def _(pe):
                ln_pe(pe, 6)
                pe.wait_ge(w_in[7], 16)
                pe.wait_ge(diag7, 18)
                pe.wait_ge(ln_done, 14)
                for m in range(9):
                    mm = pe.matmul(bank(4), DGI[:, m, :], pair(YP, 0, 1 + m // 3, 1 + m % 3), start=(m == 0), stop=(m == 8))
                mm.then_inc(z_ps, 1)
                for h in range(2):
                    pe.wait_ge(z_in[h], 1)
                    pe.matmul(bank(6 + h)[0:32, :], wt("red"), pair(ZP, h, 2, 2), start=True, stop=True).then_inc(r_ps, 1)
                    pe.wait_ge(r_in, h + 1)
                    for k in range(9):
                        n = 9 * h + k
                        if n >= 4:
                            pe.wait_ge(k_used, n - 3)
                        pe.matmul(bank(n % 4), wt("span", k * P, P), R[:, h * HC:(h + 1) * HC],
                                  start=True, stop=True).then_inc(k_ps, 1)
                for h in range(2):
                    pe.wait_ge(o_ready, h + 1)
                    taps = 9 if h == 0 else PTAPS
                    for m in range(taps):
                        mm = pe.matmul(bank(4 + h), DGI[:, 9 + m, :], pair(OP, h, 1 + m // 3, 1 + m % 3), start=(m == 0), stop=(m == taps - 1))
                    mm.then_inc(o_ps, 1)

            @block.scalar
            def _(act):
                ln_act(act, 6, "epsc")
                act.wait_ge(w_in[7], 16)
                act.wait_ge(pads, 1)
                act.wait_ge(ones_set, 1)
                act.wait_ge(z_ps, 1)
                act.activation(pair(ZP, 0, 2, 2), images(bank(4)), ACT.Identity, bias=wt("dbi")).then_inc(z_in[0], 1)
                for h in range(2):
                    act.wait_ge(r_ps, h + 1)
                    act.activation(R[0:32, h * HC:(h + 1) * HC], bank(6 + h)[0:32, :], ACT.Relu, bias=wt("bred", 0, 1, 0, 32)).then_inc(r_in, 1)

            @block.vector
            def _(dve):
                dve.wait_ge(y_pad, 1)
                ln_dve(dve, 6, padded_y7)
                dve.wait_ge(w_in[7], 16)
                dve.wait_ge(pads, 2)
                dve.wait_ge(ln_done, 14)
                def window(pad, m):
                    return pad[:, 2 * PITCH + 1 + m // 3:2 * PITCH + 1 + m // 3 + WROWS, 1 + m % 3:1 + m % 3 + W]

                after(dve, dve.tensor_scalar(WIN[:, :, :], window(YP, 0), wt("dwi", 0, 1), wt("dbi"), ALU.mult, ALU.add))
                for m in range(1, 8):
                    after(dve, dve.scalar_tensor_tensor(out=WIN[:, :, :], in0=window(YP, m), scalar=wt("dwi", m, 1), in1=WIN[:, :, :],
                                                        op0=ALU.mult, op1=ALU.add))
                for i in range(2):
                    r = i * PITCH
                    ins = dve.scalar_tensor_tensor(out=ZP[:, 2 * PITCH + 2 + r:2 * PITCH + 2 + r + H, 2:2 + W],
                                                   in0=window(YP, 8)[:, r:r + H, :], scalar=wt("dwi", 8, 1), in1=WIN[:, r:r + H, :],
                                                   op0=ALU.mult, op1=ALU.add)
                ins.then_inc(z_in[1], 1)
                for h in range(2):
                    dve.wait_ge(z_in[h], 1)
                    for k in range(9):
                        n = 9 * h + k
                        c = slice(h * HC, (h + 1) * HC)
                        dve.wait_ge(k_ps, n + 1)
                        o = ACC[:, c] if k == 0 else M[:, n % 2, :]
                        dve.tensor_tensor(images(o), images(bank(n % 4)), pair(ZP, h, 1 + k // 3, 1 + k % 3), ALU.mult).then_inc(k_used, 1)
                        dve.wait_ge(k_used, n + 1)
                        if k == 8:
                            dve.tensor_tensor(pair(OP, h, 2, 2), images(ACC[:, c]), images(M[:, n % 2, :]), ALU.add).then_inc(o_ready, 1)
                        elif k:
                            after(dve, dve.tensor_tensor(ACC[:, c], ACC[:, c], M[:, n % 2, :], ALU.add))
                dve.wait_ge(o_ready, 2)
                after(dve, dve.tensor_scalar(WIN[:, :, :], window(OP, PTAPS), wt("dwo", PTAPS, 1), wt("dbo"), ALU.mult, ALU.add))
                for m in range(PTAPS + 1, 9):
                    after(dve, dve.scalar_tensor_tensor(out=WIN[:, :, :], in0=window(OP, m), scalar=wt("dwo", m, 1), in1=WIN[:, :, :],
                                                        op0=ALU.mult, op1=ALU.add))
                for i in range(2):
                    x = X[:, HC + i * PIX:HC + (i + 1) * PIX].rearrange("p (r w) -> p r w", w=W)
                    ins = dve.tensor_tensor(x, x, WIN[:, i * PITCH:i * PITCH + H, :], ALU.add)
                after(dve, ins)
                dve.wait_ge(o_ps, 1)
                dve.scalar_tensor_tensor(out=X[:, 0:HC], in0=bank(4), scalar=wt("dbo"), in1=X[:, 0:HC], op0=ALU.add, op1=ALU.add)
                dve.wait_ge(o_ps, 2)
                dve.tensor_tensor(X[:, HC:COLS], bank(5), X[:, HC:COLS], ALU.add)

        with ExitStack() as sctx, nc.Block() as block:
            LG = sb("LG8", [P, TILES, E], F32, sctx)
            RED = sb("RED8", [P, TILES], F32, sctx)
            RANK = sb("RANK8", [P, TILES, E], F32, sctx)
            OH8 = sb("OH8", [P, TILES, E], F32, sctx)
            TOT = sb("TOT", [P, 3, TILES, E], F32, sctx)
            GATE = sb("GATE8", [P, 2, TILES], F32, sctx)
            DIAG = sb("DIAG8", [P, TILES, P], F32, sctx)
            YU = sb("YU", [P, TILES * P], F32, sctx)
            OHT = sb("OHT", [P, TILES * P], F32, sctx)
            SCB = sb("SCB", [P, COLS], F32, sctx)
            HID = sb("HID8", [P, 4, HC], F32, sctx)
            FIN = sb("FIN", [P, 4, HC], F32, sctx)
            MASK = sb("MASK8", [P, 3, HC], I32, sctx)
            oht_ps, oht_in, limits, x_final = sem("s8_oht_ps"), sem("s8_oht_in"), sem("s8_limits"), sem("s8_x_final")
            (g_ps, g_exp, g_sum, oh_ready, cum_ps, nm_ready, t_ps, t_in, yu_in, scale_ready, sc_ps, sc_in, hid_ps, hid_in_a, hid_in_v,
             hid_used, f_ps) = (sem("s8_" + n) for n in (
                "g_ps", "g_exp", "g_sum", "oh_ready", "cum_ps", "nm_ready", "t_ps", "t_in", "yu_in", "scale_ready", "sc_ps", "sc_in",
                "hid_ps", "hid_in_a", "hid_in_v", "hid_used", "f_ps"))
            UNITS = [(e, m, bp, bh) for bp in range(2) for e in range(E) for m in range(2) for bh in range(2)]
            OHT_AT, SCALE_AT = {4: 0, 8: 1, 12: 2, 16: 3}, {20: 0, 24: 1}
            NU = len(UNITS)
            zeroed = sem("s8_zeroed")

            @block.sync
            def _(sp):
                ov = out_dram.rearrange("(g b) c p -> g c b p", g=2)
                for bp in range(2):
                    sp.wait_ge(x_final, bp + 1)
                    for g in range(2):
                        sp.dma_start(ov[g, :, 2 * bp:2 * bp + 2, :],
                                     X[C * g:C * g + C, bp * HC:(bp + 1) * HC].rearrange("c (b p) -> c b p", b=2)).then_inc(stored, 16)
                sp.wait_ge(stored, 64)

            @block.gpsimd
            def _(pool):
                pool.memset(YU[:, :], 0.0).then_inc(zeroed, 1)
                pool.memset(OHT[:, :], 0.0).then_inc(zeroed, 1)

            @block.tensor
            def _(pe):
                ln_pe(pe, 7)
                pe.wait_ge(w_in[8], 16)
                for r in range(TILES // 2):
                    pe.wait_ge(ln_done, 15 + r // NB)
                    mm = pe.matmul(bank(4)[:, r * 2 * E:(r + 1) * 2 * E], Y[:, r * P:(r + 1) * P], wt("gate3"), start=True, stop=True)
                mm.then_inc(g_ps, 1)
                pe.wait_ge(oh_ready, 1)
                oh = OH8[:, :, :].rearrange("p t e -> p (t e)")
                pe.matmul(bank(6, P), wt("tri"), oh, start=True, stop=True)
                pe.matmul(bank(7, P), wt("ones"), oh, start=True, stop=True).then_inc(cum_ps, 1)
                for q in range(4):
                    for i in range(4):
                        mm = pe.transpose(bank(q)[0:E, i * P:(i + 1) * P], RANK[:, 4 * q + i, :], wt("ident"))
                    mm.then_inc(t_ps, 1)
                pe.wait_ge(t_in, 4)
                pe.wait_ge(yu_in, 2)

                def transpose_one_hot(q):
                    pe.wait_ge(scale_ready, 1)
                    if q >= 2:
                        pe.wait_ge(oht_in, q - 1)
                    for i in range(4):
                        mm = pe.transpose(bank(6 + q % 2)[0:E, i * P:(i + 1) * P], OH8[:, 4 * q + i, :], wt("ident"))
                    mm.then_inc(oht_ps, 1)

                def spread_scale(bp):
                    pe.wait_ge(oht_in, 3 + bp)
                    for bh in range(2):
                        q = 2 * bh + bp
                        mm = pe.matmul(bank(6 + bp)[C * bh:C * bh + C, :], wt("ones", 0, C), DIAG[:, 4 * q:4 * q + 4, :],
                                       start=True, stop=True)
                    mm.then_inc(sc_ps, 1)

                def finish(bp):
                    for bh in range(2):
                        mm = pe.matmul(bank(bp)[C * bh:C * bh + C, :], wt("b2_3"),
                                       OHT[:, (2 * bh + bp) * HC:(2 * bh + bp + 1) * HC], start=False, stop=True)
                    mm.then_inc(f_ps, 1)

                def up(n):
                    e, m, bp, bh = UNITS[n]
                    if n >= 4:
                        pe.wait_ge((hid_in_a, hid_in_v)[n % 2], n // 2 - 1)
                    pe.matmul(bank(2 + n % 4), wt("w1_3", e * FH3 + m * P, P), YU[:, (2 * bh + bp) * HC:(2 * bh + bp + 1) * HC],
                              start=True, stop=True).then_inc(hid_ps, 1)

                up(0)
                up(1)
                for n in range(0, NU, 2):
                    if n + 2 < NU:
                        up(n + 2)
                        up(n + 3)
                    for i, hid_in in enumerate((hid_in_a, hid_in_v)):
                        e, m, bp, bh = UNITS[n + i]
                        pe.wait_ge(hid_in, n // 2 + 1)
                        pe.matmul(bank(bp)[C * bh:C * bh + C, :], wt("w2_3", (2 * e + m) * C, C), HID[:, (n + i) % 4, :],
                                  start=(e == 0 and m == 0), stop=False).then_inc(hid_used, 1)
                    if n in OHT_AT:
                        transpose_one_hot(OHT_AT[n])
                    if n in SCALE_AT:
                        spread_scale(SCALE_AT[n])
                    if n + 2 == NU // 2:
                        finish(0)
                pe.wait_ge(oht_in, 4)
                finish(1)

            @block.scalar
            def _(act):
                ln_act(act, 7, "epst")
                act.wait_ge(w_in[8], 16)
                warm(act, ACT.Exp)
                act.wait_ge(zeroed, 2)
                for h in range(2):
                    act.wait_ge(ln_done, 15 + h)
                    act.activation(YU[0:C, :].rearrange("p (b c) -> p b c", b=2)[:, 0, h * HC:(h + 1) * HC],
                                   Y[0:C, h * HC:(h + 1) * HC], ACT.Copy)
                    act.activation(YU[0:C, :].rearrange("p (b c) -> p b c", b=2)[:, 1, h * HC:(h + 1) * HC],
                                   Y[C:P, h * HC:(h + 1) * HC], ACT.Copy).then_inc(yu_in, 1)
                act.wait_ge(g_exp, 1)
                act.activation(LG[:, :, :], LG[:, :, :], ACT.Exp).then_inc(g_sum, 1)
                for q in range(4):
                    act.wait_ge(t_ps, q + 1)
                    act.activation(YU[C:C + E, q * HC:(q + 1) * HC], bank(q)[0:E, :], ACT.Copy).then_inc(t_in, 1)
                for n in range(0, NU, 2):
                    e, m, bp, bh = UNITS[n]
                    act.wait_ge(hid_ps, n + 1)
                    if n >= 4:
                        act.wait_ge(hid_used, n - 3)
                    act.activation(HID[:, n % 4, :], bank(2 + n % 4), ACT.Relu, bias=wt("b1_3", 2 * e + m, 1)).then_inc(hid_in_a, 1)
                    if n in OHT_AT:
                        q = OHT_AT[n]
                        act.wait_ge(oht_ps, q + 1)
                        act.activation(OHT[0:E, q * HC:(q + 1) * HC], bank(6 + q % 2)[0:E, :], ACT.Copy).then_inc(oht_in, 1)
                    if n in SCALE_AT:
                        bp = SCALE_AT[n]
                        act.wait_ge(sc_ps, bp + 1)
                        act.activation(SCB[:, bp * HC:(bp + 1) * HC], bank(6 + bp), ACT.Copy).then_inc(sc_in, 1)

            @block.vector
            def _(dve):
                ln_dve(dve, 7, flat)
                dve.wait_ge(w_in[8], 16)
                dve.wait_ge(g_ps, 1)
                for bh in range(2):
                    gb = wt("gb3").rearrange("p (o e) -> p o e", o=1).broadcast_to([P, 8, E])
                    raw = bank(4, TILES * E).rearrange("p (r h e) -> p h r e", h=2, e=E)
                    ins = dve.tensor_tensor(LG[:, 8 * bh:8 * bh + 8, :], raw[:, bh], gb, ALU.add)
                after(dve, ins)
                softmax_dve(dve, LG, RED, TILES, g_exp, 1, g_sum)
                first_max_dve(dve, LG, RANK, RED, OH8)
                dve.tensor_scalar(RANK[:, :, :], OH8[:, :, :], -1.0, 1.0, ALU.mult, ALU.add).then_inc(oh_ready, 1)
                dve.tensor_reduce(GATE[:, 0, :], LG[:, :, :], AX.X, ALU.max)
                dve.wait_ge(cum_ps, 1)
                tot = bank(7, P).rearrange("p (t e) -> p t e", e=E)
                after(dve, dve.tensor_copy(TOT[:, 0, :, :], tot))
                for i, d in enumerate((1, 2, 4, 8)):
                    src, dst = TOT[:, i % 2], TOT[:, (i + 1) % 2]
                    dve.tensor_copy(dst[:, 0:d, :], src[:, 0:d, :])
                    after(dve, dve.tensor_tensor(dst[:, d:TILES, :], src[:, d:TILES, :], src[:, 0:TILES - d, :], ALU.add))
                after(dve, dve.tensor_tensor(TOT[:, 1, :, :], TOT[:, 0, :, :], tot, ALU.subtract))
                after(dve, dve.tensor_tensor(TOT[:, 1, :, :], TOT[:, 1, :, :], bank(6, P).rearrange("p (t e) -> p t e", e=E), ALU.add))
                after(dve, dve.tensor_tensor(TOT[:, 1, :, :], TOT[:, 1, :, :], OH8[:, :, :], ALU.mult))
                after(dve, dve.tensor_reduce(GATE[:, 1, :], TOT[:, 1, :, :], AX.X, ALU.add))
                after(dve, dve.tensor_scalar(GATE[:, 1, :], GATE[:, 1, :], float(CAP), None, ALU.is_le))
                after(dve, dve.tensor_tensor(GATE[:, 0, :], GATE[:, 0, :], GATE[:, 1, :], ALU.mult))
                for t in range(TILES):
                    ins = dve.tensor_scalar(DIAG[:, t, :], wt("ident"), GATE[:, 0, t:t + 1], None, ALU.mult)
                ins.then_inc(scale_ready, 1)
                for n in range(3):
                    dve.memset(FIN[:, 1 + n, :], (0.0, 1.0e4, -1.0e4)[n]).then_inc(limits, 1)

                def finish(bp):
                    c = slice(bp * HC, (bp + 1) * HC)
                    dve.wait_ge(limits, 3)
                    dve.wait_ge(f_ps, bp + 1)
                    dve.wait_ge(sc_in, bp + 1)
                    after(dve, dve.tensor_tensor(FIN[:, 0, :], bank(bp), SCB[:, c], ALU.mult))
                    dve.tensor_tensor(MASK[:, 0, :], FIN[:, 0, :], FIN[:, 0, :], ALU.not_equal)
                    dve.tensor_scalar(MASK[:, 1, :], FIN[:, 0, :], 3.4028234e38, None, ALU.is_gt)
                    after(dve, dve.tensor_scalar(MASK[:, 2, :], FIN[:, 0, :], -3.4028234e38, None, ALU.is_lt))
                    for n in range(3):
                        after(dve, dve.copy_predicated(FIN[:, 0, :], MASK[:, n, :], FIN[:, 1 + n, :]))
                    dve.tensor_tensor(X[:, c], X[:, c], FIN[:, 0, :], ALU.add).then_inc(x_final, 1)

                for n in range(1, NU, 2):
                    e, m, bp, bh = UNITS[n]
                    dve.wait_ge(hid_ps, n + 1)
                    if n >= 4:
                        dve.wait_ge(hid_used, n - 3)
                    dve.tensor_scalar(HID[:, n % 4, :], bank(2 + n % 4), wt("b1_3", 2 * e + m, 1), 0.0, ALU.add, ALU.max).then_inc(hid_in_v, 1)
                    if n == NU // 2 + 9:
                        finish(0)
                finish(1)



def pack_weights(v):
    packs = [np.zeros((P, w), np.float32) for w in WIDTH]

    def put(name, a, p0=0, at=0):
        a = np.asarray(a)
        a = a.reshape(a.shape[0], -1)
        s, c0, cols = AT[name]
        assert at + a.shape[1] <= cols, name
        packs[s][p0:p0 + a.shape[0], c0 + at:c0 + at + a.shape[1]] = a

    def twice(name, a, at=0):
        a = np.asarray(a)
        put(name, a.reshape(a.shape[0], -1), 0, at)
        put(name, a.reshape(a.shape[0], -1), 64, at)

    def diag2(name, a, at=0, width=None):
        width = width or a.shape[1]
        put(name, a, 0, at)
        put(name, a, 64 if a.shape[0] == 64 else a.shape[0], at + width)

    def rows(name, a, at=0):
        put(name, np.broadcast_to(np.asarray(a).reshape(1, -1), (P, np.asarray(a).size)), 0, at)

    f = np.float32
    eye = np.eye(P, dtype=f)
    blocks = np.kron(np.eye(2, dtype=f), np.ones((C, C), f))
    put("ident", eye)
    put("center", eye - blocks / C)
    put("mean32", np.kron(np.eye(2, dtype=f), np.full((C, 16), 1.0 / C, f)))
    for q in range(4):
        for bh in range(2):
            put("spread", np.ones((1, C), f), 32 * q + 16 * bh, q * P + C * bh)
    put("epsc", np.full((P, 1), 1e-6, f))
    put("epst", np.full((P, 1), 1e-5, f))
    put("epsa", np.full((P, 1), 1e-15, f))
    put("epsb", np.full((P, 1), 1e-3, f))

    ch = [np.array([g * 24 + j * HD + e for g in range(8) for e in range(HD)]) for j in range(3)]
    qkv_w = v["L0_conv_qkv_w"][:, :, 0, 0]
    for j in range(3):
        diag2("wq3", qkv_w[ch[j]].T, j * P)
        twice("bq3", v["L0_conv_qkv_b"][ch[j]][:, None], j)
        for k in ("3", "5"):
            w = v[f"L0_conv_dw{k}_w"][ch[j], 0]
            twice("dw" + k, w.reshape(C, -1), j * w.shape[1] * w.shape[2])
            twice("db" + k, v[f"L0_conv_dw{k}_b"][ch[j]][:, None], j)
    for i in range(2):
        diag2("wkv", qkv_w[ch[1 + i]].T, i * P)
    for s, (w, b) in enumerate((("qkv_w", "qkv_b"), ("pw3_w", "pw3_b"), ("pw5_w", "pw5_b"))):
        b = v["L0_conv_" + b]
        rows("bkv", np.concatenate([b[ch[1]], b[ch[1]], b[ch[2]], b[ch[2]]]), s * 2 * P)
        twice("bqq", b[ch[0]][:, None], s)
        if s == 0:
            continue
        pw = v["L0_conv_" + w][:, :, 0, 0]
        for j in range(3):
            m = np.zeros((3, C, C), f)
            for o in range(3):
                for g in range(8):
                    m[o, g * HD:(g + 1) * HD, g * HD:(g + 1) * HD] = pw[g * 24 + o * HD:g * 24 + (o + 1) * HD,
                                                                        j * HD:(j + 1) * HD].T
            diag2("pwq", m[0], ((s - 1) * 3 + j) * P)
            for i in range(2):
                diag2("pwkv", m[1 + i], (2 * ((s - 1) * 3 + j) + i) * P)
    for s in range(SCALES):
        diag2("proj", v["L0_conv_proj_w"][:, s * C:(s + 1) * C, 0, 0].T, s * P)
    twice("bproj", v["L0_conv_proj_b"][:, None])
    heads = np.kron(np.eye(2 * E, dtype=f), np.ones((HD, 1), f))
    put("headmask", np.concatenate([heads, heads], 1))
    for bl in range(NB):
        put("headspread", heads.T, 32 * bl, bl * P)
    put("vkmask", np.kron(np.eye(16, dtype=f), np.ones((HD, HD), f)))

    diag2("gate0", v["L0_ffn_gate_w"])
    rows("gb0", v["L0_ffn_gate_b"])
    rows("rev", np.arange(E, 0, -1).astype(f))
    for e in range(E):
        diag2("w1_0", v["L0_ffn_W1"][e], e * 2 * FH0)
    put("b1_0", v["L0_ffn_b1"].T)
    for e in range(E):
        put("w2_0", v["L0_ffn_W2"][e], 0, e * C)
    put("b2_0", v["L0_ffn_b2"])
    put("sel24", np.tile(np.eye(E, dtype=f), (3, 1)))

    c1, c2 = v["L1_conv_w1"], v["L1_conv_w2"]
    order = np.array([(s * 2 + xy) for xy in range(2) for s in range(SAMPLES)])
    for m in range(9):
        diag2("c1w", c1[:, :, m // 3, m % 3].T, m * P)
        diag2("c2w", c2[order][:, :, m // 3, m % 3].T, m * 144)
    twice("c1b", v["L1_conv_b1"][:, None])
    rows("c2b", v["L1_conv_b2"][order])
    pix = np.arange(P)
    tap = np.arange(SAMPLES) % 9
    for h in range(2):
        py = (pix // W + h * H // 2)[:, None] + (tap // 3 - 1)[None]
        px = (pix % W)[:, None] + (tap % 3 - 1)[None]
        put("pos", np.concatenate([py, px], 1).astype(f), 0, h * 72)
        put("qidx", (pix + h * P)[:, None].astype(f), 0, h)
    wd = v["L1_conv_wd"].reshape(C, 4, CG, 9).transpose(1, 3, 2, 0).reshape(SAMPLES * CG, C)
    for n in range(5):
        put("wd", wd[n * P:(n + 1) * P], 0, n * C)

    diag2("wr1", v["L1_ffn_wr"])
    rows("br1", v["L1_ffn_br"])
    for h in range(2):
        put("before1", (np.arange(PIX)[None] < (pix + h * P)[:, None]).astype(f), 0, h * PIX)
    diag2("w1_1", v["L1_ffn_w1"])
    put("b1_1", v["L1_ffn_b1"].reshape(2, P).T)
    for m in range(2):
        put("w2_1", v["L1_ffn_w2"][m * P:(m + 1) * P], 0, m * C)
    twice("b2_1", v["L1_ffn_b2"][:, None])
    put("ones", np.ones((P, P), f))

    for k in range(4):
        diag2("ssw", v["L2_conv_weight"][k * C:(k + 1) * C].T, k * P)
        twice("ssb", v["L2_conv_bias"][k * C:(k + 1) * C, None], k)

    twice("wr2", v["L2_ffn_Wr"])
    rows("br2", v["L2_ffn_br"])
    for e in range(E):
        diag2("w1_2", v["L2_ffn_W1"][e], e * P)
        diag2("w2_2", v["L2_ffn_W2"][e], e * P)
        diag2("wo_2", v["L2_ffn_Wo"][e], e * P)
    for n in (1, 2):
        for i, name in enumerate(("b", "g", "be", "m", "v")):
            twice(f"bn{n}", v[f"L2_ffn_{name}{n}"].T, i * E)
    put("bo2", np.concatenate([v["L2_ffn_bo"], v["L2_ffn_bo"]], 1))

    twice("dwi", v["L3_conv_w_in"].reshape(C, 9))
    twice("dbi", v["L3_conv_b_in"][:, None])
    diag2("red", v["L3_conv_w_red"].T, 0)
    put("bred", v["L3_conv_b_red"][:, None], 0)
    put("bred", v["L3_conv_b_red"][:, None], 16)
    for k in range(9):
        a = np.broadcast_to(v["L3_conv_w_span"][k][:, None], (16, C))
        put("span", a, 0, k * P)
        put("span", a, 16, k * P + C)
        put("span", np.broadcast_to(v["L3_conv_b_span"][k:k + 1, None], (1, P)), 32, k * P)
    twice("dwo", v["L3_conv_w_out"].reshape(C, 9))
    twice("dbo", v["L3_conv_b_out"][:, None])

    diag2("gate3", v["L3_ffn_gate_w"])
    rows("gb3", v["L3_ffn_gate_b"])
    put("tri", np.triu(np.ones((P, P), f)))
    put("w1_3", v["L3_ffn_w1"].transpose(1, 0, 2))
    for e in range(E):
        put("w1_3", np.full((1, FH3), -BIG, f), C + e, e * FH3)
        for m in range(2):
            put("b1_3", v["L3_ffn_b1"][e, m * P:(m + 1) * P, None], 0, 2 * e + m)
            put("w2_3", v["L3_ffn_w2"][e, m * P:(m + 1) * P], 0, (2 * e + m) * C)
    put("b2_3", v["L3_ffn_b2"])
    return packs


def kernel(**inputs):
    import concourse.bacc as bacc
    from concourse.bass_utils import run_bass_kernel_spmd

    v = {k: np.asarray(a) for k, a in inputs.items()}
    nc = bacc.Bacc("TRN2", target_bir_lowering=False, num_devices=1)
    arrays = {"x_dram": np.ascontiguousarray(v["x"]).reshape(B, C, PIX)}
    x_dram = nc.dram_tensor("x_dram", (B, C, PIX), F32, kind="ExternalInput").ap()
    packs = []
    for n, a in enumerate(pack_weights(v)):
        arrays[f"pack{n}_dram"] = a
        packs.append(nc.dram_tensor(f"pack{n}_dram", a.shape, F32, kind="ExternalInput").ap())
    out = nc.dram_tensor("out_dram", (B, C, PIX), F32, kind="ExternalOutput").ap()
    idx_dram = nc.dram_tensor("idx_dram", (SAMPLES, TILES * P), FP16, kind="Internal").ap()
    build(nc, x_dram, packs, idx_dram, out)
    r = run_bass_kernel_spmd(nc, [arrays], core_ids=[0])
    return r.results[0]["out_dram"].reshape(B, C, H, W)
```

```python
from contextlib import ExitStack

import concourse.bass as bass
import numpy as np
from concourse import mybir

ALU = mybir.AluOpType
ACT = mybir.ActivationFunctionType
F32 = mybir.dt.float32
BF16 = mybir.dt.bfloat16
FP16 = mybir.dt.float16
I32 = mybir.dt.int32
AX = mybir.AxisListType

P = 128
B, C, H, W = 8, 64, 16, 16
NB = B // 2
PIX = H * W
COLS = NB * PIX
HC = COLS // 2
TILES = B * PIX // P
PITCH, PW = H + 2, W + 4
PROWS = 2 + NB * PITCH
AROWS = (NB - 1) * PITCH + H
E = 8
HD = 8
SCALES = 3
SAMPLES = 36
CG = 16
FH0, FH1, FH3 = 128, 256, 256
CAP = -(-5 * B * PIX // (4 * E))
TOPK = PIX // 2 - 1
GSCALE = 4096.0
BIG = 1.0e30

SECTIONS = [
    [("center", P), ("mean32", 32), ("spread", 4 * P), ("ident", P), ("ones", P), ("rev", E), ("epsc", 1), ("epst", 1), ("epsa", 1), ("epsb", 1)],
    [("wq3", 3 * P), ("bq3", 3), ("wkv", 2 * P), ("bkv", SCALES * 2 * P), ("dw5", 75), ("db5", 3), ("dw3", 27), ("db3", 3),
     ("pwq", 6 * P), ("bqq", 3), ("pwkv", 12 * P), ("proj", 3 * P), ("bproj", 1), ("vkmask", P), ("headmask", 32), ("headspread", 4 * P)],
    [("gate0", 2 * E), ("gb0", E), ("w1_0", E * 2 * FH0), ("b1_0", E), ("w2_0", E * C), ("b2_0", C),
     ("sel24", E)],
    [("c1w", 9 * P), ("c1b", 1), ("c2w", 9 * 144), ("c2b", 72), ("pos", 2 * 72),
     ("qidx", 2), ("negq1", 1), ("wd", 5 * C)],
    [("wr1", 2), ("br1", 1), ("before1", 2 * PIX), ("w1_1", 2 * FH1), ("b1_1", 2), ("w2_1", 2 * C), ("b2_1", 1)],
    [("ssw", 4 * P), ("ssb", 4)],
    [("wr2", E), ("br2", E), ("w1_2", E * P), ("w2_2", E * P), ("wo_2", E * P), ("bn1", 5 * E),
     ("bn2", 5 * E), ("bo2", P)],
    [("dwi", 9), ("dbi", 1), ("red", 32), ("bred", 1), ("span", 9 * P), ("dwo", 9), ("dbo", 1)],
    [("gate3", 2 * E), ("gb3", E), ("tri", P), ("w1_3", E * FH3), ("drop", E), ("b1_3", E * 2), ("w2_3", E * 2 * C), ("b2_3", C)],
]
AT = {}
WIDTH = []
for _n, _s in enumerate(SECTIONS):
    _at = 0
    for _name, _cols in _s:
        AT[_name] = (_n, _at, _cols)
        _at += _cols
    WIDTH.append(_at)


def build(nc, x_dram, packs, idx_dram, out_dram):
    with ExitStack() as ctx:
        def sb(name, shape, dt=F32, where=None):
            return (where or ctx).enter_context(nc.sbuf_tensor(name, shape, dt))

        def sem(name):
            return ctx.enter_context(nc.semaphore(name))

        X = sb("X", [P, COLS])
        Y = sb("Y", [P, COLS])
        SQ = sb("SQ", [P, COLS])
        SD = sb("SD", [P, COLS])
        wconst = sb("wconst", [P, WIDTH[0]])
        wbuf = [sb(f"wbuf{i}", [P, max(w for n, w in enumerate(WIDTH) if n and n % 2 == i)]) for i in range(2)]
        wsb = [wconst if n == 0 else wbuf[n % 2] for n in range(len(SECTIONS))]
        PS = ctx.enter_context(nc.psum_tensor("PS", [P, 8 * 512], F32))

        def bank(n, cols=512):
            return PS[:, n * 512:n * 512 + cols]

        def wt(name, a=0, n=None, p0=0, p1=P):
            s, at, cols = AT[name]
            n = cols - a if n is None else n
            return wsb[s][p0:p1, at + a:at + a + n]

        x_in = sem("x_in")
        w_in = [sem(f"w_in{n}") for n in range(len(SECTIONS))]
        stored = sem("stored")
        ln_centered, ln_squared, ln_var, ln_sd, ln_rstd, ln_spread, ln_placed, ln_done = (sem(n) for n in (
            "ln_centered", "ln_squared", "ln_var", "ln_sd", "ln_rstd", "ln_spread", "ln_placed", "ln_done"))
        dve_step = sem("dve_step")
        act_step = sem("act_step")
        pool_step = sem("pool_step")
        steps = {"dve": 0, "act": 0, "pool": 0}

        def load_weights(sp, n):
            sp.dma_start(wsb[n][:, 0:WIDTH[n]], packs[n]).then_inc(w_in[n], 16)

        def after(eng, ins):
            steps["dve"] += 1
            ins.then_inc(dve_step, 1)
            eng.wait_ge(dve_step, steps["dve"])

        def after_act(eng, ins):
            steps["act"] += 1
            ins.then_inc(act_step, 1)
            eng.wait_ge(act_step, steps["act"])

        def after_pool(eng, ins):
            steps["pool"] += 1
            ins.then_inc(pool_step, 1)
            eng.wait_ge(pool_step, steps["pool"])

        WARM = sb("WARM", [P, 32])
        warmed = [0]

        def warm(act, func):
            k = warmed[0]
            warmed[0] += 1
            act.activation(WARM[:, k:k + 1], wt("epsc"), func)

        def ln_pe(pe, n):
            for h in range(2):
                pe.matmul(bank(h), wt("center"), X[:, h * HC:(h + 1) * HC], start=True, stop=True).then_inc(ln_centered, 1)
            for h in range(2):
                pe.wait_ge(ln_squared, 2 * n + h + 1)
                for q in range(4):
                    mm = pe.matmul(bank(2 + h, P)[32 * q:32 * q + 32, :], wt("mean32"), SQ[:, h * HC + q * P:h * HC + (q + 1) * P],
                                   start=True, stop=True, tile_position=(0, 32 * q))
                mm.then_inc(ln_var, 1)
            for h in range(2):
                pe.wait_ge(ln_rstd, 2 * n + h + 1)
                for q in range(4):
                    mm = pe.matmul(bank(2 + h)[:, q * P:(q + 1) * P], wt("spread", q * P, P), SD[:, h * P:(h + 1) * P],
                                   start=True, stop=True)
                mm.then_inc(ln_spread, 1)

        def ln_act(act, n, eps):
            if n == 0:
                warm(act, ACT.Sqrt)
            for h in range(2):
                act.wait_ge(ln_centered, 2 * n + h + 1)
                act.activation(SQ[:, h * HC:(h + 1) * HC], bank(h), ACT.Square).then_inc(ln_squared, 1)
            for h in range(2):
                act.wait_ge(ln_var, 2 * n + h + 1)
                act.activation(SD[:, h * P:(h + 1) * P], bank(2 + h, P), ACT.Sqrt, bias=wt(eps)).then_inc(ln_sd, 1)

        def ln_dve(dve, n, out_of):
            for h in range(2):
                o, view = out_of(h)
                dve.wait_ge(ln_squared, 2 * n + h + 1)
                dve.tensor_copy(o, view(bank(h))).then_inc(ln_placed, 1)
            for h in range(2):
                c = slice(h * P, (h + 1) * P)
                dve.wait_ge(ln_sd, 2 * n + h + 1)
                dve.reciprocal(SD[:, c], SD[:, c]).then_inc(ln_rstd, 1)
            for h in range(2):
                o, view = out_of(h)
                dve.wait_ge(ln_placed, 2 * n + h + 1)
                dve.wait_ge(ln_spread, 2 * n + h + 1)
                dve.tensor_tensor(o, o, view(bank(2 + h)), ALU.mult).then_inc(ln_done, 1)

        def flat(h):
            return Y[:, h * HC:(h + 1) * HC], lambda a: a

        def images(a):
            return a.rearrange("p (b r w) -> p b r w", b=2, r=H)

        def pair(pad, h, dy, dx):
            r0 = 2 * h * PITCH + dy
            if r0 + 2 * PITCH <= PROWS:
                v = pad[:, r0:r0 + 2 * PITCH, dx:dx + W].rearrange("p (b r) w -> p b r w", b=2)
                return v[:, :, 0:H, :]
            v = pad[:, r0 - (PITCH - H):r0 + 2 * PITCH - (PITCH - H), dx:dx + W].rearrange("p (b r) w -> p b r w", b=2)
            return v[:, :, PITCH - H:PITCH, :]

        def acc_images(acc, h):
            r0 = 2 * h * PITCH
            if r0 + 2 * PITCH <= AROWS:
                return acc[:, r0:r0 + 2 * PITCH, :].rearrange("p (b r) w -> p b r w", b=2)[:, :, 0:H, :]
            r0 -= PITCH - H
            return acc[:, r0:r0 + 2 * PITCH, :].rearrange("p (b r) w -> p b r w", b=2)[:, :, PITCH - H:PITCH, :]

        with ExitStack() as sctx, nc.Block() as block:
            QKVP = [sb(f"QKVP{j}", [P, PROWS, PW], F32, sctx) for j in range(3)]
            D5 = [sb(f"D5_{j}", [P, AROWS, W], F32, sctx) for j in range(3)]
            D3 = [sb(f"D3_{j}", [P, COLS], F32, sctx) for j in range(3)]
            QR = [sb(f"QR{s}", [P, COLS], F32, sctx) for s in range(SCALES)]
            ATT = [sb(f"ATT{s}", [P, COLS], F32, sctx) for s in range(SCALES)]
            KV = sb("KV", [P, SCALES, NB, 2, 257], F32, sctx)
            VK = sb("VK", [P, SCALES, NB, P], F32, sctx)
            KSUM = sb("KSUM", [P, SCALES, NB, 32], F32, sctx)
            DG = sb("DG", [P, 33, P], F32, sctx)
            RD = sb("RD", [P, PIX], F32, sctx)
            TAP = [sb(f"TAP{i}", [P, AROWS, W], F32, sctx) for i in range(2)]
            D5B = [sb(f"D5B{i}", [P, AROWS, W], F32, sctx) for i in range(2)]
            padded, diag, ones_set, qkv_in, kv_ps, kv_biased, kv_ready, dw3_ps, d3_ready, d5_ready = (sem(n) for n in (
                "padded", "diag", "ones_set", "qkv_in", "kv_ps", "kv_biased", "kv_ready", "dw3_ps", "d3_ready", "d5_ready"))
            qkv_ps, q_ps, q_ready, vk_ps, vk_ready, den_ps, den_out, den_inv, num_ps, num_out, inv_ps, att_ready, proj_ps = (
                sem(n) for n in ("qkv_ps", "q_ps", "q_ready", "vk_ps", "vk_ready", "den_ps", "den_out", "den_inv", "num_ps",
                                 "num_out", "inv_ps", "att_ready", "proj_ps"))
            tap_ready, tap_used, d5a_ready = sem("tap_ready"), sem("tap_used"), sem("d5a_ready")
            VTAPS, PTAPS = (17, 17, 13), (0, 0, 6)
            GTAPS = [25 - v - p for v, p in zip(VTAPS, PTAPS)]
            ADDS = [g - 1 + (p > 0) for g, p in zip(GTAPS, PTAPS)]
            D3_AT = 6
            tensor_taps = sem("tensor_taps")

            @block.sync
            def _(sp):
                xv = x_dram.rearrange("(g b) c p -> g c b p", g=2)
                for g in range(2):
                    sp.dma_start(X[C * g:C * g + C, :].rearrange("c (b p) -> c b p", b=NB), xv[g]).then_inc(x_in, 16)
                for n in range(3):
                    load_weights(sp, n)

            @block.gpsimd
            def _(pool):
                for j in range(3):
                    pool.memset(QKVP[j][:, :, :], 0.0).then_inc(padded, 1)
                pool.memset(KV[:, :, :, :, 256:257], 1.0).then_inc(ones_set, 1)

                def keys(s):
                    for g in range(NB):
                        pool.wait_ge(kv_biased, 4 * s + g + 1)
                        k = KV[:, s, g, :, 0:P]
                        pool.tensor_scalar(k, k, 0.0, None, ALU.max).then_inc(kv_ready, 1)

                def join(j):
                    pool.wait_ge(d5a_ready, j + 1)
                    pool.tensor_tensor(D5[j][:, :, :], D5[j][:, :, :], D5B[j % 2][:, :, :], ALU.add).then_inc(d5_ready, 1)

                keys(0)
                for j in range(3):
                    for i in range(1, ADDS[j] + 1):
                        n = sum(ADDS[:j]) + i
                        pool.wait_ge(tap_ready, n + j + 1)
                        pool.tensor_tensor(D5B[j % 2][:, :, :], D5B[j % 2][:, :, :], TAP[n % 2][:, :, :], ALU.add).then_inc(tap_used, 1)
                        pool.wait_ge(tap_used, n)
                    if j >= 1:
                        join(j - 1)
                join(2)
                keys(1)
                keys(2)

            @block.tensor
            def _(pe):
                pe.wait_ge(x_in, 32)
                pe.wait_ge(w_in[0], 16)
                ln_pe(pe, 0)
                pe.wait_ge(w_in[1], 16)
                qbank = [4, 5, 6, 7, 2, 3]
                for j in range(3):
                    for h in range(2):
                        if j == 0 or (j, h) == (2, 0):
                            pe.wait_ge(ln_done, 2 if j else h + 1)
                        pe.matmul(bank(qbank[2 * j + h]), wt("wq3", j * P, P), Y[:, h * HC:(h + 1) * HC],
                                  start=True, stop=True).then_inc(qkv_ps, 1)

                def kv_group(s, g):
                    n = 4 * s + g
                    if n >= 2:
                        pe.wait_ge(kv_biased, n - 1)
                    for i in range(2):
                        r = 2 * g + i
                        cc = slice(r * P, (r + 1) * P)
                        o = bank(n % 2)[:, i * 2 * P:(i + 1) * 2 * P]
                        if s == 0:
                            mm = pe.matmul(o, Y[:, cc], wt("wkv"), start=True, stop=True)
                        else:
                            for j in range(3):
                                r0 = g * PITCH + i * (H // 2)
                                src = D3[j][:, cc] if s == 1 else D5[j][:, r0:r0 + H // 2, :].rearrange("p r w -> p (r w)")
                                mm = pe.matmul(o, src, wt("pwkv", ((s - 1) * 3 + j) * 2 * P, 2 * P),
                                               start=(j == 0), stop=(j == 2))
                    mm.then_inc(kv_ps, 1)

                def vk(s):
                    pe.wait_ge(kv_ready, 4 * s + 4)
                    if s == 0:
                        pe.wait_ge(ones_set, 1)
                    for bp in range(2):
                        n = 2 * s + bp
                        if n >= 2:
                            pe.wait_ge(vk_ready, n - 1)
                            if bp == 1:
                                pe.wait_ge(den_out, s)
                        for i in range(2):
                            for half in range(2):
                                kv = KV[:, s, 2 * bp + i, half, :]
                                mm = pe.matmul(bank(6 + n % 2)[:, i * 129:(i + 1) * 129], kv[:, 0:P], kv[:, P:257],
                                               start=(half == 0), stop=(half == 1))
                        mm.then_inc(vk_ps, 1)

                def den(s):
                    pe.wait_ge(vk_ready, 2 * s + 2)
                    pe.wait_ge(q_ready, 2 * s + 2)
                    for bl in range(NB):
                        mm = pe.matmul(bank(7, PIX)[32 * bl:32 * bl + 32, :], KSUM[:, s, bl, :], QR[s][:, bl * PIX:(bl + 1) * PIX],
                                       start=True, stop=True, tile_position=(0, 32 * bl))
                    mm.then_inc(den_ps, 1)

                def attend(s):
                    for bp in range(2):
                        n = 2 * s + bp
                        if n >= 1:
                            pe.wait_ge(num_out, n)
                        for i in range(2):
                            bl = 2 * bp + i
                            mm = pe.matmul(bank(2)[:, i * PIX:(i + 1) * PIX], VK[:, s, bl, :],
                                           QR[s][:, bl * PIX:(bl + 1) * PIX], start=True, stop=True)
                        mm.then_inc(num_ps, 1)
                        pe.wait_ge(den_inv, s + 1)
                        if n >= 1:
                            pe.wait_ge(att_ready, n)
                        for i in range(2):
                            bl = 2 * bp + i
                            mm = pe.matmul(bank(3)[:, i * PIX:(i + 1) * PIX], wt("headspread", bl * P, P), RD[:, :],
                                           start=True, stop=True)
                        mm.then_inc(inv_ps, 1)

                def queries(s):
                    for h in range(2):
                        if s == 2:
                            pe.wait_ge(q_ready, 3 + h)
                        for j in range(3):
                            src = D3[j][:, h * HC:(h + 1) * HC] if s == 1 else acc_images(D5[j], h)
                            mm = pe.matmul(bank(4 + h), wt("pwq", ((s - 1) * 3 + j) * P, P), src,
                                           start=(j == 0), stop=(j == 2))
                        mm.then_inc(q_ps, 1)

                for g in range(4):
                    kv_group(0, g)
                pe.wait_ge(qkv_in, 6)
                pe.wait_ge(diag, 27)
                for j in range(3):
                    for h in range(2):
                        for m in range(9):
                            mm = pe.matmul(bank(qbank[2 * j + h]), DG[:, j * 9 + m, :],
                                           pair(QKVP[j], h, 1 + m // 3, 1 + m % 3), start=(m == 0), stop=(m == 8))
                        mm.then_inc(dw3_ps, 1)
                pe.wait_ge(d3_ready, 2)
                pe.wait_ge(diag, 27 + PTAPS[2])
                for h in range(2):
                    for i in range(PTAPS[2]):
                        m = VTAPS[2] + i
                        mm = pe.matmul(bank(4 + h), DG[:, 27 + i, :], pair(QKVP[2], h, m // 5, m % 5),
                                       start=(i == 0), stop=(i == PTAPS[2] - 1))
                    mm.then_inc(tensor_taps, 1)
                pe.wait_ge(d3_ready, 6)
                vk(0)
                pe.wait_ge(tap_ready, sum(ADDS) + 3)
                queries(1)
                for g in range(4):
                    kv_group(1, g)
                den(0)
                pe.wait_ge(d5_ready, 3)
                queries(2)
                for g in range(4):
                    kv_group(2, g)
                attend(0)
                vk(1)
                den(1)
                vk(2)
                attend(1)
                den(2)
                attend(2)
                pe.wait_ge(att_ready, 2 * SCALES)
                for h in range(2):
                    for s in range(SCALES):
                        mm = pe.matmul(bank(h), wt("proj", s * P, P), ATT[s][:, h * HC:(h + 1) * HC],
                                       start=(s == 0), stop=(s == SCALES - 1))
                    mm.then_inc(proj_ps, 1)

            @block.scalar
            def _(act):
                qbank = [4, 5, 6, 7, 2, 3]
                act.wait_ge(w_in[0], 16)
                ln_act(act, 0, "epsc")
                act.wait_ge(w_in[1], 16)
                act.wait_ge(padded, 3)
                for j in range(3):
                    for h in range(2):
                        act.wait_ge(qkv_ps, 2 * j + h + 1)
                        src = bank(qbank[2 * j + h])
                        if j == 0:
                            act.activation(QR[0][:, h * HC:(h + 1) * HC], src, ACT.Relu, bias=wt("bqq", 0, 1)).then_inc(q_ready, 1)
                        act.activation(pair(QKVP[j], h, 2, 2), images(src), ACT.Identity, bias=wt("bq3", j, 1)).then_inc(qkv_in, 1)

                def convolved(j):
                    for h in range(2):
                        act.wait_ge(dw3_ps, 2 * j + h + 1)
                        act.activation(D3[j][:, h * HC:(h + 1) * HC], bank(qbank[2 * j + h]), ACT.Identity,
                                       bias=wt("db3", j, 1)).then_inc(d3_ready, 1)

                for j in range(3):
                    act.wait_ge(qkv_in, 2 * j + 2)
                    for i in range(ADDS[j] + 1):
                        n = sum(ADDS[:j]) + i
                        if i == D3_AT:
                            convolved(j)
                        if i == GTAPS[j]:
                            for h in range(2):
                                act.wait_ge(tensor_taps, h + 1)
                                if n > 2 and h == 0:
                                    act.wait_ge(tap_used, n - 2)
                                ins = act.activation(acc_images(TAP[n % 2], h), images(bank(4 + h)), ACT.Copy)
                            ins.then_inc(tap_ready, 1)
                            continue
                        m = VTAPS[j] + PTAPS[j] + i
                        src = QKVP[j][:, m // 5:m // 5 + AROWS, m % 5:m % 5 + W]
                        if i == 0:
                            if j >= 2:
                                act.wait_ge(d5_ready, j - 1)
                            act.activation(D5B[j % 2][:, :, :], src, ACT.Identity, bias=wt("db5", j, 1), scale=wt("dw5", j * 25 + m, 1)).then_inc(tap_ready, 1)
                            continue
                        if n > 2:
                            act.wait_ge(tap_used, n - 2)
                        act.activation(TAP[n % 2][:, :, :], src, ACT.Copy, scale=wt("dw5", j * 25 + m, 1)).then_inc(tap_ready, 1)

                def queries(s):
                    for h in range(2):
                        act.wait_ge(q_ps, 2 * (s - 1) + h + 1)
                        act.activation(QR[s][:, h * HC:(h + 1) * HC], bank(4 + h), ACT.Relu, bias=wt("bqq", s, 1)).then_inc(q_ready, 1)

                def den(s):
                    act.wait_ge(den_ps, s + 1)
                    if s >= 1:
                        act.wait_ge(inv_ps, 2 * s)
                    act.activation(RD[:, :], bank(7, PIX), ACT.Identity, bias=wt("epsa")).then_inc(den_out, 1)

                def numerators(s):
                    for bp in range(2):
                        n = 2 * s + bp
                        act.wait_ge(num_ps, n + 1)
                        act.activation(ATT[s][:, bp * HC:(bp + 1) * HC], bank(2), ACT.Copy).then_inc(num_out, 1)

                queries(1)
                den(0)
                queries(2)
                numerators(0)
                den(1)
                numerators(1)
                den(2)
                numerators(2)
                warm(act, ACT.Sqrt)

            @block.vector
            def _(dve):
                dve.wait_ge(w_in[0], 16)
                ln_dve(dve, 0, flat)
                dve.wait_ge(w_in[1], 16)

                def kv_bias(s):
                    for g in range(NB):
                        n = 4 * s + g
                        dve.wait_ge(kv_ps, n + 1)
                        bias = wt("bkv", s * 2 * P, 2 * P).rearrange("p (o c) -> p o c", o=1).broadcast_to([P, 2, 2 * P])
                        dve.tensor_tensor(KV[:, s, g, :, 0:2 * P], bank(n % 2).rearrange("p (t c) -> p t c", t=2), bias,
                                          ALU.add).then_inc(kv_biased, 1)

                def mask_vk(s):
                    for bp in range(2):
                        n = 2 * s + bp
                        dve.wait_ge(vk_ps, n + 1)
                        for i in range(2):
                            ps = bank(6 + n % 2)[:, i * 129:(i + 1) * 129]
                            dve.tensor_tensor(VK[:, s, 2 * bp + i, :], ps[:, 0:P], wt("vkmask"), ALU.mult)
                            ins = dve.tensor_scalar(KSUM[:, s, 2 * bp + i, :], wt("headmask"), ps[:, P:P + 1], None, ALU.mult)
                        ins.then_inc(vk_ready, 1)

                def invert(s):
                    dve.wait_ge(den_out, s + 1)
                    dve.reciprocal(RD[:, :], RD[:, :]).then_inc(den_inv, 1)

                def divide(s):
                    for bp in range(2):
                        n = 2 * s + bp
                        a = ATT[s][:, bp * HC:(bp + 1) * HC]
                        dve.wait_ge(num_out, n + 1)
                        dve.wait_ge(inv_ps, n + 1)
                        dve.tensor_tensor(a, a, bank(3), ALU.mult).then_inc(att_ready, 1)

                def depthwise5(j):
                    for m in range(VTAPS[j]):
                        src = QKVP[j][:, m // 5:m // 5 + AROWS, m % 5:m % 5 + W]
                        w = wt("dw5", j * 25 + m, 1)
                        if m == 0:
                            after(dve, dve.tensor_scalar(D5[j][:, :, :], src, w, None, ALU.mult))
                        else:
                            ins = dve.scalar_tensor_tensor(out=D5[j][:, :, :], in0=src, scalar=w, in1=D5[j][:, :, :],
                                                           op0=ALU.mult, op1=ALU.add)
                            if m < VTAPS[j] - 1:
                                after(dve, ins)
                            else:
                                ins.then_inc(d5a_ready, 1)

                for m in range(27 + PTAPS[2]):
                    w = wt("dw3", m, 1) if m < 27 else wt("dw5", 50 + VTAPS[2] + m - 27, 1)
                    dve.tensor_scalar(DG[:, m, :], wt("ident"), w, None, ALU.mult).then_inc(diag, 1)
                kv_bias(0)
                dve.wait_ge(qkv_in, 6)
                for j in range(3):
                    depthwise5(j)
                mask_vk(0)
                kv_bias(1)
                invert(0)
                kv_bias(2)
                divide(0)
                mask_vk(1)
                invert(1)
                mask_vk(2)
                divide(1)
                invert(2)
                divide(2)
                for h in range(2):
                    c = slice(h * HC, (h + 1) * HC)
                    dve.wait_ge(proj_ps, h + 1)
                    dve.scalar_tensor_tensor(out=X[:, c], in0=bank(h), scalar=wt("bproj"), in1=X[:, c],
                                             op0=ALU.add, op1=ALU.add)

        def softmax_dve(dve, LG, RED, n, exps, k, summed):
            mx = RED[:, 0:n].rearrange("p (t o) -> p t o", o=1)
            after(dve, dve.tensor_reduce(RED[:, 0:n], LG[:, :, :], AX.X, ALU.max))
            dve.tensor_tensor(LG[:, :, :], LG[:, :, :], mx.broadcast_to([P, n, E]), ALU.subtract).then_inc(exps, 1)
            dve.wait_ge(summed, k)
            after(dve, dve.tensor_reduce(RED[:, 0:n], LG[:, :, :], AX.X, ALU.add))
            after(dve, dve.reciprocal(RED[:, 0:n], RED[:, 0:n]))
            after(dve, dve.tensor_tensor(LG[:, :, :], LG[:, :, :], mx.broadcast_to([P, n, E]), ALU.mult))

        def diagonals(dve, DIAG, col, q):
            ident = wt("ident").rearrange("p (o c) -> p o c", o=1).broadcast_to([P, 4, P])
            values = col[:, 4 * q:4 * q + 4].rearrange("p (t o) -> p t o", o=1).broadcast_to([P, 4, P])
            return dve.tensor_tensor(DIAG[:, 4 * q:4 * q + 4, :], ident, values, ALU.mult)

        def first_max_dve(dve, V, KEY, RED, OUT):
            mx = RED[:, 0:TILES].rearrange("p (t o) -> p t o", o=1).broadcast_to([P, TILES, E])
            rev = wt("rev").rearrange("p (o e) -> p o e", o=1).broadcast_to([P, TILES, E])
            after(dve, dve.tensor_reduce(RED[:, 0:TILES], V[:, :, :], AX.X, ALU.max))
            after(dve, dve.tensor_tensor(KEY[:, :, :], V[:, :, :], mx, ALU.is_equal))
            after(dve, dve.tensor_tensor(KEY[:, :, :], KEY[:, :, :], rev, ALU.mult))
            after(dve, dve.tensor_reduce(RED[:, 0:TILES], KEY[:, :, :], AX.X, ALU.max))
            after(dve, dve.tensor_tensor(OUT[:, :, :], KEY[:, :, :], mx, ALU.is_equal))

        with ExitStack() as sctx, nc.Block() as block:
            LG = sb("LG", [P, TILES, E], F32, sctx)
            RED = sb("RED", [P, TILES], F32, sctx)
            KEY, FIRST, REST, SECOND, CHOSEN = (sb(n, [P, TILES, E], F32, sctx) for n in ("KEY", "FIRST", "REST", "SECOND", "CHOSEN"))
            CW3 = sb("CW3", [P, TILES, 3, E], BF16, sctx)
            CWT = sb("CWT", [P, TILES * P], F32, sctx)
            CWT3 = sb("CWT3", [P, TILES * P], BF16, sctx)
            SELB = sb("SELB", [P, E * P], BF16, sctx)
            IDB = sb("IDB", [P, P], BF16, sctx)
            AHEAD, HBUF = 8, 8
            HID = sb("HID", [P, HBUF, HC], F32, sctx)
            HS = sb("HS", [P, 4, HC], F32, sctx)
            g_ps, g_exp, g_sum, cw_ready, cwt_ps, cwt_in, hid_ps, hid_in, bc_ps, hs_ready, hs_used, f0_ps, cast0, cwt3_ps = (
                sem(n) for n in ("g_ps", "g_exp", "g_sum", "cw_ready", "cwt_ps", "cwt_in", "hid_ps", "hid_in",
                                 "bc_ps", "hs_ready", "hs_used", "f0_ps", "cast0", "cwt3_ps"))
            CH = 4
            zeroed = sem("zeroed")

            @block.sync
            def _(sp):
                load_weights(sp, 3)

            @block.gpsimd
            def _(pool):
                pool.memset(CWT[:, :], 0.0).then_inc(zeroed, 1)
                pool.memset(CWT3[:, :], 0.0).then_inc(zeroed, 1)

            @block.tensor
            def _(pe):
                def up(n):
                    e, bp, bh = n // CH, (n // 2) % 2, n % 2
                    if n >= 3:
                        pe.wait_ge(hid_in, n - 2)
                    if n == 0:
                        pe.wait_ge(ln_done, 4)
                    pe.matmul(bank(5 + n % 3), wt("w1_0", (2 * e + bh) * FH0, FH0), Y[:, bp * HC:(bp + 1) * HC],
                              start=True, stop=True).then_inc(hid_ps, 1)

                def bc(n):
                    e, bp, bh = n // CH, (n // 2) % 2, n % 2
                    if n >= 3:
                        pe.wait_ge(hs_ready, n - 2)
                    pe.matmul(bank(2 + n % 3), SELB[:, e * P:(e + 1) * P], CWT3[:, (2 * bh + bp) * HC:(2 * bh + bp + 1) * HC],
                              start=True, stop=True).then_inc(bc_ps, 1)

                def down(n):
                    e, bp = n // CH, (n // 2) % 2
                    for bh in range(2):
                        pe.wait_ge(hs_ready, n + bh + 1)
                        pe.matmul(bank(bp)[C * bh:C * bh + C, :], wt("w2_0", e * C, C), HS[:, (n + bh) % 4, :],
                                  start=(e == 0), stop=False).then_inc(hs_used, 1)

                ln_pe(pe, 1)
                pe.wait_ge(w_in[2], 16)
                for r in range(TILES // 2):
                    pe.wait_ge(ln_done, 3 + r // NB)
                    mm = pe.matmul(bank(4)[:, r * 2 * E:(r + 1) * 2 * E], Y[:, r * P:(r + 1) * P], wt("gate0"), start=True, stop=True)
                mm.then_inc(g_ps, 1)
                for n in range(AHEAD):
                    up(n)
                pe.wait_ge(cast0, 2)
                for q in range(2):
                    for i in range(8):
                        t = 8 * q + i
                        o = bank(2 + q).bitcast(BF16)
                        mm = pe.transpose(o[0:3 * E, i * P:(i + 1) * P], CW3[:, t, :, :].rearrange("p s e -> p (s e)"), IDB[:, :])
                    mm.then_inc(cwt3_ps, 1)
                for q in range(4):
                    if q >= 2:
                        pe.wait_ge(cwt_in, q + 1)
                    for i in range(4):
                        t = 4 * q + i
                        mm = pe.transpose(bank(q % 2)[0:E, i * P:(i + 1) * P], LG[:, t, :], wt("ident"))
                    mm.then_inc(cwt_ps, 1)
                pe.wait_ge(cwt_in, 6)

                bc(0)
                bc(1)
                for n in range(0, E * CH, 2):
                    for i in (n + AHEAD, n + AHEAD + 1):
                        if i < E * CH:
                            up(i)
                    for i in (n + 2, n + 3):
                        if i < E * CH:
                            bc(i)
                    down(n)
                for bp in range(2):
                    for bh in range(2):
                        mm = pe.matmul(bank(bp)[C * bh:C * bh + C, :], wt("b2_0"), CWT[:, (2 * bh + bp) * HC:(2 * bh + bp + 1) * HC],
                                       start=False, stop=True)
                    mm.then_inc(f0_ps, 1)

            @block.scalar
            def _(act):
                ln_act(act, 1, "epst")
                act.wait_ge(w_in[2], 16)
                warm(act, ACT.Exp)
                act.wait_ge(g_exp, 1)
                act.activation(LG[:, :, :], LG[:, :, :], ACT.Exp).then_inc(g_sum, 1)
                act.wait_ge(zeroed, 2)

                def hidden(n):
                    act.wait_ge(hid_ps, n + 1)
                    if n >= HBUF:
                        act.wait_ge(hs_ready, n - HBUF + 1)
                    act.activation(HID[:, n % HBUF, :], bank(5 + n % 3), ACT.Gelu, bias=wt("b1_0", n // CH, 1)).then_inc(hid_in, 1)

                for n in range(AHEAD - 2):
                    hidden(n)
                for q in range(2):
                    act.wait_ge(cwt3_ps, q + 1)
                    act.activation(CWT3[0:3 * E, q * 1024:(q + 1) * 1024], bank(2 + q).bitcast(BF16)[0:3 * E, :], ACT.Copy).then_inc(cwt_in, 1)
                for q in range(4):
                    act.wait_ge(cwt_ps, q + 1)
                    act.activation(CWT[0:E, q * HC:(q + 1) * HC], bank(q % 2)[0:E, :], ACT.Copy).then_inc(cwt_in, 1)
                for n in range(AHEAD - 2, E * CH):
                    hidden(n)
                warm(act, ACT.Sqrt)

            @block.vector
            def _(dve):
                ln_dve(dve, 1, flat)
                dve.wait_ge(w_in[2], 16)
                sel = wt("sel24").rearrange("p (e o) -> p e o", o=1).broadcast_to([P, E, P])
                dve.tensor_copy(SELB[:, :].rearrange("p (e m) -> p e m", e=E), sel).then_inc(cast0, 1)
                dve.tensor_copy(IDB[:, :], wt("ident"))
                dve.wait_ge(g_ps, 1)
                for bh in range(2):
                    gb = wt("gb0").rearrange("p (o e) -> p o e", o=1).broadcast_to([P, 8, E])
                    raw = bank(4, TILES * E).rearrange("p (r h e) -> p h r e", h=2, e=E)
                    ins = dve.tensor_tensor(LG[:, 8 * bh:8 * bh + 8, :], raw[:, bh], gb, ALU.add)
                after(dve, ins)
                softmax_dve(dve, LG, RED, TILES, g_exp, 1, g_sum)
                first_max_dve(dve, LG, KEY, RED, FIRST)
                after(dve, dve.scalar_tensor_tensor(out=REST[:, :, :], in0=FIRST[:, :, :], scalar=-2.0, in1=LG[:, :, :],
                                                    op0=ALU.mult, op1=ALU.add))
                first_max_dve(dve, REST, KEY, RED, SECOND)
                after(dve, dve.tensor_tensor(CHOSEN[:, :, :], FIRST[:, :, :], SECOND[:, :, :], ALU.add))
                dve.tensor_tensor(LG[:, :, :], LG[:, :, :], CHOSEN[:, :, :], ALU.mult).then_inc(cw_ready, 1)
                dve.wait_ge(cw_ready, 1)
                after(dve, dve.tensor_copy(CW3[:, :, 0, :], LG[:, :, :]))
                after(dve, dve.tensor_tensor(CHOSEN[:, :, :], LG[:, :, :], CW3[:, :, 0, :], ALU.subtract))
                after(dve, dve.tensor_copy(CW3[:, :, 1, :], CHOSEN[:, :, :]))
                after(dve, dve.tensor_tensor(CHOSEN[:, :, :], CHOSEN[:, :, :], CW3[:, :, 1, :], ALU.subtract))
                dve.tensor_copy(CW3[:, :, 2, :], CHOSEN[:, :, :]).then_inc(cast0, 1)
                for n in range(E * CH):
                    dve.wait_ge(hid_in, n + 1)
                    dve.wait_ge(bc_ps, n + 1)
                    if n >= 4:
                        dve.wait_ge(hs_used, n - 3)
                    dve.tensor_tensor(HS[:, n % 4, :], bank(2 + n % 3), HID[:, n % HBUF, :], ALU.mult).then_inc(hs_ready, 1)
                for bp in range(2):
                    c = slice(bp * HC, (bp + 1) * HC)
                    dve.wait_ge(f0_ps, bp + 1)
                    dve.tensor_tensor(X[:, c], bank(bp), X[:, c], ALU.add)

        with ExitStack() as sctx, nc.Block() as block:
            VTA = sb("VTA", [P, 4, TILES * P], F32, sctx)
            front = VTA[:, :, :].rearrange("p n c -> p (n c)")
            YP = front[:, 0:PROWS * PW].rearrange("p (r w) -> p r w", w=PW)
            shifted = [front[:, PROWS * (PW + k * W):PROWS * (PW + (k + 1) * W)].rearrange("p (r w) -> p r w", w=W) for k in range(5)]
            XS, HS3 = shifted[0:2], shifted[2:5]
            GX = sb("GX", [P, 2, 2, NB, 4, P], FP16, sctx)
            POS = sb("POS", [P, 4, 72], F32, sctx)
            PY = sb("PY", [P, TILES, 72], F32, sctx)
            BASE = sb("BASE", [P, TILES, 72], F32, sctx)
            U0 = sb("U0", [P, TILES, 72], F32, sctx)
            U1 = sb("U1", [P, TILES, 72], F32, sctx)
            WC = sb("WC", [P, SAMPLES, TILES, 4], F32, sctx)
            IDX = sb("IDX", [P, TILES, SAMPLES], FP16, sctx)
            IDXT = sb("IDXT", [SAMPLES, TILES * P], FP16, sctx)
            IDH = sb("IDH", [P, P], FP16, sctx)
            NBC = 4
            NOH = 3

            def scalars(s):
                return (s + 1) // 2
            BC = sb("BC", [P, NBC, TILES * P], FP16, sctx)
            OH = sb("OH", [P, NOH, 2, TILES * P], FP16, sctx)
            DIST = sb("DIST", [P, TILES * P], FP16, sctx)
            scalar_oh = sem("s3_scalar_oh")
            U = [a[:, :].rearrange("p (t k c) -> p t k c", t=TILES, k=4) for a in (SQ, SD)]
            V1 = sb("V1", [P, TILES, 2, CG], F32, sctx)
            VAL = sb("VAL", [P, 2, TILES, 8, CG], F32, sctx)
            (y_pad, c1_ps, h_in, h_pad, c2_ps, gx_ps, gx_hi, gx_done, idx_ready, cast1, idxt_ps, idxt_in, idx_out,
             oh_ready, ga_ps, u_ready, val_ready, vt_ps, vt_in, dc_ps, xs_ready) = (
                sem("s3_" + n) for n in ("y_pad", "c1_ps", "h_in", "h_pad", "c2_ps", "gx_ps", "gx_hi", "gx_done", "idx_ready",
                "cast1", "idxt_ps", "idxt_in", "idx_out", "oh_ready", "ga_ps", "u_ready",
                "val_ready", "vt_ps", "vt_in", "dc_ps", "xs_ready"))

            bc_in = [sem(f"bc_in{i}") for i in range(NBC)]

            @block.sync
            def _(sp):
                load_weights(sp, 4)
                for g in range(NB):
                    sp.wait_ge(idxt_in, g + 1)
                    sp.dma_start(idx_dram[:, g * HC:(g + 1) * HC], IDXT[:, g * HC:(g + 1) * HC]).then_inc(idx_out, 16)
                sp.wait_ge(idx_out, 16 * NB)
                for s in range(SAMPLES):
                    if s >= NBC:
                        sp.wait_ge(oh_ready, s - NBC + 1)
                        if scalars(s - NBC):
                            sp.wait_ge(scalar_oh, scalars(s - NBC))
                    sp.dma_start(BC[:, s % NBC, :], idx_dram[s:s + 1, :].broadcast_to([P, TILES * P])).then_inc(bc_in[s % NBC], 16)

            def padded_y(h):
                return pair(YP, h, 2, 2), images

            @block.gpsimd
            def _(pool):
                pool.memset(YP[:, :, :], 0.0).then_inc(y_pad, 1)
                for k in range(3):
                    pool.memset(HS3[k][:, :, :], 0.0).then_inc(h_pad, 1)
                for s in range(SAMPLES):
                    pool.wait_ge(u_ready, s + 1)
                    after_pool(pool, pool.tensor_tensor(V1[:, :, :, :], U[s % 2][:, :, 0:2, :], U[s % 2][:, :, 2:4, :], ALU.add))
                    if s >= 16 and s % 8 == 0:
                        pool.wait_ge(vt_ps, 4 * (s // 8 - 1))
                    pool.tensor_tensor(VAL[:, (s // 8) % 2, :, s % 8, :], V1[:, :, 0, :], V1[:, :, 1, :], ALU.add).then_inc(val_ready, 1)
                    pool.wait_ge(val_ready, s + 1)

            @block.tensor
            def _(pe):
                ln_pe(pe, 2)
                pe.wait_ge(w_in[3], 16)
                for h in range(2):
                    pe.wait_ge(ln_done, 5 + h)
                    for m in range(9):
                        mm = pe.matmul(bank(4 + h), wt("c1w", m * P, P), pair(YP, h, 1 + m // 3, 1 + m % 3),
                                       start=(m == 0), stop=(m == 8))
                    mm.then_inc(c1_ps, 1)
                pe.wait_ge(xs_ready, 2)
                for n in range(2 * NB):
                    bl, qh = n // 2, n % 2
                    if n >= 4:
                        pe.wait_ge(gx_done, n - 3)
                    for k in range(4):
                        r0 = bl * PITCH + 2 + qh * (H // 2) + k // 2
                        src = XS[k % 2][:, r0:r0 + H // 2, :].rearrange("p r w -> p (r w)")
                        mm = pe.transpose(bank(n % 4)[:, k * P:(k + 1) * P], src, wt("ident"))
                    mm.then_inc(gx_ps, 1)
                pe.wait_ge(h_in, 6)
                for g in range(NB):
                    for i in range(2):
                        for m in range(9):
                            r0 = g * PITCH + i * (H // 2) + 1 + m // 3
                            src = HS3[m % 3][:, r0:r0 + H // 2, :].rearrange("p r w -> p (r w)")
                            mm = pe.matmul(bank(4 + g)[:, i * 144:(i + 1) * 144], src, wt("c2w", m * 144, 144),
                                           start=(m == 0), stop=(m == 8))
                    mm.then_inc(c2_ps, 1)
                for g in range(NB):
                    pe.wait_ge(idx_ready, g + 1)
                    for i in range(4):
                        mm = pe.transpose(bank(g).bitcast(FP16)[0:SAMPLES, i * P:(i + 1) * P], IDX[:, 4 * g + i, :], IDH[:, :])
                    mm.then_inc(idxt_ps, 1)
                def gather(s):
                    g = s // 9
                    pe.wait_ge(oh_ready, s + 1)
                    if scalars(s):
                        pe.wait_ge(scalar_oh, scalars(s))
                    if s >= 2:
                        pe.wait_ge(u_ready, s - 1)
                    for t in range(TILES):
                        bl, bh = t // 4, (t // 2) % 2
                        o = bank(4 + 2 * (s % 2) + t // 8)[:, (t % 8) * 64:(t % 8 + 1) * 64]
                        for qh in range(2):
                            for part in range(2):
                                src = GX[:, part, qh, bl, :, bh * C + g * CG:bh * C + (g + 1) * CG]
                                mm = pe.matmul(o, OH[:, s % NOH, qh, t * P:(t + 1) * P], src,
                                               start=(qh == 0 and part == 0), stop=(qh == 1 and part == 1))
                    mm.then_inc(ga_ps, 1)

                def contract(ch):
                    ns = min(8, SAMPLES - 8 * ch)
                    rows = ns * CG
                    pe.wait_ge(val_ready, 8 * ch + ns)
                    for q in range(4):
                        n = 4 * ch + q
                        if n >= 2:
                            pe.wait_ge(vt_in, n - 1)
                        for i in range(4):
                            t = 4 * (2 * (q % 2) + i // 2) + 2 * (q // 2) + i % 2
                            src = VAL[:, ch % 2, t, 0:ns, :].rearrange("p s c -> p (s c)")
                            mm = pe.transpose(bank(q % 2)[0:rows, i * P:(i + 1) * P], src, wt("ident"))
                        mm.then_inc(vt_ps, 1)
                    return rows

                def project(ch):
                    rows = P if ch < 4 else 64
                    pe.wait_ge(vt_in, 4 * ch + 4)
                    for bp in range(2):
                        for bh in range(2):
                            mm = pe.matmul(bank(2 + bp)[C * bh:C * bh + C, :], wt("wd", ch * C, C, 0, rows),
                                           VTA[0:rows, ch % 4, (2 * bh + bp) * HC:(2 * bh + bp + 1) * HC],
                                           start=(ch == 0), stop=(ch == 4))
                        mm.then_inc(dc_ps, 1)

                for s in range(SAMPLES):
                    gather(s)
                    if s >= 11 and s % 8 == 3:
                        contract(s // 8 - 1)
                    if s >= 15 and s % 8 == 7:
                        project(s // 8 - 1)
                contract(4)
                project(3)
                project(4)

            @block.scalar
            def _(act):
                ln_act(act, 2, "epsc")
                act.wait_ge(w_in[3], 16)
                act.wait_ge(h_pad, 3)
                for h in range(2):
                    act.wait_ge(c1_ps, h + 1)
                    for k in range(3):
                        a, b = max(0, 1 - k), min(W, W + 1 - k)
                        act.activation(pair(HS3[k], h, 2, 0)[:, :, :, a:b], images(bank(4 + h))[:, :, :, a + k - 1:b + k - 1],
                                       ACT.Identity, bias=wt("c1b")).then_inc(h_in, 1)
                for n in range(2 * NB):
                    bl, qh = n // 2, n % 2
                    act.wait_ge(gx_ps, n + 1)
                    act.activation(GX[:, 0, qh, bl, :, :], bank(n % 4).rearrange("p (k c) -> p k c", k=4), ACT.Copy,
                                   scale=GSCALE).then_inc(gx_hi, 1)
                for g in range(NB):
                    act.wait_ge(idxt_ps, g + 1)
                    act.activation(IDXT[:, g * HC:(g + 1) * HC], bank(g).bitcast(FP16)[0:SAMPLES, 0:HC], ACT.Copy).then_inc(idxt_in, 1)

                def evac(ch):
                    rows = P if ch < 4 else 64
                    for q in range(4):
                        act.wait_ge(vt_ps, 4 * ch + q + 1)
                        act.activation(VTA[0:rows, ch % 4, q * 512:(q + 1) * 512], bank(q % 2)[0:rows, :], ACT.Copy).then_inc(vt_in, 1)
                for s in range(1, SAMPLES, 2):
                    act.wait_ge(bc_in[s % NBC], 16 * (s // NBC + 1))
                    if scalars(s - 1):
                        act.wait_ge(scalar_oh, scalars(s - 1))
                    after_act(act, act.activation(DIST[:, :], BC[:, s % NBC, :], ACT.Abs, bias=wt("negq1")))
                    if s >= NOH:
                        act.wait_ge(ga_ps, s - NOH + 1)
                    act.activation(OH[:, s % NOH, 1, :], DIST[:, :], ACT.Relu, bias=1.0, scale=-1.0).then_inc(scalar_oh, 1)
                    if s >= 13 and s % 8 == 5:
                        evac(s // 8 - 1)
                evac(3)
                evac(4)
                warm(act, ACT.Sqrt)

            @block.vector
            def _(dve):
                dve.wait_ge(y_pad, 1)
                ln_dve(dve, 2, padded_y)
                dve.wait_ge(w_in[3], 16)
                dve.wait_ge(ln_done, 6)
                for k in range(2):
                    dve.tensor_copy(XS[k][:, :, :], YP[:, :, 2 + k:2 + k + W]).then_inc(xs_ready, 1)
                dve.tensor_copy(IDH[:, :], wt("ident")).then_inc(cast1, 1)
                for n in range(2 * NB):
                    bl, qh = n // 2, n % 2
                    dve.wait_ge(gx_hi, n + 1)
                    dve.scalar_tensor_tensor(out=GX[:, 1, qh, bl, :, :].rearrange("p k c -> p (k c)"), in0=bank(n % 4), scalar=GSCALE,
                                             in1=GX[:, 0, qh, bl, :, :].rearrange("p k c -> p (k c)"), op0=ALU.mult,
                                             op1=ALU.subtract).then_inc(gx_done, 1)
                for h in range(2):
                    pos = wt("pos").rearrange("p (i k) -> p i k", i=2)
                    bias = wt("c2b").rearrange("p (o k) -> p o k", o=1).broadcast_to([P, 2, 72])
                    ins = dve.tensor_tensor(POS[:, 2 * h:2 * h + 2, :], pos, bias, ALU.add)
                after(dve, ins)
                for g in range(NB):
                    t = slice(4 * g, 4 * g + 4)
                    py, base, u0, u1 = PY[:, t, :], BASE[:, t, :], U0[:, t, :], U1[:, t, :]
                    dve.wait_ge(c2_ps, g + 1)
                    after(dve, dve.tensor_tensor(py.rearrange("p (h i) k -> p h i k", h=2),
                                                 bank(4 + g, 288).rearrange("p (i h k) -> p h i k", i=2, h=2),
                                                 POS[:, :, :].rearrange("p (h i) k -> p h i k", h=2), ALU.add))
                    after(dve, dve.tensor_scalar(base, py, -0.5, 0.0, ALU.add, ALU.max))
                    after(dve, dve.tensor_scalar(base, base, float(H - 2), 8388608.0, ALU.min, ALU.add))
                    after(dve, dve.tensor_scalar(base, base, -8388608.0, None, ALU.add))
                    dve.scalar_tensor_tensor(out=IDX[:, t, :], in0=base[:, :, 0:36], scalar=float(W), in1=base[:, :, 36:72],
                                             op0=ALU.mult, op1=ALU.add).then_inc(idx_ready, 1)
                    after(dve, dve.tensor_tensor(py, py, base, ALU.subtract))
                    dve.tensor_scalar(u0, py, -1.0, 1.0, ALU.mult, ALU.add)
                    after(dve, dve.tensor_scalar(u1, py, -1.0, 2.0, ALU.mult, ALU.add))
                    dve.scalar_tensor_tensor(out=u0, in0=py, scalar=1.0, in1=u0, op0=ALU.add, op1=ALU.min)
                    after(dve, dve.scalar_tensor_tensor(out=u1, in0=py, scalar=0.0, in1=u1, op0=ALU.add, op1=ALU.min))
                    dve.tensor_scalar(u0, u0, 0.0, None, ALU.max)
                    after(dve, dve.tensor_scalar(u1, u1, 0.0, None, ALU.max))
                    for k in range(4):
                        wy = (u0, u1)[k // 2][:, :, 0:36].rearrange("p t s -> p s t")
                        wx = (u0, u1)[k % 2][:, :, 36:72].rearrange("p t s -> p s t")
                        ins = dve.scalar_tensor_tensor(out=WC[:, :, t, k], in0=wy, scalar=1.0 / GSCALE, in1=wx,
                                                       op0=ALU.mult, op1=ALU.mult)
                after(dve, ins)

                def compare(s):
                    dve.wait_ge(bc_in[s % NBC], 16 * (s // NBC + 1))
                    if s >= NOH:
                        dve.wait_ge(ga_ps, s - NOH + 1)
                    for qh in range(1 if s % 2 else 2):
                        ins = dve.tensor_scalar(OH[:, s % NOH, qh, :], BC[:, s % NBC, :], wt("qidx", qh, 1), None, ALU.is_equal)
                    ins.then_inc(oh_ready, 1)

                def weigh(s):
                    dve.wait_ge(ga_ps, s + 1)
                    if s >= 2:
                        dve.wait_ge(val_ready, s - 1)
                    for half in range(2):
                        o = U[s % 2][:, 8 * half:8 * half + 8, :, :].rearrange("p t k c -> p (t k) c")
                        src = bank(4 + 2 * (s % 2) + half).rearrange("p (k c) -> p k c", c=CG)
                        w = WC[:, s, 8 * half:8 * half + 8, :].rearrange("p t (k o) -> p (t k) o", o=1).broadcast_to([P, 32, CG])
                        ins = dve.tensor_tensor(o, src, w, ALU.mult)
                    ins.then_inc(u_ready, 1)

                compare(0)
                for s in range(SAMPLES):
                    if s + 1 < SAMPLES:
                        compare(s + 1)
                    weigh(s)
                for bp in range(2):
                    c = slice(bp * HC, (bp + 1) * HC)
                    dve.wait_ge(dc_ps, 8 + bp + 1)
                    dve.scalar_tensor_tensor(out=X[:, c], in0=bank(2 + bp), scalar=0.0, in1=X[:, c], op0=ALU.max, op1=ALU.add)

        with ExitStack() as sctx, nc.Block() as block:
            WCOL = sb("WCOL", [P, TILES], F32, sctx)
            WSEL = sb("WSEL", [P, TILES], F32, sctx)
            CNT = sb("CNT", [P, 2, TILES], F32, sctx)
            JUNK = sb("JUNK", [P, 2, TILES, PIX], F32, sctx)
            DIAG = sb("DIAG", [P, TILES, P], F32, sctx)
            DIAG2 = sb("DIAG2", [P, TILES, P], F32, sctx)
            NEG = sb("NEG", [P, TILES], F32, sctx)
            FFN = sb("FFN", [P, COLS], F32, sctx)
            negated, signed, f_in = sem("s4_negated"), sem("s4_signed"), sem("s4_f_in")
            HID = sb("HID1", [P, 4, HC], F32, sctx)
            w_ps, dg_ready, row_ps, dg2_ready, wm_ps, hid_ps, hid_in, hid_used = (sem("s4_" + n) for n in (
                "w_ps", "dg_ready", "row_ps", "dg2_ready", "wm_ps", "hid_ps", "hid_in", "hid_used"))
            FIRST = 2
            OUT = (7, 4)
            UNITS = [(bh, bp, m) for bp in range(2) for m in range(2) for bh in range(2)]

            @block.sync
            def _(sp):
                load_weights(sp, 5)

            @block.tensor
            def _(pe):
                ln_pe(pe, 3)
                pe.wait_ge(w_in[4], 16)
                for r in range(TILES // 2):
                    pe.wait_ge(ln_done, 7 + r // NB)
                    mm = pe.matmul(bank(4)[:, r * 2:(r + 1) * 2], Y[:, r * P:(r + 1) * P], wt("wr1"), start=True, stop=True)
                mm.then_inc(w_ps, 1)
                def up(n):
                    bh, bp, m = UNITS[n]
                    if n >= 2:
                        pe.wait_ge(hid_in, n - 1)
                    pe.matmul(bank(5 + n % 2), wt("w1_1", bh * FH1 + m * P, P),
                              Y[:, bp * HC:(bp + 1) * HC], start=True, stop=True).then_inc(hid_ps, 1)

                up(0)
                up(1)
                for q in range(4):
                    pe.wait_ge(dg_ready, q + 1)
                    pe.matmul(bank(q), wt("ones"), DIAG[:, 4 * q:4 * q + 4, :], start=True, stop=True).then_inc(row_ps, 1)
                for n in range(0, len(UNITS), 2):
                    if n + 2 < len(UNITS):
                        up(n + 2)
                        up(n + 3)
                    for i in range(2):
                        bh, bp, m = UNITS[n + i]
                        pe.wait_ge(hid_in, n + i + 1)
                        pe.matmul(bank(OUT[bp])[C * bh:C * bh + C, :], wt("w2_1", m * C, C), HID[:, (n + i) % 4, :],
                                  start=(m == 0), stop=(m == 1)).then_inc(hid_used, 1)
                pe.wait_ge(dg2_ready, 1)
                for bp in range(2):
                    for bh in range(2):
                        q = 2 * bh + bp
                        mm = pe.matmul(bank(bp)[C * bh:C * bh + C, :], wt("ones", 0, C), DIAG2[:, 4 * q:4 * q + 4, :],
                                       start=True, stop=True)
                    mm.then_inc(wm_ps, 1)

            @block.scalar
            def _(act):
                ln_act(act, 3, "epst")
                act.wait_ge(w_in[4], 16)
                warm(act, ACT.Gelu_apprx_tanh)
                def hidden(n):
                    bh, bp, m = UNITS[n]
                    act.wait_ge(hid_ps, n + 1)
                    if n >= 4:
                        act.wait_ge(hid_used, n - 3)
                    act.activation(HID[:, n % 4, :], bank(5 + n % 2), ACT.Gelu_apprx_tanh, bias=wt("b1_1", m, 1)).then_inc(hid_in, 1)

                for n in range(FIRST):
                    hidden(n)
                act.wait_ge(negated, 1)
                for t in range(TILES):
                    act.wait_ge(row_ps, t // 4 + 1)
                    row = bank(t // 4)[:, ((t // 2) % 2) * PIX:((t // 2) % 2 + 1) * PIX]
                    act.activation(JUNK[:, 0, t, :], row, ACT.Sign, bias=NEG[:, t:t + 1], accum_out=CNT[:, 0, t:t + 1]).then_inc(signed, 1)
                for n in range(FIRST, len(UNITS)):
                    hidden(n)
                for bp in range(2):
                    act.wait_ge(hid_used, 4 * bp + 4)
                    act.activation(FFN[:, bp * HC:(bp + 1) * HC], bank(OUT[bp]), ACT.Identity, bias=wt("b2_1")).then_inc(f_in, 1)
                warm(act, ACT.Sqrt)

            @block.vector
            def _(dve):
                ln_dve(dve, 3, flat)
                dve.wait_ge(w_in[4], 16)
                dve.wait_ge(w_ps, 1)
                for bh in range(2):
                    raw = bank(4, TILES).rearrange("p (r h) -> p h r", h=2)
                    ins = dve.tensor_scalar(WCOL[:, 8 * bh:8 * bh + 8], raw[:, bh], wt("br1"), None, ALU.add)
                after(dve, ins)
                dve.tensor_scalar(NEG[:, :], WCOL[:, :], -1.0, None, ALU.mult).then_inc(negated, 1)
                for q in range(4):
                    diagonals(dve, DIAG, WCOL, q).then_inc(dg_ready, 1)
                for t in range(TILES):
                    if t % 4 == 0:
                        dve.wait_ge(signed, t + 4)
                    row = bank(t // 4)[:, ((t // 2) % 2) * PIX:((t // 2) % 2 + 1) * PIX]
                    ins = dve.scalar_tensor_tensor(out=JUNK[:, 1, t, :], in0=row, scalar=WCOL[:, t:t + 1],
                                                   in1=wt("before1", (t % 2) * PIX, PIX), op0=ALU.is_equal, op1=ALU.mult,
                                                   accum_out=CNT[:, 1, t:t + 1])
                after(dve, ins)
                after(dve, dve.scalar_tensor_tensor(out=WSEL[:, :], in0=CNT[:, 0, :], scalar=0.5, in1=CNT[:, 1, :], op0=ALU.mult, op1=ALU.add))
                after(dve, dve.tensor_scalar(WSEL[:, :], WSEL[:, :], float(TOPK - PIX // 2), None, ALU.is_lt))
                after(dve, dve.tensor_tensor(WSEL[:, :], WSEL[:, :], WCOL[:, :], ALU.mult))
                for q in range(4):
                    ins = diagonals(dve, DIAG2, WSEL, q)
                ins.then_inc(dg2_ready, 1)
                after(dve, dve.tensor_tensor(X[:, :], X[:, :], Y[:, :], ALU.add))
                for bp in range(2):
                    c = slice(bp * HC, (bp + 1) * HC)
                    dve.wait_ge(f_in, bp + 1)
                    dve.wait_ge(wm_ps, bp + 1)
                    after(dve, dve.tensor_tensor(FFN[:, c], bank(bp), FFN[:, c], ALU.mult))
                    dve.tensor_tensor(X[:, c], X[:, c], FFN[:, c], ALU.add)

        with ExitStack() as sctx, nc.Block() as block:
            GATES = [sb(f"GATE{k}", [P, COLS], F32, sctx) for k in range(4)]
            ST = sb("ST", [P, COLS], F32, sctx)
            gate_ps, gate_in = sem("s5_gate_ps"), sem("s5_gate_in")
            gbank = [4, 5, 6, 7, 0, 1, 2, 3]

            @block.sync
            def _(sp):
                load_weights(sp, 6)

            @block.tensor
            def _(pe):
                ln_pe(pe, 4)
                pe.wait_ge(w_in[5], 16)
                for k in range(4):
                    for h in range(2):
                        if k == 0:
                            pe.wait_ge(ln_done, 9 + h)
                        pe.matmul(bank(gbank[2 * k + h]), wt("ssw", k * P, P), Y[:, h * HC:(h + 1) * HC],
                                  start=True, stop=True).then_inc(gate_ps, 1)

            @block.scalar
            def _(act):
                ln_act(act, 4, "epsc")
                act.wait_ge(w_in[5], 16)
                warm(act, ACT.Sigmoid)
                for k in range(4):
                    for h in range(2):
                        act.wait_ge(gate_ps, 2 * k + h + 1)
                        act.activation(GATES[k][:, h * HC:(h + 1) * HC], bank(gbank[2 * k + h]), ACT.Sigmoid,
                                       bias=wt("ssb", k, 1)).then_inc(gate_in, 1)
                warm(act, ACT.Sqrt)

            @block.vector
            def _(dve):
                ln_dve(dve, 4, flat)
                A, BG, CG_, DG_ = GATES
                dve.wait_ge(gate_in, 2)
                dve.memset(A[:, :].rearrange("p (r w) -> p r w", w=W)[:, :, 0:1], 0.0)
                dve.wait_ge(gate_in, 4)
                after(dve, dve.tensor_tensor(BG[:, :], BG[:, :], Y[:, :], ALU.mult))
                after(dve, dve.tensor_tensor_scan(ST[:, :], A[:, :], BG[:, :], 0.0, ALU.mult, ALU.add))
                dve.wait_ge(gate_in, 8)
                dve.tensor_tensor(DG_[:, :], DG_[:, :], Y[:, :], ALU.mult)
                after(dve, dve.tensor_tensor(CG_[:, :], CG_[:, :], ST[:, :], ALU.mult))
                after(dve, dve.tensor_tensor(X[:, :], X[:, :], DG_[:, :], ALU.add))
                dve.tensor_tensor(X[:, :], X[:, :], CG_[:, :], ALU.add)

        with ExitStack() as sctx, nc.Block() as block:
            DGI = sb("DGI", [P, 18, P])
            diag7 = sem("s7_diag")
            SUM = sb("SUM", [P, PIX], F32, sctx)
            LG = sb("LG2", [P, 2, E], F32, sctx)
            RED = sb("RED2", [P, 2], F32, sctx)
            WT = sb("WT", [P, PIX], F32, sctx)
            SEL2 = sb("SEL2", [P, E, P], F32, sctx)
            WB = sb("WB", [P, E, PIX], F32, sctx)
            BNS = [sb(f"BNS{i}", [P, E], F32, sctx) for i in range(2)]
            BNT = [sb(f"BNT{i}", [P, E], F32, sctx) for i in range(2)]
            H1 = sb("H1", [P, 2, HC], F32, sctx)
            BEFORE_WT, BEFORE_WB, H2BUF = 3, 5, 8
            H2 = sb("H2", [P, H2BUF, HC], F32, sctx)
            H2W = sb("H2W", [P, 2, HC], F32, sctx)
            (bn_sd, bn_done, sum_done, g_ps, g_exp, g_sum, g_ready, wt_ps, wt_in, wb_ps, wb_in, a_ps, a_in, b_ps, b_in, weighted,
             c_done, f_ps) = (sem("s6_" + n) for n in (
                "bn_sd", "bn_done", "sum_done", "g_ps", "g_exp", "g_sum", "g_ready", "wt_ps", "wt_in", "wb_ps", "wb_in", "a_ps",
                "a_in", "b_ps", "b_in", "weighted", "c_done", "f_ps"))
            NU = 2 * E

            wt_zeroed = sem("s6_wt_zeroed")

            @block.sync
            def _(sp):
                load_weights(sp, 7)

            @block.gpsimd
            def _(pool):
                pool.memset(WT[:, :], 0.0).then_inc(wt_zeroed, 1)
                pool.wait_ge(w_in[7], 16)
                for i, name in enumerate(("dwi", "dwo")):
                    for m in range(9):
                        pool.tensor_scalar(DGI[:, 9 * i + m, :], wt("ident"), wt(name, m, 1), None, ALU.mult).then_inc(diag7, 1)

            @block.tensor
            def _(pe):
                ln_pe(pe, 5)
                pe.wait_ge(w_in[6], 16)
                pe.wait_ge(sum_done, 1)
                for h in range(2):
                    mm = pe.matmul(bank(6)[:, h * E:(h + 1) * E], SUM[:, h * P:(h + 1) * P], wt("wr2"), start=True, stop=True)
                mm.then_inc(g_ps, 1)

                def first(n):
                    e, h = n // 2, n % 2
                    if n >= 2:
                        pe.wait_ge(a_in, n - 1)
                    pe.matmul(bank(2 + n % 2), wt("w1_2", e * P, P), Y[:, h * HC:(h + 1) * HC], start=True, stop=True).then_inc(a_ps, 1)

                def second(n):
                    pe.wait_ge(a_in, n + 1)
                    if n >= 2:
                        pe.wait_ge(b_in, n - 1)
                    pe.matmul(bank(4 + n % 2), wt("w2_2", (n // 2) * P, P), H1[:, n % 2, :], start=True, stop=True).then_inc(b_ps, 1)

                def third(n):
                    pe.wait_ge(weighted, n + 1)
                    pe.matmul(bank(n % 2), wt("wo_2", (n // 2) * P, P), H2W[:, n % 2, :], start=(n < 2), stop=False).then_inc(c_done, 1)

                def step(n):
                    if n + 1 < NU:
                        first(n + 1)
                    second(n)

                first(0)
                for n in range(BEFORE_WT):
                    step(n)
                pe.wait_ge(g_ready, 1)
                for h in range(2):
                    mm = pe.transpose(bank(7)[0:E, h * P:(h + 1) * P], LG[:, h, :], wt("ident"))
                mm.then_inc(wt_ps, 1)
                for n in range(BEFORE_WT, BEFORE_WB):
                    step(n)
                pe.wait_ge(wt_in, 1)
                for q in range(4):
                    if q >= 2:
                        pe.wait_ge(wb_in, q - 1)
                    for i in range(2):
                        mm = pe.matmul(bank(6 + q % 2)[:, i * PIX:(i + 1) * PIX], SEL2[:, 2 * q + i, :], WT[:, :], start=True, stop=True)
                    mm.then_inc(wb_ps, 1)
                for n in range(BEFORE_WB - 1):
                    third(n)
                for n in range(BEFORE_WB, NU):
                    step(n)
                    third(n - 1)
                third(NU - 1)
                for h in range(2):
                    rhs = WT[:, :].rearrange("p (o n) -> p o n", o=1).broadcast_to([P, 2, PIX])
                    pe.matmul(bank(h), wt("bo2"), rhs, start=False, stop=True).then_inc(f_ps, 1)

            @block.scalar
            def _(act):
                ln_act(act, 5, "epst")
                act.wait_ge(w_in[6], 16)
                for i in range(2):
                    act.activation(BNS[i][:, :], wt(f"bn{i + 1}", 4 * E, E), ACT.Sqrt, bias=wt("epsb")).then_inc(bn_sd, 1)
                warm(act, ACT.Exp)
                act.wait_ge(bn_done, 1)

                def relu1(n):
                    act.wait_ge(a_ps, n + 1)
                    if n >= 2:
                        act.wait_ge(b_ps, n - 1)
                    act.activation(H1[:, n % 2, :], bank(2 + n % 2), ACT.Relu, bias=BNT[0][:, n // 2:n // 2 + 1],
                                   scale=BNS[0][:, n // 2:n // 2 + 1]).then_inc(a_in, 1)

                def relu2(n):
                    act.wait_ge(b_ps, n + 1)
                    if n >= H2BUF:
                        act.wait_ge(weighted, n - H2BUF + 1)
                    act.activation(H2[:, n % H2BUF, :], bank(4 + n % 2), ACT.Relu, bias=BNT[1][:, n // 2:n // 2 + 1],
                                   scale=BNS[1][:, n // 2:n // 2 + 1]).then_inc(b_in, 1)

                def step(n):
                    if n + 1 < NU:
                        relu1(n + 1)
                    relu2(n)

                relu1(0)
                step(0)
                act.wait_ge(g_exp, 1)
                act.activation(LG[:, :, :], LG[:, :, :], ACT.Exp).then_inc(g_sum, 1)
                for n in range(1, BEFORE_WT):
                    step(n)
                act.wait_ge(wt_ps, 1)
                act.wait_ge(wt_zeroed, 1)
                act.activation(WT[0:E, :], bank(7)[0:E, 0:PIX], ACT.Copy).then_inc(wt_in, 1)
                for n in range(BEFORE_WT, BEFORE_WB):
                    step(n)
                for q in range(4):
                    act.wait_ge(wb_ps, q + 1)
                    act.activation(WB[:, 2 * q:2 * q + 2, :], bank(6 + q % 2).rearrange("p (e n) -> p e n", e=2), ACT.Copy).then_inc(wb_in, 1)
                for n in range(BEFORE_WB, NU):
                    step(n)
                warm(act, ACT.Sqrt)

            @block.vector
            def _(dve):
                ln_dve(dve, 5, flat)
                dve.wait_ge(ln_done, 12)
                dve.tensor_reduce(SUM[:, :], Y[:, :].rearrange("p (b n) -> p n b", b=NB), AX.X, ALU.add).then_inc(sum_done, 1)
                dve.wait_ge(w_in[6], 16)
                dve.tensor_copy(SEL2[:, :, :], wt("ident", 0, E).rearrange("p (e o) -> p e o", o=1).broadcast_to([P, E, P]))
                dve.wait_ge(bn_sd, 2)
                for i in range(2):
                    name = f"bn{i + 1}"
                    after(dve, dve.reciprocal(BNS[i][:, :], BNS[i][:, :]))
                    dve.tensor_tensor(BNS[i][:, :], BNS[i][:, :], wt(name, E, E), ALU.mult)
                    after(dve, dve.tensor_tensor(BNT[i][:, :], wt(name, 0, E), wt(name, 3 * E, E), ALU.subtract))
                    after(dve, dve.tensor_tensor(BNT[i][:, :], BNT[i][:, :], BNS[i][:, :], ALU.mult))
                    ins = dve.tensor_tensor(BNT[i][:, :], BNT[i][:, :], wt(name, 2 * E, E), ALU.add)
                ins.then_inc(bn_done, 1)
                dve.wait_ge(g_ps, 1)
                br = wt("br2").rearrange("p (o e) -> p o e", o=1).broadcast_to([P, 2, E])
                after(dve, dve.scalar_tensor_tensor(out=LG[:, :, :], in0=bank(6, 2 * E).rearrange("p (h e) -> p h e", h=2),
                                                    scalar=1.0 / B, in1=br, op0=ALU.mult, op1=ALU.add))
                softmax_dve(dve, LG, RED, 2, g_exp, 1, g_sum)
                dve.engine_nop().then_inc(g_ready, 1)
                for n in range(NU):
                    dve.wait_ge(b_in, n + 1)
                    dve.wait_ge(wb_in, n // 4 + 1)
                    if n >= 2:
                        dve.wait_ge(c_done, n - 1)
                    w = WB[:, n // 2, :].rearrange("p (o n) -> p o n", o=1).broadcast_to([P, 2, PIX])
                    dve.tensor_tensor(H2W[:, n % 2, :].rearrange("p (b n) -> p b n", b=2),
                                      H2[:, n % H2BUF, :].rearrange("p (b n) -> p b n", b=2), w, ALU.mult).then_inc(weighted, 1)
                for h in range(2):
                    c = slice(h * HC, (h + 1) * HC)
                    dve.wait_ge(f_ps, h + 1)
                    dve.tensor_tensor(X[:, c], bank(h), X[:, c], ALU.add)

        with ExitStack() as sctx, nc.Block() as block:
            W1P = [sb(f"W1P{i}", [P, E * FH3], BF16) for i in range(3)]
            WREST = sb("WREST", [P, E * FH3], F32, sctx)
            split_step = sem("s7_split_step")
            YP, ZP, OP = (sb(n, [P, PROWS, PW], F32, sctx) for n in ("YP7", "ZP7", "OP7"))
            R = sb("R", [P, COLS], F32, sctx)
            M = sb("M7", [P, 2, HC], F32, sctx)
            ACC = sb("ACC7", [P, COLS], F32, sctx)
            y_pad, pads, ones_set, z_ps, r_ps, r_in, k_ps, k_used, o_ready, o_ps = (sem("s7_" + n) for n in (
                "y_pad", "pads", "ones_set", "z_ps", "r_ps", "r_in", "k_ps", "k_used", "o_ready", "o_ps"))
            z_in = [sem(f"s7_z_in{h}") for h in range(2)]
            PTAPS = 4
            WROWS = PITCH + H
            WIN = sb("WIN", [P, WROWS, W], F32, sctx)

            def padded_y7(h):
                return pair(YP, h, 2, 2), images

            @block.sync
            def _(sp):
                load_weights(sp, 8)

            @block.gpsimd
            def _(pool):
                pool.memset(YP[:, :, :], 0.0).then_inc(y_pad, 1)
                for b in (ZP, OP):
                    pool.memset(b[:, :, :], 0.0).then_inc(pads, 1)
                after_pool(pool, pool.memset(R[:, :], 0.0))
                pool.memset(R[32:33, :], 1.0).then_inc(ones_set, 1)
                for i in range(2):
                    pool.wait_ge(split_step, 2 * i + 2)
                    pool.tensor_tensor(WREST[:, :], WREST[:, :], W1P[i][:, :], ALU.subtract).then_inc(split_step, 1)

            @block.tensor
            def _(pe):
                ln_pe(pe, 6)
                pe.wait_ge(w_in[7], 16)
                pe.wait_ge(diag7, 18)
                pe.wait_ge(ln_done, 14)
                for m in range(9):
                    mm = pe.matmul(bank(4), DGI[:, m, :], pair(YP, 0, 1 + m // 3, 1 + m % 3), start=(m == 0), stop=(m == 8))
                mm.then_inc(z_ps, 1)
                for h in range(2):
                    pe.wait_ge(z_in[h], 1)
                    pe.matmul(bank(6 + h)[0:32, :], wt("red"), pair(ZP, h, 2, 2), start=True, stop=True).then_inc(r_ps, 1)
                    pe.wait_ge(r_in, h + 1)
                    for k in range(9):
                        n = 9 * h + k
                        if n >= 4:
                            pe.wait_ge(k_used, n - 3)
                        pe.matmul(bank(n % 4), wt("span", k * P, P), R[:, h * HC:(h + 1) * HC],
                                  start=True, stop=True).then_inc(k_ps, 1)
                for h in range(2):
                    pe.wait_ge(o_ready, h + 1)
                    taps = 9 if h == 0 else PTAPS
                    for m in range(taps):
                        mm = pe.matmul(bank(4 + h), DGI[:, 9 + m, :], pair(OP, h, 1 + m // 3, 1 + m % 3), start=(m == 0), stop=(m == taps - 1))
                    mm.then_inc(o_ps, 1)

            @block.scalar
            def _(act):
                ln_act(act, 6, "epsc")
                act.wait_ge(w_in[7], 16)
                act.wait_ge(pads, 1)
                act.wait_ge(ones_set, 1)
                act.wait_ge(z_ps, 1)
                act.activation(pair(ZP, 0, 2, 2), images(bank(4)), ACT.Identity, bias=wt("dbi")).then_inc(z_in[0], 1)
                for h in range(2):
                    act.wait_ge(r_ps, h + 1)
                    act.activation(R[0:32, h * HC:(h + 1) * HC], bank(6 + h)[0:32, :], ACT.Relu, bias=wt("bred", 0, 1, 0, 32)).then_inc(r_in, 1)
                act.wait_ge(w_in[8], 16)
                act.activation(WREST[:, :], wt("w1_3"), ACT.Copy, scale=1.0 / GSCALE).then_inc(split_step, 1)
                act.activation(W1P[2][C:P, :].rearrange("p (e f) -> p e f", e=E),
                               wt("drop", 0, E, C, P).rearrange("p (e o) -> p e o", o=1).broadcast_to([C, E, FH3]), ACT.Copy)
                for i in range(3):
                    act.wait_ge(split_step, 2 * i + 1)
                    n = P if i < 2 else C
                    act.activation(W1P[i][0:n, :], WREST[0:n, :], ACT.Copy).then_inc(split_step, 1)
                warm(act, ACT.Sqrt)

            @block.vector
            def _(dve):
                dve.wait_ge(y_pad, 1)
                ln_dve(dve, 6, padded_y7)
                dve.wait_ge(w_in[7], 16)
                dve.wait_ge(pads, 2)
                dve.wait_ge(ln_done, 14)
                def window(pad, m):
                    return pad[:, 2 * PITCH + 1 + m // 3:2 * PITCH + 1 + m // 3 + WROWS, 1 + m % 3:1 + m % 3 + W]

                after(dve, dve.tensor_scalar(WIN[:, :, :], window(YP, 0), wt("dwi", 0, 1), wt("dbi"), ALU.mult, ALU.add))
                for m in range(1, 8):
                    after(dve, dve.scalar_tensor_tensor(out=WIN[:, :, :], in0=window(YP, m), scalar=wt("dwi", m, 1), in1=WIN[:, :, :],
                                                        op0=ALU.mult, op1=ALU.add))
                for i in range(2):
                    r = i * PITCH
                    ins = dve.scalar_tensor_tensor(out=ZP[:, 2 * PITCH + 2 + r:2 * PITCH + 2 + r + H, 2:2 + W],
                                                   in0=window(YP, 8)[:, r:r + H, :], scalar=wt("dwi", 8, 1), in1=WIN[:, r:r + H, :],
                                                   op0=ALU.mult, op1=ALU.add)
                ins.then_inc(z_in[1], 1)
                for h in range(2):
                    dve.wait_ge(z_in[h], 1)
                    for k in range(9):
                        n = 9 * h + k
                        c = slice(h * HC, (h + 1) * HC)
                        dve.wait_ge(k_ps, n + 1)
                        o = ACC[:, c] if k == 0 else M[:, n % 2, :]
                        dve.tensor_tensor(images(o), images(bank(n % 4)), pair(ZP, h, 1 + k // 3, 1 + k % 3), ALU.mult).then_inc(k_used, 1)
                        dve.wait_ge(k_used, n + 1)
                        if k == 8:
                            dve.tensor_tensor(pair(OP, h, 2, 2), images(ACC[:, c]), images(M[:, n % 2, :]), ALU.add).then_inc(o_ready, 1)
                        elif k:
                            after(dve, dve.tensor_tensor(ACC[:, c], ACC[:, c], M[:, n % 2, :], ALU.add))
                dve.wait_ge(o_ready, 2)
                after(dve, dve.tensor_scalar(WIN[:, :, :], window(OP, PTAPS), wt("dwo", PTAPS, 1), wt("dbo"), ALU.mult, ALU.add))
                for m in range(PTAPS + 1, 9):
                    after(dve, dve.scalar_tensor_tensor(out=WIN[:, :, :], in0=window(OP, m), scalar=wt("dwo", m, 1), in1=WIN[:, :, :],
                                                        op0=ALU.mult, op1=ALU.add))
                for i in range(2):
                    x = X[:, HC + i * PIX:HC + (i + 1) * PIX].rearrange("p (r w) -> p r w", w=W)
                    ins = dve.tensor_tensor(x, x, WIN[:, i * PITCH:i * PITCH + H, :], ALU.add)
                after(dve, ins)
                dve.wait_ge(o_ps, 1)
                dve.scalar_tensor_tensor(out=X[:, 0:HC], in0=bank(4), scalar=wt("dbo"), in1=X[:, 0:HC], op0=ALU.add, op1=ALU.add)
                dve.wait_ge(o_ps, 2)
                dve.tensor_tensor(X[:, HC:COLS], bank(5), X[:, HC:COLS], ALU.add)

        with ExitStack() as sctx, nc.Block() as block:
            LG = sb("LG8", [P, TILES, E], F32, sctx)
            RED = sb("RED8", [P, TILES], F32, sctx)
            OTHERS = sb("OTHERS8", [P, TILES, E], F32, sctx)
            OH8 = sb("OH8", [P, TILES, E], F32, sctx)
            TOT = sb("TOT", [P, 3, TILES, E], F32, sctx)
            GATE = sb("GATE8", [P, 2, TILES], F32, sctx)
            DIAG = sb("DIAG8", [P, TILES, P], F32, sctx)
            YS = sb("YS", [P, TILES * P], FP16, sctx)
            YM = sb("YM", [P, TILES * P], FP16, sctx)
            Y4 = sb("Y4", [P, COLS], F32, sctx)
            HI = sb("HI", [P, COLS], FP16, sctx)
            LO = sb("LO", [P, COLS], FP16, sctx)
            parts_ready, ys_ready = sem("s8_parts_ready"), sem("s8_ys_ready")
            OHT = sb("OHT", [P, TILES * P], F32, sctx)
            SCB = sb("SCB", [P, COLS], F32, sctx)
            HID = sb("HID8", [P, 4, HC], F32, sctx)
            FIN = sb("FIN", [P, 4, HC], F32, sctx)
            MASK = sb("MASK8", [P, 3, HC], I32, sctx)
            oht_ps, oht_in, x_final = sem("s8_oht_ps"), sem("s8_oht_in"), sem("s8_x_final")
            (g_ps, g_exp, g_sum, oh_ready, cum_ps, t_ps, t_in, scale_ready, sc_ps, sc_in, hid_ps, hid_in_a, hid_in_v,
             hid_used, f_ps) = (sem("s8_" + n) for n in (
                "g_ps", "g_exp", "g_sum", "oh_ready", "cum_ps", "t_ps", "t_in", "scale_ready", "sc_ps", "sc_in",
                "hid_ps", "hid_in_a", "hid_in_v", "hid_used", "f_ps"))
            UNITS = [(e, m, bp, bh) for bp in range(2) for e in range(E) for m in range(2) for bh in range(2)]
            OHT_AT, SCALE_AT = {4: 0, 8: 1, 12: 2, 16: 3}, {20: 0, 24: 1}
            NU = len(UNITS)
            zeroed = sem("s8_zeroed")

            @block.sync
            def _(sp):
                ov = out_dram.rearrange("(g b) c p -> g c b p", g=2)
                for bp in range(2):
                    sp.wait_ge(x_final, bp + 1)
                    for g in range(2):
                        sp.dma_start(ov[g, :, 2 * bp:2 * bp + 2, :],
                                     X[C * g:C * g + C, bp * HC:(bp + 1) * HC].rearrange("c (b p) -> c b p", b=2)).then_inc(stored, 16)
                sp.wait_ge(stored, 64)

            @block.gpsimd
            def _(pool):
                pool.memset(YM[:, :], 0.0).then_inc(zeroed, 1)
                pool.memset(OHT[:, :], 0.0).then_inc(zeroed, 1)
                for n in range(3):
                    pool.memset(FIN[:, 1 + n, :], (0.0, 1.0e4, -1.0e4)[n]).then_inc(zeroed, 1)
                pool.wait_ge(parts_ready, 2)
                pool.tensor_tensor(LO[:, :], Y4[:, :], HI[:, :], ALU.subtract).then_inc(parts_ready, 1)

            @block.tensor
            def _(pe):
                ln_pe(pe, 7)
                pe.wait_ge(w_in[8], 16)
                for r in range(TILES // 2):
                    pe.wait_ge(ln_done, 15 + r // NB)
                    mm = pe.matmul(bank(4)[:, r * 2 * E:(r + 1) * 2 * E], Y[:, r * P:(r + 1) * P], wt("gate3"), start=True, stop=True)
                mm.then_inc(g_ps, 1)
                pe.wait_ge(oh_ready, 1)
                oh = OH8[:, :, :].rearrange("p t e -> p (t e)")
                pe.matmul(bank(6, P), wt("tri"), oh, start=True, stop=True)
                pe.matmul(bank(7, P), wt("ones"), oh, start=True, stop=True).then_inc(cum_ps, 1)
                for q in range(4):
                    for i in range(4):
                        mm = pe.transpose(bank(q)[0:E, i * P:(i + 1) * P], OTHERS[:, 4 * q + i, :], wt("ident"))
                    mm.then_inc(t_ps, 1)
                pe.wait_ge(t_in, 4)
                pe.wait_ge(ys_ready, 6)

                def transpose_one_hot(q):
                    pe.wait_ge(scale_ready, 1)
                    if q >= 2:
                        pe.wait_ge(oht_in, q - 1)
                    for i in range(4):
                        mm = pe.transpose(bank(6 + q % 2)[0:E, i * P:(i + 1) * P], OH8[:, 4 * q + i, :], wt("ident"))
                    mm.then_inc(oht_ps, 1)

                def spread_scale(bp):
                    pe.wait_ge(oht_in, 3 + bp)
                    for bh in range(2):
                        q = 2 * bh + bp
                        mm = pe.matmul(bank(6 + bp)[C * bh:C * bh + C, :], wt("ones", 0, C), DIAG[:, 4 * q:4 * q + 4, :],
                                       start=True, stop=True)
                    mm.then_inc(sc_ps, 1)

                def finish(bp):
                    for bh in range(2):
                        mm = pe.matmul(bank(bp)[C * bh:C * bh + C, :], wt("b2_3"),
                                       OHT[:, (2 * bh + bp) * HC:(2 * bh + bp + 1) * HC], start=False, stop=True)
                    mm.then_inc(f_ps, 1)

                def up(n):
                    e, m, bp, bh = UNITS[n]
                    if n >= 4:
                        pe.wait_ge((hid_in_a, hid_in_v)[n % 2], n // 2 - 1)
                    c = slice((2 * bh + bp) * HC, (2 * bh + bp + 1) * HC)
                    for i in range(3):
                        mm = pe.matmul(bank(2 + n % 4), W1P[i][:, e * FH3 + m * P:e * FH3 + (m + 1) * P], (YM if i == 2 else YS)[:, c],
                                       start=(i == 0), stop=(i == 2))
                    mm.then_inc(hid_ps, 1)

                up(0)
                up(1)
                for n in range(0, NU, 2):
                    if n + 2 < NU:
                        up(n + 2)
                        up(n + 3)
                    for i, hid_in in enumerate((hid_in_a, hid_in_v)):
                        e, m, bp, bh = UNITS[n + i]
                        pe.wait_ge(hid_in, n // 2 + 1)
                        pe.matmul(bank(bp)[C * bh:C * bh + C, :], wt("w2_3", (2 * e + m) * C, C), HID[:, (n + i) % 4, :],
                                  start=(e == 0 and m == 0), stop=False).then_inc(hid_used, 1)
                    if n in OHT_AT:
                        transpose_one_hot(OHT_AT[n])
                    if n in SCALE_AT:
                        spread_scale(SCALE_AT[n])
                    if n + 2 == NU // 2:
                        finish(0)
                pe.wait_ge(oht_in, 4)
                finish(1)

            @block.scalar
            def _(act):
                ln_act(act, 7, "epst")
                act.wait_ge(w_in[8], 16)
                warm(act, ACT.Exp)
                act.wait_ge(ln_done, 16)
                act.activation(HI[:, :], Y[:, :], ACT.Copy, scale=GSCALE).then_inc(parts_ready, 1)
                act.activation(Y4[:, :], Y[:, :], ACT.Copy, scale=GSCALE).then_inc(parts_ready, 1)
                act.wait_ge(g_exp, 1)
                act.activation(LG[:, :, :], LG[:, :, :], ACT.Exp).then_inc(g_sum, 1)
                for bh in range(2):
                    act.activation(YS[0:C, bh * COLS:(bh + 1) * COLS], Y[C * bh:C * bh + C, :], ACT.Copy, scale=GSCALE).then_inc(ys_ready, 1)
                act.wait_ge(parts_ready, 3)
                for bh in range(2):
                    act.activation(YS[C:P, bh * COLS:(bh + 1) * COLS], LO[C * bh:C * bh + C, :], ACT.Copy).then_inc(ys_ready, 1)
                act.wait_ge(zeroed, 2)
                for bh in range(2):
                    act.activation(YM[0:C, bh * COLS:(bh + 1) * COLS], Y[C * bh:C * bh + C, :], ACT.Copy, scale=GSCALE).then_inc(ys_ready, 1)
                for q in range(4):
                    act.wait_ge(t_ps, q + 1)
                    act.activation(YM[C:C + E, q * HC:(q + 1) * HC], bank(q)[0:E, :], ACT.Copy).then_inc(t_in, 1)
                for n in range(0, NU, 2):
                    e, m, bp, bh = UNITS[n]
                    act.wait_ge(hid_ps, n + 1)
                    if n >= 4:
                        act.wait_ge(hid_used, n - 3)
                    act.activation(HID[:, n % 4, :], bank(2 + n % 4), ACT.Relu, bias=wt("b1_3", 2 * e + m, 1)).then_inc(hid_in_a, 1)
                    if n in OHT_AT:
                        q = OHT_AT[n]
                        act.wait_ge(oht_ps, q + 1)
                        act.activation(OHT[0:E, q * HC:(q + 1) * HC], bank(6 + q % 2)[0:E, :], ACT.Copy).then_inc(oht_in, 1)
                    if n in SCALE_AT:
                        bp = SCALE_AT[n]
                        act.wait_ge(sc_ps, bp + 1)
                        act.activation(SCB[:, bp * HC:(bp + 1) * HC], bank(6 + bp), ACT.Copy).then_inc(sc_in, 1)

            @block.vector
            def _(dve):
                ln_dve(dve, 7, flat)
                dve.wait_ge(w_in[8], 16)
                dve.wait_ge(g_ps, 1)
                for bh in range(2):
                    gb = wt("gb3").rearrange("p (o e) -> p o e", o=1).broadcast_to([P, 8, E])
                    raw = bank(4, TILES * E).rearrange("p (r h e) -> p h r e", h=2, e=E)
                    ins = dve.tensor_tensor(LG[:, 8 * bh:8 * bh + 8, :], raw[:, bh], gb, ALU.add)
                after(dve, ins)
                softmax_dve(dve, LG, RED, TILES, g_exp, 1, g_sum)
                first_max_dve(dve, LG, OTHERS, RED, OH8)
                dve.tensor_scalar(OTHERS[:, :, :], OH8[:, :, :], -1.0, 1.0, ALU.mult, ALU.add).then_inc(oh_ready, 1)
                dve.tensor_reduce(GATE[:, 0, :], LG[:, :, :], AX.X, ALU.max)
                dve.wait_ge(cum_ps, 1)
                tot = bank(7, P).rearrange("p (t e) -> p t e", e=E)
                after(dve, dve.tensor_copy(TOT[:, 0, :, :], tot))
                for i, d in enumerate((1, 2, 4, 8)):
                    src, dst = TOT[:, i % 2], TOT[:, (i + 1) % 2]
                    dve.tensor_copy(dst[:, 0:d, :], src[:, 0:d, :])
                    after(dve, dve.tensor_tensor(dst[:, d:TILES, :], src[:, d:TILES, :], src[:, 0:TILES - d, :], ALU.add))
                after(dve, dve.tensor_tensor(TOT[:, 1, :, :], TOT[:, 0, :, :], tot, ALU.subtract))
                after(dve, dve.tensor_tensor(TOT[:, 1, :, :], TOT[:, 1, :, :], bank(6, P).rearrange("p (t e) -> p t e", e=E), ALU.add))
                after(dve, dve.tensor_tensor(TOT[:, 1, :, :], TOT[:, 1, :, :], OH8[:, :, :], ALU.mult))
                after(dve, dve.tensor_reduce(GATE[:, 1, :], TOT[:, 1, :, :], AX.X, ALU.add))
                after(dve, dve.tensor_scalar(GATE[:, 1, :], GATE[:, 1, :], float(CAP), None, ALU.is_le))
                after(dve, dve.tensor_tensor(GATE[:, 0, :], GATE[:, 0, :], GATE[:, 1, :], ALU.mult))
                for q in range(4):
                    ins = diagonals(dve, DIAG, GATE[:, 0, :], q)
                ins.then_inc(scale_ready, 1)

                def finish(bp):
                    c = slice(bp * HC, (bp + 1) * HC)
                    dve.wait_ge(f_ps, bp + 1)
                    dve.wait_ge(zeroed, 5)
                    dve.wait_ge(sc_in, bp + 1)
                    after(dve, dve.tensor_tensor(FIN[:, 0, :], bank(bp), SCB[:, c], ALU.mult))
                    dve.tensor_tensor(MASK[:, 0, :], FIN[:, 0, :], FIN[:, 0, :], ALU.not_equal)
                    dve.tensor_scalar(MASK[:, 1, :], FIN[:, 0, :], 3.4028234e38, None, ALU.is_gt)
                    after(dve, dve.tensor_scalar(MASK[:, 2, :], FIN[:, 0, :], -3.4028234e38, None, ALU.is_lt))
                    for n in range(3):
                        after(dve, dve.copy_predicated(FIN[:, 0, :], MASK[:, n, :], FIN[:, 1 + n, :]))
                    dve.tensor_tensor(X[:, c], X[:, c], FIN[:, 0, :], ALU.add).then_inc(x_final, 1)

                for n in range(1, NU, 2):
                    e, m, bp, bh = UNITS[n]
                    dve.wait_ge(hid_ps, n + 1)
                    if n >= 4:
                        dve.wait_ge(hid_used, n - 3)
                    dve.tensor_scalar(HID[:, n % 4, :], bank(2 + n % 4), wt("b1_3", 2 * e + m, 1), 0.0, ALU.add, ALU.max).then_inc(hid_in_v, 1)
                    if n == NU // 2 + 9:
                        finish(0)
                finish(1)


def pack_weights(v):
    packs = [np.zeros((P, w), np.float32) for w in WIDTH]

    def put(name, a, p0=0, at=0):
        a = np.asarray(a)
        a = a.reshape(a.shape[0], -1)
        s, c0, cols = AT[name]
        assert at + a.shape[1] <= cols, name
        packs[s][p0:p0 + a.shape[0], c0 + at:c0 + at + a.shape[1]] = a

    def twice(name, a, at=0):
        a = np.asarray(a)
        put(name, a.reshape(a.shape[0], -1), 0, at)
        put(name, a.reshape(a.shape[0], -1), 64, at)

    def diag2(name, a, at=0, width=None):
        width = width or a.shape[1]
        put(name, a, 0, at)
        put(name, a, 64 if a.shape[0] == 64 else a.shape[0], at + width)

    def rows(name, a, at=0):
        put(name, np.broadcast_to(np.asarray(a).reshape(1, -1), (P, np.asarray(a).size)), 0, at)

    f = np.float32
    eye = np.eye(P, dtype=f)
    blocks = np.kron(np.eye(2, dtype=f), np.ones((C, C), f))
    put("ident", eye)
    put("center", eye - blocks / C)
    put("mean32", np.kron(np.eye(2, dtype=f), np.full((C, 16), 1.0 / C, f)))
    for q in range(4):
        for bh in range(2):
            put("spread", np.ones((1, C), f), 32 * q + 16 * bh, q * P + C * bh)
    put("epsc", np.full((P, 1), 1e-6, f))
    put("epst", np.full((P, 1), 1e-5, f))
    put("epsa", np.full((P, 1), 1e-15, f))
    put("epsb", np.full((P, 1), 1e-3, f))

    ch = [np.array([g * 24 + j * HD + e for g in range(8) for e in range(HD)]) for j in range(3)]
    qkv_w = v["L0_conv_qkv_w"][:, :, 0, 0]
    for j in range(3):
        diag2("wq3", qkv_w[ch[j]].T, j * P)
        twice("bq3", v["L0_conv_qkv_b"][ch[j]][:, None], j)
        for k in ("3", "5"):
            w = v[f"L0_conv_dw{k}_w"][ch[j], 0]
            twice("dw" + k, w.reshape(C, -1), j * w.shape[1] * w.shape[2])
            twice("db" + k, v[f"L0_conv_dw{k}_b"][ch[j]][:, None], j)
    for i in range(2):
        diag2("wkv", qkv_w[ch[1 + i]].T, i * P)
    for s, (w, b) in enumerate((("qkv_w", "qkv_b"), ("pw3_w", "pw3_b"), ("pw5_w", "pw5_b"))):
        b = v["L0_conv_" + b]
        rows("bkv", np.concatenate([b[ch[1]], b[ch[1]], b[ch[2]], b[ch[2]]]), s * 2 * P)
        twice("bqq", b[ch[0]][:, None], s)
        if s == 0:
            continue
        pw = v["L0_conv_" + w][:, :, 0, 0]
        for j in range(3):
            m = np.zeros((3, C, C), f)
            for o in range(3):
                for g in range(8):
                    m[o, g * HD:(g + 1) * HD, g * HD:(g + 1) * HD] = pw[g * 24 + o * HD:g * 24 + (o + 1) * HD,
                                                                        j * HD:(j + 1) * HD].T
            diag2("pwq", m[0], ((s - 1) * 3 + j) * P)
            for i in range(2):
                diag2("pwkv", m[1 + i], (2 * ((s - 1) * 3 + j) + i) * P)
    for s in range(SCALES):
        diag2("proj", v["L0_conv_proj_w"][:, s * C:(s + 1) * C, 0, 0].T, s * P)
    twice("bproj", v["L0_conv_proj_b"][:, None])
    heads = np.kron(np.eye(2 * E, dtype=f), np.ones((HD, 1), f))
    put("headmask", np.concatenate([heads, heads], 1))
    for bl in range(NB):
        put("headspread", heads.T, 32 * bl, bl * P)
    put("vkmask", np.kron(np.eye(16, dtype=f), np.ones((HD, HD), f)))

    diag2("gate0", v["L0_ffn_gate_w"])
    rows("gb0", v["L0_ffn_gate_b"])
    rows("rev", np.arange(E, 0, -1).astype(f))
    for e in range(E):
        diag2("w1_0", v["L0_ffn_W1"][e], e * 2 * FH0)
    put("b1_0", v["L0_ffn_b1"].T)
    for e in range(E):
        put("w2_0", v["L0_ffn_W2"][e], 0, e * C)
    put("b2_0", v["L0_ffn_b2"])
    put("sel24", np.tile(np.eye(E, dtype=f), (3, 1)))

    c1, c2 = v["L1_conv_w1"], v["L1_conv_w2"]
    order = np.array([(s * 2 + xy) for xy in range(2) for s in range(SAMPLES)])
    for m in range(9):
        diag2("c1w", c1[:, :, m // 3, m % 3].T, m * P)
        diag2("c2w", c2[order][:, :, m // 3, m % 3].T, m * 144)
    twice("c1b", v["L1_conv_b1"][:, None])
    rows("c2b", v["L1_conv_b2"][order])
    pix = np.arange(P)
    tap = np.arange(SAMPLES) % 9
    for h in range(2):
        py = (pix // W + h * H // 2)[:, None] + (tap // 3 - 1)[None]
        px = (pix % W)[:, None] + (tap % 3 - 1)[None]
        put("pos", np.concatenate([py, px], 1).astype(f), 0, h * 72)
        put("qidx", (pix + h * P)[:, None].astype(f), 0, h)
    put("negq1", -(pix + P)[:, None].astype(f))
    wd = v["L1_conv_wd"].reshape(C, 4, CG, 9).transpose(1, 3, 2, 0).reshape(SAMPLES * CG, C)
    for n in range(5):
        put("wd", wd[n * P:(n + 1) * P], 0, n * C)

    diag2("wr1", v["L1_ffn_wr"])
    rows("br1", v["L1_ffn_br"])
    for h in range(2):
        put("before1", (np.arange(PIX)[None] < (pix + h * P)[:, None]).astype(f) - f(0.5), 0, h * PIX)
    diag2("w1_1", v["L1_ffn_w1"])
    put("b1_1", v["L1_ffn_b1"].reshape(2, P).T)
    for m in range(2):
        put("w2_1", v["L1_ffn_w2"][m * P:(m + 1) * P], 0, m * C)
    twice("b2_1", v["L1_ffn_b2"][:, None])
    put("ones", np.ones((P, P), f))

    for k in range(4):
        diag2("ssw", v["L2_conv_weight"][k * C:(k + 1) * C].T, k * P)
        twice("ssb", v["L2_conv_bias"][k * C:(k + 1) * C, None], k)

    twice("wr2", v["L2_ffn_Wr"])
    rows("br2", v["L2_ffn_br"])
    for e in range(E):
        diag2("w1_2", v["L2_ffn_W1"][e], e * P)
        diag2("w2_2", v["L2_ffn_W2"][e], e * P)
        diag2("wo_2", v["L2_ffn_Wo"][e], e * P)
    for n in (1, 2):
        for i, name in enumerate(("b", "g", "be", "m", "v")):
            twice(f"bn{n}", v[f"L2_ffn_{name}{n}"].T, i * E)
    put("bo2", np.concatenate([v["L2_ffn_bo"], v["L2_ffn_bo"]], 1))

    twice("dwi", v["L3_conv_w_in"].reshape(C, 9))
    twice("dbi", v["L3_conv_b_in"][:, None])
    diag2("red", v["L3_conv_w_red"].T, 0)
    put("bred", v["L3_conv_b_red"][:, None], 0)
    put("bred", v["L3_conv_b_red"][:, None], 16)
    for k in range(9):
        a = np.broadcast_to(v["L3_conv_w_span"][k][:, None], (16, C))
        put("span", a, 0, k * P)
        put("span", a, 16, k * P + C)
        put("span", np.broadcast_to(v["L3_conv_b_span"][k:k + 1, None], (1, P)), 32, k * P)
    twice("dwo", v["L3_conv_w_out"].reshape(C, 9))
    twice("dbo", v["L3_conv_b_out"][:, None])

    diag2("gate3", v["L3_ffn_gate_w"])
    rows("gb3", v["L3_ffn_gate_b"])
    put("tri", np.triu(np.ones((P, P), f)))
    twice("w1_3", v["L3_ffn_w1"].transpose(1, 0, 2))
    put("drop", -BIG * np.eye(E, dtype=f), C)
    for e in range(E):
        for m in range(2):
            put("b1_3", v["L3_ffn_b1"][e, m * P:(m + 1) * P, None], 0, 2 * e + m)
            put("w2_3", v["L3_ffn_w2"][e, m * P:(m + 1) * P], 0, (2 * e + m) * C)
    put("b2_3", v["L3_ffn_b2"])
    return packs


def kernel(**inputs):
    import concourse.bacc as bacc
    from concourse.bass_utils import run_bass_kernel_spmd

    v = {k: np.asarray(a) for k, a in inputs.items()}
    nc = bacc.Bacc("TRN2", target_bir_lowering=False, num_devices=1)
    arrays = {"x_dram": np.ascontiguousarray(v["x"]).reshape(B, C, PIX)}
    x_dram = nc.dram_tensor("x_dram", (B, C, PIX), F32, kind="ExternalInput").ap()
    packs = []
    for n, a in enumerate(pack_weights(v)):
        arrays[f"pack{n}_dram"] = a
        packs.append(nc.dram_tensor(f"pack{n}_dram", a.shape, F32, kind="ExternalInput").ap())
    out = nc.dram_tensor("out_dram", (B, C, PIX), F32, kind="ExternalOutput").ap()
    idx_dram = nc.dram_tensor("idx_dram", (SAMPLES, TILES * P), FP16, kind="Internal").ap()
    build(nc, x_dram, packs, idx_dram, out)
    r = run_bass_kernel_spmd(nc, [arrays], core_ids=[0])
    return r.results[0]["out_dram"].reshape(B, C, H, W)
```
